# Optimizing a Trainium2 kernel written in Bass

```python
import numpy as np
import jax
import jax.numpy as jnp

def _softmax(x, axis=-1):
    return jax.nn.softmax(x, axis=axis)

def _gelu(x):
    return jax.nn.gelu(x, approximate=True)

def _silu(x):
    return jax.nn.silu(x)

def _sigmoid(x):
    return jax.nn.sigmoid(x)

def _layernorm(x, axis=-1, eps=1e-05):
    m = jnp.mean(x, axis=axis, keepdims=True)
    v = jnp.var(x, axis=axis, keepdims=True)
    return (x - m) / jnp.sqrt(v + eps)

def _scatter_add(tgt, idx, src, axis=0):
    return tgt.at[idx].add(src)

def _segment_sum(src, seg, n):
    return jax.ops.segment_sum(src, seg, n)
kernel_name = 'mk_adaln_d2_jaxref_r4_07535e'

def setup_inputs(seed: int=0):
    np.random.seed(seed)
    _w = jnp.asarray

    def _L0_attn_setup():
        import jax, jax.numpy as jnp
        import numpy as np
        D_MODEL = 256
        N_HEADS = 16
        D_HEAD = 64
        D_REC = N_HEADS * D_HEAD
        BATCH = 4
        SEQ = 2048
        CHUNK = 64

        def _make_decay_bias():
            n_fast, n_medium, n_slow = (5, 6, 5)
            b = np.zeros(D_REC, dtype=np.float32)
            fast_end = n_fast * D_HEAD
            medium_end = (n_fast + n_medium) * D_HEAD
            b[:fast_end] = -2.2
            b[fast_end:medium_end] = 0.0
            b[medium_end:] = 4.6
            return jnp.asarray(b)

        def _chunked_scan(decay, value, chunk_size=CHUNK):
            b, s, d = decay.shape
            pad = -s % chunk_size
            if pad:
                decay = jnp.pad(decay, ((0, 0), (0, pad), (0, 0)), constant_values=1.0)
                value = jnp.pad(value, ((0, 0), (0, pad), (0, 0)))
            total = s + pad
            n = total // chunk_size
            dc = decay.reshape(b, n, chunk_size, d)
            vc = value.reshape(b, n, chunk_size, d)
            cum_log = jnp.cumsum(jnp.log(jnp.maximum(dc, 1e-10)), axis=2)
            cum_decay = jnp.exp(cum_log)
            weighted = vc / jnp.maximum(cum_decay, 1e-10)
            intra_state = cum_decay * jnp.cumsum(weighted, axis=2)
            chunk_final_state = intra_state[:, :, -1, :]
            chunk_total_decay = cum_decay[:, :, -1, :]
            cum_log_chunk = jnp.cumsum(jnp.log(jnp.maximum(chunk_total_decay, 1e-10)), axis=1)
            cum_chunk_decay = jnp.exp(cum_log_chunk)
            cum_weighted_chunk = jnp.cumsum(chunk_final_state / jnp.maximum(cum_chunk_decay, 1e-10), axis=1)
            zeros = jnp.zeros((b, 1, d), dtype=cum_weighted_chunk.dtype)
            ones = jnp.ones((b, 1, d), dtype=cum_chunk_decay.dtype)
            incoming_cum_weighted = jnp.concatenate([zeros, cum_weighted_chunk[:, :-1]], axis=1)
            incoming_cum_decay = jnp.concatenate([ones, cum_chunk_decay[:, :-1]], axis=1)
            incoming_state = incoming_cum_decay * incoming_cum_weighted
            cross_contrib = cum_decay * incoming_state[:, :, None, :]
            states = (intra_state + cross_contrib).reshape(b, total, d)[:, :s]
            return states
        key = jax.random.key(seed)
        k_x, k_w1, k_w2 = jax.random.split(key, 3)
        x = jax.random.normal(k_x, (BATCH, SEQ, D_MODEL), dtype=jnp.float32)
        W_aiv = jax.random.normal(k_w1, (D_MODEL, 3 * D_REC), dtype=jnp.float32) / np.sqrt(D_MODEL)
        decay_bias = _make_decay_bias()
        W_mix = jax.random.normal(k_w2, (D_REC, D_MODEL), dtype=jnp.float32) / np.sqrt(D_REC)
        b_mix = jnp.zeros((D_MODEL,), dtype=jnp.float32)
        return {'x': x, 'W_aiv': W_aiv, 'decay_bias': decay_bias, 'W_mix': W_mix, 'b_mix': b_mix}
    _L0_attn_in = _L0_attn_setup()

    def _L0_ffn_setup():
        import jax, jax.numpy as jnp
        import numpy as np
        TOP_K = 2
        E = 8
        D = 256
        F = 512
        B, S = (2, 256)
        key = jax.random.key(seed)
        ks = jax.random.split(key, 8)
        sc = 0.02
        return {'x_bsD': jax.random.normal(ks[0], (B, S, D), dtype=jnp.float32), 'router_DE': jax.random.normal(ks[1], (D, E), dtype=jnp.float32) * sc, 'w_in_shared_FD': jax.random.normal(ks[2], (F, D), dtype=jnp.float32) * sc, 'w_out_shared_DF': jax.random.normal(ks[3], (D, F), dtype=jnp.float32) * sc, 'w_swiglu_FD': jax.random.normal(ks[4], (F, D), dtype=jnp.float32) * sc, 'w_in_eDF': jax.random.normal(ks[5], (E, D, F), dtype=jnp.float32) * sc, 'w_swiglu_eDF': jax.random.normal(ks[6], (E, D, F), dtype=jnp.float32) * sc, 'w_out_eFD': jax.random.normal(ks[7], (E, F, D), dtype=jnp.float32) * sc}
    _L0_ffn_in = _L0_ffn_setup()
    _L0_c = _w((lambda *s: np.random.randn(*s).astype(np.float32) * 0.05)(2, 256))
    _L0_wmod = _w((lambda *s: np.random.randn(*s).astype(np.float32) * 0.05)(256, 6 * 256) * 256 ** (-0.5))

    def _L1_attn_setup():
        import jax, jax.numpy as jnp
        import numpy as np
        EMBED = 256
        WIN = 128
        NUM_HEADS = 16
        HQ = 16
        HKV = 4
        HEAD_DIM = EMBED // NUM_HEADS
        G = HQ // HKV
        key = jax.random.key(seed)
        k = jax.random.split(key, 5)
        B, S = (1, 512)
        x = jax.random.normal(k[0], (B, S, EMBED), dtype=jnp.float32)
        Wq = jax.random.normal(k[1], (HQ * HEAD_DIM, EMBED), dtype=jnp.float32) * 0.02
        Wk = jax.random.normal(k[2], (HKV * HEAD_DIM, EMBED), dtype=jnp.float32) * 0.02
        Wv = jax.random.normal(k[3], (HKV * HEAD_DIM, EMBED), dtype=jnp.float32) * 0.02
        Wo = jax.random.normal(k[4], (EMBED, HQ * HEAD_DIM), dtype=jnp.float32) * 0.02
        return {'x': x, 'Wq': Wq, 'Wk': Wk, 'Wv': Wv, 'Wo': Wo}
    _L1_attn_in = _L1_attn_setup()

    def _L1_ffn_setup():
        import jax, jax.numpy as jnp
        import numpy as np
        DIM = 256
        DEPTH = 2
        HEADS = 8
        DIM_HEAD = 64
        WINDOW = 128
        INNER = HEADS * DIM_HEAD
        HID = int(DIM * 4 * 2 / 3)
        B, N = (2, 2048)
        QK_SCALE = 8.0

        def shift_token(t):
            t1, t2 = jnp.split(t, 2, axis=-1)
            t2 = jnp.pad(t2, ((0, 0), (1, 0), (0, 0)))[:, :-1]
            return jnp.concatenate([t1, t2], axis=-1)

        def l2norm(t):
            return t / jnp.clip(jnp.linalg.norm(t, axis=-1, keepdims=True), 1e-12)

        def rotate_half(x):
            x1, x2 = jnp.split(x, 2, axis=-1)
            return jnp.concatenate([-x2, x1], axis=-1)

        def rotary_xpos(q, k):
            n = q.shape[-2]
            half_idx = jnp.arange(0, DIM_HEAD, 2, dtype=jnp.float32)
            inv_freq = 1.0 / 10000.0 ** (half_idx / DIM_HEAD)
            t = jnp.arange(n, dtype=jnp.float32)
            freqs = t[:, None] * inv_freq[None, :]
            freqs = jnp.concatenate([freqs, freqs], axis=-1)
            base = (half_idx + 0.4 * DIM_HEAD) / (1.4 * DIM_HEAD)
            power = (t - n // 2) / float(WINDOW // 2)
            scale = base[None, :] ** power[:, None]
            scale = jnp.concatenate([scale, scale], axis=-1)
            cos, sin = (jnp.cos(freqs), jnp.sin(freqs))
            q = q * cos * scale + rotate_half(q) * sin * scale
            k = k * cos / scale + rotate_half(k) * sin / scale
            return (q, k)

        def local_attention(q, k, v):
            b, h, n, d = q.shape
            w = n // WINDOW
            bq = q.reshape(b, h, w, WINDOW, d) * QK_SCALE
            bk = k.reshape(b, h, w, WINDOW, d)
            bv = v.reshape(b, h, w, WINDOW, d)

            def look_around(t):
                p = jnp.pad(t, ((0, 0), (0, 0), (1, 0), (0, 0), (0, 0)))
                return jnp.concatenate([p[:, :, :w], p[:, :, 1:]], axis=3)
            bk, bv = (look_around(bk), look_around(bv))
            bt = jnp.arange(n).reshape(w, WINDOW)
            btp = jnp.pad(bt, ((1, 0), (0, 0)), constant_values=-1)
            btk = jnp.concatenate([btp[:w], btp[1:]], axis=1)
            sim = jnp.einsum('bhwid,bhwjd->bhwij', bq, bk)
            i = bt[:, :, None]
            j = btk[:, None, :]
            mask = (i < j) | (i > j + WINDOW) | (j == -1)
            sim = jnp.where(mask, -jnp.finfo(sim.dtype).max, sim)
            attn = jax.nn.softmax(sim, axis=-1)
            out = jnp.einsum('bhwij,bhwjd->bhwid', attn, bv)
            return out.reshape(b, h, n, d)

        def _layer(x, wqkv, qs, ksc, wo, lg, lb, w1, b1, w2, b2):
            b, n, _ = x.shape
            h = shift_token(x)
            qkv = h @ wqkv
            q, k, v = jnp.split(qkv, 3, axis=-1)
            to_heads = lambda t: t.reshape(b, n, HEADS, DIM_HEAD).transpose(0, 2, 1, 3)
            q, k, v = (to_heads(q), to_heads(k), to_heads(v))
            q = l2norm(q) * qs
            k = l2norm(k) * ksc
            q, k = rotary_xpos(q, k)
            o = local_attention(q, k, v)
            o = o.transpose(0, 2, 1, 3).reshape(b, n, INNER)
            x = x + o @ wo
            h = shift_token(x)
            mu = h.mean(-1, keepdims=True)
            var = h.var(-1, keepdims=True)
            h = (h - mu) / jnp.sqrt(var + 1e-05) * lg + lb
            h = h @ w1 + b1
            a, g = jnp.split(h, 2, axis=-1)
            h = a * jax.nn.gelu(g, approximate=False)
            x = x + h @ w2 + b2
            return x
        key = jax.random.key(seed)
        ks = jax.random.split(key, 6)
        return {'x': jax.random.normal(ks[0], (B, N, DIM), jnp.float32), 'wqkv': jax.random.normal(ks[1], (DEPTH, DIM, 3 * INNER), jnp.float32) * 0.02, 'q_scale': jnp.ones((DEPTH, DIM_HEAD), jnp.float32), 'k_scale': jnp.ones((DEPTH, DIM_HEAD), jnp.float32), 'wo': jax.random.normal(ks[2], (DEPTH, INNER, DIM), jnp.float32) * 0.02, 'ln_g': jnp.ones((DEPTH, DIM), jnp.float32), 'ln_b': jnp.zeros((DEPTH, DIM), jnp.float32), 'w1': jax.random.normal(ks[3], (DEPTH, DIM, 2 * HID), jnp.float32) * 0.02, 'b1': jnp.zeros((DEPTH, 2 * HID), jnp.float32), 'w2': jax.random.normal(ks[4], (DEPTH, HID, DIM), jnp.float32) * 0.02, 'b2': jnp.zeros((DEPTH, DIM), jnp.float32)}
    _L1_ffn_in = _L1_ffn_setup()
    _L1_c = _w((lambda *s: np.random.randn(*s).astype(np.float32) * 0.05)(2, 256))
    _L1_wmod = _w((lambda *s: np.random.randn(*s).astype(np.float32) * 0.05)(256, 6 * 256) * 256 ** (-0.5))
    _d = {'L0_attn_x': _L0_attn_in['x'], 'L0_attn_W_aiv': _L0_attn_in['W_aiv'], 'L0_attn_decay_bias': _L0_attn_in['decay_bias'], 'L0_attn_W_mix': _L0_attn_in['W_mix'], 'L0_attn_b_mix': _L0_attn_in['b_mix'], 'L0_ffn_router_DE': _L0_ffn_in['router_DE'], 'L0_ffn_w_in_shared_FD': _L0_ffn_in['w_in_shared_FD'], 'L0_ffn_w_out_shared_DF': _L0_ffn_in['w_out_shared_DF'], 'L0_ffn_w_swiglu_FD': _L0_ffn_in['w_swiglu_FD'], 'L0_ffn_w_in_eDF': _L0_ffn_in['w_in_eDF'], 'L0_ffn_w_swiglu_eDF': _L0_ffn_in['w_swiglu_eDF'], 'L0_ffn_w_out_eFD': _L0_ffn_in['w_out_eFD'], 'L0_c': _L0_c, 'L0_wmod': _L0_wmod, 'L1_attn_Wq': _L1_attn_in['Wq'], 'L1_attn_Wk': _L1_attn_in['Wk'], 'L1_attn_Wv': _L1_attn_in['Wv'], 'L1_attn_Wo': _L1_attn_in['Wo'], 'L1_ffn_wqkv': _L1_ffn_in['wqkv'], 'L1_ffn_q_scale': _L1_ffn_in['q_scale'], 'L1_ffn_k_scale': _L1_ffn_in['k_scale'], 'L1_ffn_wo': _L1_ffn_in['wo'], 'L1_ffn_ln_g': _L1_ffn_in['ln_g'], 'L1_ffn_ln_b': _L1_ffn_in['ln_b'], 'L1_ffn_w1': _L1_ffn_in['w1'], 'L1_ffn_b1': _L1_ffn_in['b1'], 'L1_ffn_w2': _L1_ffn_in['w2'], 'L1_ffn_b2': _L1_ffn_in['b2'], 'L1_c': _L1_c, 'L1_wmod': _L1_wmod}
    _x0 = _d['L0_attn_x']
    _d['L0_attn_x'] = jax.random.normal(jax.random.fold_in(jax.random.key(seed), 1), (2, 2048, 256), dtype=_x0.dtype)
    del _x0
    return _d

def reference(L0_attn_x, L0_attn_W_aiv, L0_attn_decay_bias, L0_attn_W_mix, L0_attn_b_mix, L0_ffn_router_DE, L0_ffn_w_in_shared_FD, L0_ffn_w_out_shared_DF, L0_ffn_w_swiglu_FD, L0_ffn_w_in_eDF, L0_ffn_w_swiglu_eDF, L0_ffn_w_out_eFD, L0_c, L0_wmod, L1_attn_Wq, L1_attn_Wk, L1_attn_Wv, L1_attn_Wo, L1_ffn_wqkv, L1_ffn_q_scale, L1_ffn_k_scale, L1_ffn_wo, L1_ffn_ln_g, L1_ffn_ln_b, L1_ffn_w1, L1_ffn_b1, L1_ffn_w2, L1_ffn_b2, L1_c, L1_wmod):

    def _L0_attn_ref(x, W_aiv, decay_bias, W_mix, b_mix):
        import jax, jax.numpy as jnp
        import numpy as np
        D_MODEL = 256
        N_HEADS = 16
        D_HEAD = 64
        D_REC = N_HEADS * D_HEAD
        BATCH = 4
        SEQ = 2048
        CHUNK = 64

        def _make_decay_bias():
            n_fast, n_medium, n_slow = (5, 6, 5)
            b = np.zeros(D_REC, dtype=np.float32)
            fast_end = n_fast * D_HEAD
            medium_end = (n_fast + n_medium) * D_HEAD
            b[:fast_end] = -2.2
            b[fast_end:medium_end] = 0.0
            b[medium_end:] = 4.6
            return jnp.asarray(b)

        def _chunked_scan(decay, value, chunk_size=CHUNK):
            b, s, d = decay.shape
            pad = -s % chunk_size
            if pad:
                decay = jnp.pad(decay, ((0, 0), (0, pad), (0, 0)), constant_values=1.0)
                value = jnp.pad(value, ((0, 0), (0, pad), (0, 0)))
            total = s + pad
            n = total // chunk_size
            dc = decay.reshape(b, n, chunk_size, d)
            vc = value.reshape(b, n, chunk_size, d)
            cum_log = jnp.cumsum(jnp.log(jnp.maximum(dc, 1e-10)), axis=2)
            cum_decay = jnp.exp(cum_log)
            weighted = vc / jnp.maximum(cum_decay, 1e-10)
            intra_state = cum_decay * jnp.cumsum(weighted, axis=2)
            chunk_final_state = intra_state[:, :, -1, :]
            chunk_total_decay = cum_decay[:, :, -1, :]
            cum_log_chunk = jnp.cumsum(jnp.log(jnp.maximum(chunk_total_decay, 1e-10)), axis=1)
            cum_chunk_decay = jnp.exp(cum_log_chunk)
            cum_weighted_chunk = jnp.cumsum(chunk_final_state / jnp.maximum(cum_chunk_decay, 1e-10), axis=1)
            zeros = jnp.zeros((b, 1, d), dtype=cum_weighted_chunk.dtype)
            ones = jnp.ones((b, 1, d), dtype=cum_chunk_decay.dtype)
            incoming_cum_weighted = jnp.concatenate([zeros, cum_weighted_chunk[:, :-1]], axis=1)
            incoming_cum_decay = jnp.concatenate([ones, cum_chunk_decay[:, :-1]], axis=1)
            incoming_state = incoming_cum_decay * incoming_cum_weighted
            cross_contrib = cum_decay * incoming_state[:, :, None, :]
            states = (intra_state + cross_contrib).reshape(b, total, d)[:, :s]
            return states
        aiv = x @ W_aiv
        a_proj, i_proj, v = jnp.split(aiv, 3, axis=-1)
        a = jax.nn.sigmoid(a_proj + decay_bias)
        i = jax.nn.sigmoid(i_proj)
        input_signal = jnp.sqrt(jnp.maximum(1.0 - a * a, 1e-08)) * (i * v)
        h = _chunked_scan(a.astype(jnp.float32), input_signal.astype(jnp.float32))
        h = h.astype(x.dtype)
        return h @ W_mix + b_mix

    def _L0_ffn_ref(x_bsD, router_DE, w_in_shared_FD, w_out_shared_DF, w_swiglu_FD, w_in_eDF, w_swiglu_eDF, w_out_eFD):
        import jax, jax.numpy as jnp
        import numpy as np
        TOP_K = 2
        E = 8
        D = 256
        F = 512
        B, S = (2, 256)
        b, s, d = x_bsD.shape
        x_aD = x_bsD.reshape(-1, d)
        a = x_aD.shape[0]
        scores_aE = x_aD @ router_DE
        topv_aK, topi_aK = jax.lax.top_k(scores_aE, TOP_K)
        masked_aE = jnp.full_like(scores_aE, -jnp.inf)
        masked_aE = masked_aE.at[jnp.arange(a)[:, None], topi_aK].set(topv_aK)
        gates_Ea = jax.nn.sigmoid(masked_aE.astype(jnp.float32)).astype(x_aD.dtype).T
        routed_in_EaD = x_aD[None, :, :] * gates_Ea[:, :, None]
        routed_in_EaD = jax.lax.stop_gradient(routed_in_EaD)
        mid_EaF = jnp.einsum('ead,edf->eaf', routed_in_EaD, w_in_eDF)
        sw_EaF = jnp.einsum('ead,edf->eaf', routed_in_EaD, w_swiglu_eDF)
        h_EaF = jax.nn.silu(mid_EaF) * sw_EaF
        out_EaD = jnp.einsum('eaf,efd->ead', h_EaF, w_out_eFD)
        shared_aF = jax.nn.silu(x_aD @ w_in_shared_FD.T) * (x_aD @ w_swiglu_FD.T)
        shared_out_aD = jax.lax.stop_gradient(shared_aF @ w_out_shared_DF.T)
        out_aD = shared_out_aD + jnp.sum(out_EaD, axis=0)
        return out_aD.reshape(b, s, d)

    def _L1_attn_ref(x, Wq, Wk, Wv, Wo):
        import jax, jax.numpy as jnp
        import numpy as np
        EMBED = 256
        WIN = 128
        NUM_HEADS = 16
        HQ = 16
        HKV = 4
        HEAD_DIM = EMBED // NUM_HEADS
        G = HQ // HKV
        B, S, _ = x.shape
        W = 2 * WIN + 1
        scale = 1.0 / np.sqrt(HEAD_DIM).astype(np.float32)
        Q = (x @ Wq.T).reshape(B, S, HKV, G, HEAD_DIM)
        K = (x @ Wk.T).reshape(B, S, HKV, HEAD_DIM)
        V = (x @ Wv.T).reshape(B, S, HKV, HEAD_DIM)
        offs = jnp.arange(W) - WIN
        idx = jnp.arange(S)[:, None] + offs[None, :]
        valid = (idx >= 0) & (idx < S)
        idxc = jnp.clip(idx, 0, S - 1)
        K_win = K[:, idxc]
        V_win = V[:, idxc]
        scores = jnp.einsum('bskgd,bswkd->bskgw', Q, K_win) * scale
        scores = jnp.where(valid[None, :, None, None, :], scores, jnp.float32(-jnp.inf))
        attn = jax.nn.softmax(scores, axis=-1)
        out = jnp.einsum('bskgw,bswkd->bskgd', attn, V_win)
        out = out.reshape(B, S, HQ * HEAD_DIM)
        return out @ Wo.T

    def _L1_ffn_ref(x, wqkv, q_scale, k_scale, wo, ln_g, ln_b, w1, b1, w2, b2):
        import jax, jax.numpy as jnp
        import numpy as np
        DIM = 256
        DEPTH = 2
        HEADS = 8
        DIM_HEAD = 64
        WINDOW = 128
        INNER = HEADS * DIM_HEAD
        HID = int(DIM * 4 * 2 / 3)
        B, N = (2, 2048)
        QK_SCALE = 8.0

        def shift_token(t):
            t1, t2 = jnp.split(t, 2, axis=-1)
            t2 = jnp.pad(t2, ((0, 0), (1, 0), (0, 0)))[:, :-1]
            return jnp.concatenate([t1, t2], axis=-1)

        def l2norm(t):
            return t / jnp.clip(jnp.linalg.norm(t, axis=-1, keepdims=True), 1e-12)

        def rotate_half(x):
            x1, x2 = jnp.split(x, 2, axis=-1)
            return jnp.concatenate([-x2, x1], axis=-1)

        def rotary_xpos(q, k):
            n = q.shape[-2]
            half_idx = jnp.arange(0, DIM_HEAD, 2, dtype=jnp.float32)
            inv_freq = 1.0 / 10000.0 ** (half_idx / DIM_HEAD)
            t = jnp.arange(n, dtype=jnp.float32)
            freqs = t[:, None] * inv_freq[None, :]
            freqs = jnp.concatenate([freqs, freqs], axis=-1)
            base = (half_idx + 0.4 * DIM_HEAD) / (1.4 * DIM_HEAD)
            power = (t - n // 2) / float(WINDOW // 2)
            scale = base[None, :] ** power[:, None]
            scale = jnp.concatenate([scale, scale], axis=-1)
            cos, sin = (jnp.cos(freqs), jnp.sin(freqs))
            q = q * cos * scale + rotate_half(q) * sin * scale
            k = k * cos / scale + rotate_half(k) * sin / scale
            return (q, k)

        def local_attention(q, k, v):
            b, h, n, d = q.shape
            w = n // WINDOW
            bq = q.reshape(b, h, w, WINDOW, d) * QK_SCALE
            bk = k.reshape(b, h, w, WINDOW, d)
            bv = v.reshape(b, h, w, WINDOW, d)

            def look_around(t):
                p = jnp.pad(t, ((0, 0), (0, 0), (1, 0), (0, 0), (0, 0)))
                return jnp.concatenate([p[:, :, :w], p[:, :, 1:]], axis=3)
            bk, bv = (look_around(bk), look_around(bv))
            bt = jnp.arange(n).reshape(w, WINDOW)
            btp = jnp.pad(bt, ((1, 0), (0, 0)), constant_values=-1)
            btk = jnp.concatenate([btp[:w], btp[1:]], axis=1)
            sim = jnp.einsum('bhwid,bhwjd->bhwij', bq, bk)
            i = bt[:, :, None]
            j = btk[:, None, :]
            mask = (i < j) | (i > j + WINDOW) | (j == -1)
            sim = jnp.where(mask, -jnp.finfo(sim.dtype).max, sim)
            attn = jax.nn.softmax(sim, axis=-1)
            out = jnp.einsum('bhwij,bhwjd->bhwid', attn, bv)
            return out.reshape(b, h, n, d)

        def _layer(x, wqkv, qs, ksc, wo, lg, lb, w1, b1, w2, b2):
            b, n, _ = x.shape
            h = shift_token(x)
            qkv = h @ wqkv
            q, k, v = jnp.split(qkv, 3, axis=-1)
            to_heads = lambda t: t.reshape(b, n, HEADS, DIM_HEAD).transpose(0, 2, 1, 3)
            q, k, v = (to_heads(q), to_heads(k), to_heads(v))
            q = l2norm(q) * qs
            k = l2norm(k) * ksc
            q, k = rotary_xpos(q, k)
            o = local_attention(q, k, v)
            o = o.transpose(0, 2, 1, 3).reshape(b, n, INNER)
            x = x + o @ wo
            h = shift_token(x)
            mu = h.mean(-1, keepdims=True)
            var = h.var(-1, keepdims=True)
            h = (h - mu) / jnp.sqrt(var + 1e-05) * lg + lb
            h = h @ w1 + b1
            a, g = jnp.split(h, 2, axis=-1)
            h = a * jax.nn.gelu(g, approximate=False)
            x = x + h @ w2 + b2
            return x
        for l in range(DEPTH):
            x = _layer(x, wqkv[l], q_scale[l], k_scale[l], wo[l], ln_g[l], ln_b[l], w1[l], b1[l], w2[l], b2[l])
        return x
    x = L0_attn_x
    mod = (_silu(L0_c) @ L0_wmod).reshape(L0_c.shape[0], 6, 1, -1)
    sa, ca, ga, sb, cb, gb = (mod[:, 0], mod[:, 1], mod[:, 2], mod[:, 3], mod[:, 4], mod[:, 5])
    ga = (2 * (ga >= 0) - 1) * jnp.maximum(jnp.abs(ga), 0.25)
    gb = (2 * (gb >= 0) - 1) * jnp.maximum(jnp.abs(gb), 0.25)
    h = _layernorm(x, axis=-1) * (1 + ca) + sa
    x = x + ga * _L0_attn_ref(h, L0_attn_W_aiv, L0_attn_decay_bias, L0_attn_W_mix, L0_attn_b_mix)
    h = _layernorm(x, axis=-1) * (1 + cb) + sb
    x = x + gb * _L0_ffn_ref(h, L0_ffn_router_DE, L0_ffn_w_in_shared_FD, L0_ffn_w_out_shared_DF, L0_ffn_w_swiglu_FD, L0_ffn_w_in_eDF, L0_ffn_w_swiglu_eDF, L0_ffn_w_out_eFD)
    mod = (_silu(L1_c) @ L1_wmod).reshape(L1_c.shape[0], 6, 1, -1)
    sa, ca, ga, sb, cb, gb = (mod[:, 0], mod[:, 1], mod[:, 2], mod[:, 3], mod[:, 4], mod[:, 5])
    ga = (2 * (ga >= 0) - 1) * jnp.maximum(jnp.abs(ga), 0.25)
    gb = (2 * (gb >= 0) - 1) * jnp.maximum(jnp.abs(gb), 0.25)
    h = _layernorm(x, axis=-1) * (1 + ca) + sa
    x = x + ga * _L1_attn_ref(h, L1_attn_Wq, L1_attn_Wk, L1_attn_Wv, L1_attn_Wo)
    h = _layernorm(x, axis=-1) * (1 + cb) + sb
    x = x + gb * _L1_ffn_ref(h, L1_ffn_wqkv, L1_ffn_q_scale, L1_ffn_k_scale, L1_ffn_wo, L1_ffn_ln_g, L1_ffn_ln_b, L1_ffn_w1, L1_ffn_b1, L1_ffn_w2, L1_ffn_b2)
    return x

_drawn_inputs = setup_inputs


def setup_inputs(seed=0):
    import zlib

    import numpy as np

    out = dict(_drawn_inputs(seed))
    spreads = {'L0_attn_b_mix': (0.0, 0.338),
     'L1_ffn_q_scale': (1.0, 0.6),
     'L1_ffn_k_scale': (1.0, 0.6),
     'L1_ffn_ln_g': (1.0, 0.6),
     'L1_ffn_ln_b': (0.0, 0.8),
     'L1_ffn_b1': (0.0, 0.8),
     'L1_ffn_b2': (0.0, 0.538)}
    factors = {'L0_ffn_router_DE': 8.0,
     'L0_ffn_w_in_shared_FD': 8.0,
     'L0_ffn_w_out_shared_DF': 8.0,
     'L0_ffn_w_swiglu_FD': 8.0,
     'L0_ffn_w_in_eDF': 8.0,
     'L0_ffn_w_swiglu_eDF': 8.0,
     'L0_ffn_w_out_eFD': 8.0,
     'L1_attn_Wq': 8.0,
     'L1_attn_Wk': 8.0,
     'L1_attn_Wv': 8.0,
     'L1_attn_Wo': 8.0,
     'L1_ffn_wqkv': 6.906,
     'L1_ffn_wo': 6.98,
     'L1_ffn_w1': 4.839,
     'L1_ffn_w2': 4.805}
    for name, (base, spread) in spreads.items():
        noise = np.random.default_rng([zlib.crc32(name.encode()), seed]).standard_normal(out[name].shape)
        drawn = base * np.exp(spread * noise) if base else spread * noise
        out[name] = jnp.asarray(drawn.astype(out[name].dtype))
    for name, factor in factors.items():
        out[name] = (out[name] * factor).astype(out[name].dtype)
    return out
```

```python
from contextlib import ExitStack

import numpy as np

import concourse.bass as bass
from concourse import mybir

F32 = mybir.dt.float32
BF16 = mybir.dt.bfloat16
U32 = mybir.dt.uint32
ALU = mybir.AluOpType
ACT = mybir.ActivationFunctionType
AX_X = mybir.AxisListType.X

P = 128
D = 256
KD = D // P
NB = 2
SEQ = 2048
TPB = SEQ // P
NT = NB * TPB
BLK = 512
TB = BLK // P
NBLK = SEQ // BLK
EPS = 1e-5
MODS = ("shift_a", "scale_a", "gate_a", "shift_b", "scale_b", "gate_b")
SHIFT_A, SCALE_A, GATE_A, SHIFT_B, SCALE_B, GATE_B = range(6)
LN_SET = "natural_log_exp_and_others"

REC = 1024
NG = REC // P
CHUNK = 64
CPB = BLK // CHUNK
LN_TINY = float(np.log(1e-10))
U_SCALE = 2.0 ** -10
U_LOG = float(10 * np.log(2.0) / 2)
SIG_FLOOR = float(0.5 * np.log(1e-8)) - U_LOG

AH = 16
AHD = 16
AKV = 4
AG = AH // AKV
HPC = P // AHD
AW = 3 * P
HPR = 2

DEPTH = 2
LH = 8
LHD = 64
INNER = LH * LHD
KI = INNER // P
HID = 682
KH = -(-HID // P)
HTAIL = HID - (KH - 1) * P
QK_SCALE = 8.0
SS_SCALE = 2.0 ** 20
SS_LOG = float(10 * np.log(2.0))

EXP = 8
FF = 512
KF = FF // P


def on_all(vector, n):
    return vector.rearrange("(a n) -> a n", a=1).broadcast_to([P, n])


class Pool:

    def __init__(self, nc, ctx, name):
        self.nc, self.ctx, self.name = nc, ctx, name
        self.sems = []

    def sb(self, name, shape, dt=F32):
        return self.ctx.enter_context(self.nc.sbuf_tensor(f"sb_{self.name}_{name}", shape, dt))

    def ps(self, name, shape, dt=F32):
        return self.ctx.enter_context(self.nc.psum_tensor(f"ps_{self.name}_{name}", shape, dt))

    def sem(self, name):
        self.sems.append(self.ctx.enter_context(self.nc.semaphore(f"{self.name}_{name}")))
        return self.sems[-1]

    def clear(self):
        with self.nc.Block() as block:
            @block.gpsimd
            def _(pool):
                for sem in self.sems:
                    pool.sem_clear(sem)


class BlockNorm:

    def __init__(self, m, keep, halves, scale, shift):
        self.nc, self.keep, self.halves, self.scale, self.shift = m.nc, keep, halves, scale, shift
        self.stats = m.sb("stats", [P, NB, TB, KD, 6])
        self.mv = m.sb("mv", [P, NB, TB, 2])
        self.settle = m.sb("settle", [P, 1])
        self.lnv = m.sb("lnv", [P, NB, TB])
        self.rstd = m.sb("rstd", [P, NB, TB])
        self.nmr = m.sb("nmr", [P, NB, TB])
        self.xn = m.sb("xn", [P, NB, TB, D])
        self.hT = m.sb("hT", [P, NB, KD, BLK])
        (self.s_st, self.s_mv, self.s_ln, self.s_rstd, self.s_nmr, self.s_xn, self.s_tr, self.s_hT) = (
            m.sem(n) for n in ("stats", "mv", "lnv", "rstd", "nmr", "xn", "tr", "hT"))

    def normalise(self, dve, it, j=None):
        nc = self.nc
        j = it if j is None else j
        for b in range(NB):
            for t in range(TB):
                parts = self.halves(b, t, j)
                for k, part in enumerate(parts):
                    i = nc.vector.bn_stats(self.stats[:, b, t, k], part)
            i.then_inc(self.s_st, 1)
        dve.wait_ge(self.s_st, it * NB + NB)
        nc.vector.memset(self.settle[:], 0.0)
        for b in range(NB):
            for t in range(TB):
                i = nc.vector.bn_aggr(self.mv[:, b, t], self.stats[:, b, t, 0:len(self.halves(b, t, j))])
            i.then_inc(self.s_mv, 1)
        for b in range(NB):
            dve.wait_ge(self.s_rstd, it * NB + b + 1)
            dve.wait_ge(self.s_mv, it * NB + b + 1)
            nc.vector.scalar_tensor_tensor(out=self.nmr[:, b], in0=self.mv[:, b, :, 0], scalar=-1.0,
                                           in1=self.rstd[:, b], op0=ALU.mult, op1=ALU.mult).then_inc(self.s_nmr, 1)
            dve.wait_ge(self.s_nmr, it * NB + b + 1)
            for t in range(TB):
                parts = self.halves(b, t, j)
                w = D // len(parts)
                for k, part in enumerate(parts):
                    i = nc.vector.tensor_scalar(self.xn[:, b, t, k * w:(k + 1) * w], part, self.rstd[:, b, t:t + 1],
                                                self.nmr[:, b, t:t + 1], ALU.mult, ALU.add)
            i.then_inc(self.s_xn, 1)

    def inverse_deviation(self, act, it):
        nc = self.nc
        for b in range(NB):
            act.wait_ge(self.s_mv, it * NB + b + 1)
            nc.scalar.activation(self.lnv[:, b], self.mv[:, b, :, 1], ACT.Ln,
                                 bias=self.keep["eps"][:, 0:1]).then_inc(self.s_ln, 1)
            act.wait_ge(self.s_ln, it * NB + b + 1)
            nc.scalar.activation(self.rstd[:, b], self.lnv[:, b], ACT.Exp, scale=-0.5).then_inc(self.s_rstd, 1)

    def transpose(self, pe, it, psum):
        for b in range(NB):
            pe.wait_ge(self.s_xn, it * NB + b + 1)
            for k in range(KD):
                for t in range(TB):
                    i = self.nc.tensor.transpose(psum(b, k)[:, t * P:(t + 1) * P],
                                                 self.xn[:, b, t, k * P:(k + 1) * P], self.keep["ident"][:])
            i.then_inc(self.s_tr, 1)

    def affine(self, act, it, psum):
        for b in range(NB):
            act.wait_ge(self.s_tr, it * NB + b + 1)
            for k in range(KD):
                i = self.nc.scalar.activation(self.hT[:, b, k], psum(b, k), ACT.Identity,
                                              scale=self.scale(b, k), bias=self.shift(b, k))
            i.then_inc(self.s_hT, 1)


def load_and_modulate(nc, a, keep):
    with ExitStack() as ctx:
        m = Pool(nc, ctx, "mod")
        cT = m.sb("cT", [P, 2, KD, NB])
        cs = m.sb("cs", [P, 2, KD, NB])
        cwide = m.sb("cwide", [P, 2, KD, NB, P])
        wmod = m.sb("wmod", [P, 2, KD, 6 * D])
        rows = m.sb("rows", [P, 2, NB, 6 * D])
        sign = m.sb("sign", [P, 4, D])
        size = m.sb("size", [P, 4, D])
        ps_row = m.ps("ps_row", [P, 2, 512])
        ps_col = m.ps("ps_col", [P, 2, 512])
        s_c, s_w, s_x, s_k, s_bm = (m.sem(n) for n in ("c_in", "wmod_in", "x_in", "const_in", "bmix_in"))
        s_silu, s_wide, s_row, s_rowcp, s_col, s_colcp = (
            m.sem(n) for n in ("silu", "wide", "row", "rowcp", "col", "colcp"))
        s_g = m.sem("guard")

        with nc.Block() as block:
            @block.sync
            def _(sp):
                for l, name in enumerate(("L0_c", "L1_c")):
                    sp.dma_start(cT[:, l], a[name].rearrange("(k p) b -> p k b", p=P)).then_inc(s_c, 16)
                for l, name in enumerate(("L0_wmod", "L1_wmod")):
                    sp.dma_start(wmod[:, l], a[name].rearrange("(k p) n -> p k n", p=P)).then_inc(s_w, 16)
                sp.dma_start(keep["ident"][:], a["ident"]).then_inc(s_k, 16)
                sp.dma_start(keep["bmix_gated"][:, 0], on_all(a["L0_attn_b_mix"], D)).then_inc(s_bm, 16)
                sp.dma_start(keep["x"][:], a["x"].rearrange("(t p) d -> p t d", p=P)).then_inc(s_x, 16)
                sp.wait_ge(s_k, 16)
                sp.wait_ge(s_x, 16)

            @block.scalar
            def _(act):
                act.wait_ge(s_c, 32)
                nc.scalar.activation(cs[:], cT[:], ACT.Silu).then_inc(s_silu, 1)
                for n in range(12):
                    act.wait_ge(s_row, n + 1)
                    l, b, c = n // 6, n // 3 % 2, n % 3
                    nc.scalar.copy(rows[:, l, b, c * 512:(c + 1) * 512], ps_row[:, n % 2]).then_inc(s_rowcp, 1)

            @block.tensor
            def _(pe):
                pe.wait_ge(s_w, 32)
                pe.wait_ge(s_silu, 1)
                for l in range(2):
                    for c in range(6 * KD):
                        for k in range(KD):
                            mm = nc.tensor.matmul(ps_col[:, l, 2 * c:2 * c + 2], wmod[:, l, k, c * P:(c + 1) * P],
                                                  cs[:, l, k], start=(k == 0), stop=(k == KD - 1))
                mm.then_inc(s_col, 1)
                pe.wait_ge(s_wide, 1)
                for n in range(12):
                    l, b, c = n // 6, n // 3 % 2, n % 3
                    if n >= 2:
                        pe.wait_ge(s_rowcp, n - 1)
                    for k in range(KD):
                        mm = nc.tensor.matmul(ps_row[:, n % 2], cwide[:, l, k, b],
                                              wmod[:, l, k, c * 512:(c + 1) * 512], start=(k == 0), stop=(k == KD - 1))
                    mm.then_inc(s_row, 1)

            @block.vector
            def _(dve):
                dve.wait_ge(s_silu, 1)
                for l in range(2):
                    for k in range(KD):
                        i = nc.vector.tensor_copy(cwide[:, l, k], cs[:, l, k].unsqueeze(2).broadcast_to([P, NB, P]))
                i.then_inc(s_wide, 1)
                dve.wait_ge(s_col, 1)
                nc.vector.tensor_copy(keep["modf"][:], ps_col[:, :, 0:24].rearrange("p l (j n) -> p l j n", n=2 * KD)
                                      ).then_inc(s_colcp, 1)
                dve.wait_ge(s_colcp, 1)
                for j in (SCALE_A, SCALE_B):
                    nc.vector.tensor_scalar(keep["modf"][:, :, j], keep["modf"][:, :, j], 1.0, None,
                                            ALU.add).then_inc(s_colcp, 1)
                dve.wait_ge(s_rowcp, 12)
                n = 0
                for l in range(2):
                    for w, j in enumerate((GATE_A, GATE_B)):
                        g = rows[:, l, :, j * D:(j + 1) * D]
                        sg = sign[:, 2 * w:2 * w + 2]
                        sz = size[:, 2 * w:2 * w + 2]
                        nc.vector.tensor_scalar(sg, g, 0.0, 2.0, ALU.is_ge, ALU.mult).then_inc(s_g, 1)
                        nc.vector.scalar_tensor_tensor(out=sz, in0=g, scalar=-1.0, in1=g, op0=ALU.mult,
                                                       op1=ALU.max).then_inc(s_g, 1)
                        dve.wait_ge(s_g, n + 2)
                        nc.vector.tensor_scalar(sz, sz, 0.25, None, ALU.max).then_inc(s_g, 1)
                        dve.wait_ge(s_g, n + 3)
                        nc.vector.scalar_tensor_tensor(out=keep["gates"][:, l, w], in0=sg, scalar=-1.0, in1=sz,
                                                       op0=ALU.add, op1=ALU.mult).then_inc(s_g, 1)
                        n += 4
                        dve.wait_ge(s_g, n)
                nc.vector.tensor_scalar(keep["scale_row"][:], rows[:, 1, :, SCALE_B * D:(SCALE_B + 1) * D], 1.0, None,
                                        ALU.add).then_inc(s_g, 1)
                nc.vector.tensor_copy(keep["shift_row"][:], rows[:, 1, :, SHIFT_B * D:(SHIFT_B + 1) * D]).then_inc(s_g, 1)
                dve.wait_ge(s_bm, 16)
                bm = keep["bmix_gated"]
                nc.vector.tensor_tensor(bm[:, 1], bm[:, 0], keep["gates"][:, 0, 0, 1], ALU.mult).then_inc(s_g, 1)
                dve.wait_ge(s_g, n + 3)
                nc.vector.tensor_tensor(bm[:, 0], bm[:, 0], keep["gates"][:, 0, 0, 0], ALU.mult).then_inc(s_g, 1)
                dve.wait_ge(s_g, n + 4)
                dve.wait_ge(s_colcp, 3)
        m.clear()


def gated_recurrence(nc, a, keep):
    x, modf, ident = keep["x"], keep["modf"], keep["ident"]
    with ExitStack() as ctx:
        m = Pool(nc, ctx, "rec")
        w = m.sb("w", [P, KD, 3 * REC])
        wmix = m.sb("wmix", [P, NG, D])
        nbias = m.sb("nbias", [P, NG])
        keepmask = m.sb("keepmask", [P, BLK])
        ones = m.sb("ones", [P, CPB])
        norm = BlockNorm(m, keep, lambda b, t, it: [x[:, bass.ds(it * TB + b * TPB + t, 1)]],
                         lambda b, k: modf[:, 0, SCALE_A, NB * k + b:NB * k + b + 1],
                         lambda b, k: modf[:, 0, SHIFT_A, NB * k + b:NB * k + b + 1])
        hT = norm.hT
        e = m.sb("e", [P, 2, 2, BLK])
        u = m.sb("u", [P, 2, BLK])
        l = m.sb("l", [P, 2, 2, BLK])
        lu = m.sb("lu", [P, 2, BLK])
        cum = m.sb("cum", [P, 2, BLK])
        q = m.sb("q", [P, 2, BLK])
        z = m.sb("z", [P, 2, BLK])
        ez = m.sb("ez", [P, 2, BLK])
        dec = m.sb("dec", [P, 2, BLK])
        wt = m.sb("wt", [P, 2, BLK])
        ws = m.sb("ws", [P, 2, BLK])
        st = m.sb("st", [P, 3, BLK])
        last = m.sb("last", [P, 2, CPB])
        lc = m.sb("lc", [P, NB, NG, CPB + 1])
        lcm = m.sb("lcm", [P, 2, CPB])
        c9 = m.sb("c9", [P, 2, CPB])
        rc = m.sb("rc", [P, 2, CPB])
        fin = m.sb("fin", [P, 2, CPB])
        fin2 = m.sb("fin2", [P, 2, CPB])
        cw = m.sb("cw", [P, NB, NG, CPB + 1])
        inc = m.sb("inc", [P, 2, CPB])
        og = m.sb("og", [P, TB, D])
        ps = m.ps("ps", [P, 2, 3, BLK])
        pso = m.ps("pso", [P, TB, D])

        s_w, s_wm = m.sem("w_in"), m.sem("wmix_in")
        (s_aiv, s_e, s_ec, s_u, s_l, s_lu, s_cum, s_q, s_q2, s_z, s_last, s_lc, s_lcm, s_ez, s_rc) = (
            m.sem(n) for n in ("aiv", "e", "ec", "u", "l", "lu", "cum", "q", "q2", "z", "last", "lc", "lcm", "ez", "rc"))
        (s_wt, s_ws, s_fin, s_fin2, s_cw, s_inc, s_carry, s_wi, s_state, s_mix, s_og, s_ogb, s_x) = (
            m.sem(n) for n in ("wt", "ws", "fin", "fin2", "cw", "inc", "carry", "wi", "state", "mix", "og", "ogb", "x"))
        s_init = m.sem("init")
        US = NB * NG

        with nc.Block() as block:
            @block.sync
            def _(sp):
                for k in range(KD):
                    sp.dma_start(w[:, k], a["L0_attn_W_aiv"][k * P:(k + 1) * P]).then_inc(s_w, 16)
                sp.dma_start(nbias[:], a["L0_attn_decay_bias"]).then_inc(s_w, 16)
                sp.dma_start(keepmask[:], on_all(a["keepmask"], BLK)).then_inc(s_w, 16)
                sp.dma_start(wmix[:], a["L0_attn_W_mix"].rearrange("(g p) d -> p g d", p=P)).then_inc(s_wm, 16)

            @block.gpsimd
            def _(pool):
                with pool.Fori(0, NBLK) as it:
                    for s in range(US + 1):
                        if s >= 1:
                            b, g, par, n = (s - 1) // NG, (s - 1) % NG, (s - 1) % 2, it * US + s
                            pool.wait_ge(s_inc, n)
                            nc.gpsimd.tensor_tensor(ws[:, par].rearrange("p (c t) -> p c t", c=CPB),
                                                    ws[:, par].rearrange("p (c t) -> p c t", c=CPB),
                                                    inc[:, par].unsqueeze(2).broadcast_to([P, CPB, CHUNK]),
                                                    ALU.add).then_inc(s_wi, 1)
                            pool.wait_ge(s_wi, n)
                            nc.gpsimd.tensor_tensor(st[:, (s - 1) % 3], ws[:, par], dec[:, par],
                                                    ALU.mult).then_inc(s_state, 1)
                        if s and s % NG == 0:
                            b = s // NG - 1
                            pool.wait_ge(s_og, it * NB + b + 1)
                            nc.gpsimd.tensor_tensor(og[:], og[:], keep["bmix_gated"][:, b:b + 1].broadcast_to([P, TB, D]),
                                                    ALU.add).then_inc(s_ogb, 1)
                            pool.wait_ge(s_ogb, it * NB + b + 1)
                            xt = x[:, bass.ds(it * TB + b * TPB, TB)]
                            nc.gpsimd.tensor_tensor(xt, xt, og[:], ALU.add).then_inc(s_x, 1)

            @block.scalar
            def _(act):
                nc.scalar.preload_act_table_set(LN_SET)
                act.wait_ge(s_init, 1)
                with act.Fori(0, NBLK) as it:
                    norm.inverse_deviation(act, it)
                    norm.affine(act, it, lambda b, k: ps[:, b, k])

                    def first(s):
                        b, g, par, n = s // NG, s % NG, s % 2, it * US + s
                        act.wait_ge(s_aiv, n + 1)
                        nc.scalar.activation(e[:, par, 0], ps[:, par, 0], ACT.Exp, scale=-1.0, bias=nbias[:, g:g + 1])
                        nc.scalar.activation(e[:, par, 1], ps[:, par, 1], ACT.Exp, scale=-1.0).then_inc(s_e, 1)

                    def logs(s):
                        par, n = s % 2, it * US + s
                        act.wait_ge(s_ec, n + 1)
                        nc.scalar.activation(l[:, par], e[:, par], ACT.Ln, bias=1.0).then_inc(s_l, 1)
                        act.wait_ge(s_u, n + 1)
                        nc.scalar.activation(lu[:, par], u[:, par], ACT.Ln, scale=U_SCALE).then_inc(s_lu, 1)

                    def exps(s):
                        b, g, par, n = s // NG, s % NG, s % 2, it * US + s
                        act.wait_ge(s_z, n + 1)
                        nc.scalar.activation(ez[:, par], z[:, par], ACT.Exp, scale=-1.0,
                                             bias=keep["u_log"][:, 0:1]).then_inc(s_ez, 1)
                        act.wait_ge(s_lcm, n + 1)
                        if s >= 2:
                            act.wait_ge(s_state, n - 1)
                        nc.scalar.activation(dec[:, par], cum[:, par], ACT.Exp)
                        nc.scalar.activation(c9[:, par], lc[:, b, g, 0:CPB], ACT.Exp)
                        nc.scalar.activation(rc[:, par], lcm[:, par], ACT.Exp, scale=-1.0).then_inc(s_rc, 1)

                    for s in range(US + 1):
                        if s < US:
                            first(s)
                        if s >= 1:
                            exps(s - 1)
                        if s < US:
                            logs(s)

            @block.vector
            def _(dve):
                nc.vector.memset(lc[:], 0.0)
                nc.vector.memset(cw[:], 0.0)
                nc.vector.memset(ones[:], 1.0)
                dve.wait_ge(s_w, 16 * 4)
                nc.vector.tensor_scalar(nbias[:], nbias[:], -1.0, None, ALU.mult).then_inc(s_init, 1)
                dve.wait_ge(s_init, 1)
                with dve.Fori(0, NBLK) as it:
                    norm.normalise(dve, it)

                    def clamp(s):
                        par, n = s % 2, it * US + s
                        dve.wait_ge(s_e, n + 1)
                        nc.vector.tensor_scalar(e[:, par, 0], e[:, par, 0], 1e-12, 1e10, ALU.max, ALU.min)
                        nc.vector.tensor_scalar(e[:, par, 1], e[:, par, 1], 1e19, None, ALU.min).then_inc(s_ec, 1)
                        dve.wait_ge(s_ec, n + 1)
                        nc.vector.scalar_tensor_tensor(out=u[:, par], in0=e[:, par, 0], scalar=2.0, in1=e[:, par, 0],
                                                       op0=ALU.add, op1=ALU.mult).then_inc(s_u, 1)

                    def sums(s):
                        b, g, par, n = s // NG, s % NG, s % 2, it * US + s
                        dve.wait_ge(s_l, n + 1)
                        nc.vector.tensor_tensor_scan(cum[:, par], keepmask[:], l[:, par, 0], 0.0, ALU.mult,
                                                     ALU.subtract).then_inc(s_cum, 1)
                        dve.wait_ge(s_lu, n + 1)
                        nc.vector.scalar_tensor_tensor(out=q[:, par], in0=lu[:, par], scalar=0.5, in1=l[:, par, 0],
                                                       op0=ALU.mult, op1=ALU.subtract).then_inc(s_q, 1)
                        dve.wait_ge(s_q, n + 1)
                        nc.vector.scalar_tensor_tensor(out=q[:, par], in0=q[:, par], scalar=SIG_FLOOR, in1=l[:, par, 1],
                                                       op0=ALU.max, op1=ALU.subtract).then_inc(s_q2, 1)
                        dve.wait_ge(s_q2, n + 1)
                        nc.vector.scalar_tensor_tensor(out=z[:, par], in0=cum[:, par], scalar=LN_TINY, in1=q[:, par],
                                                       op0=ALU.max, op1=ALU.subtract).then_inc(s_z, 1)
                        ends = cum[:, par].rearrange("p (c t) -> p c t", c=CPB)[:, :, CHUNK - 1]
                        nc.vector.tensor_scalar(last[:, par], ends, LN_TINY, None, ALU.max).then_inc(s_last, 1)
                        dve.wait_ge(s_last, n + 1)
                        nc.vector.tensor_tensor_scan(lc[:, b, g, 1:CPB + 1], ones[:], last[:, par], lc[:, b, g, 0:1],
                                                     ALU.mult, ALU.add).then_inc(s_lc, 1)
                        dve.wait_ge(s_lc, n + 1)
                        nc.vector.tensor_scalar(lcm[:, par], lc[:, b, g, 1:CPB + 1], LN_TINY, None,
                                                ALU.max).then_inc(s_lcm, 1)

                    def states(s):
                        b, g, par, n = s // NG, s % NG, s % 2, it * US + s
                        dve.wait_ge(s_ez, n + 1)
                        nc.vector.tensor_tensor(wt[:, par], ps[:, par, 2], ez[:, par], ALU.mult).then_inc(s_wt, 1)
                        dve.wait_ge(s_wt, n + 1)
                        if s >= 2:
                            dve.wait_ge(s_state, n - 1)
                        nc.vector.tensor_tensor_scan(ws[:, par], keepmask[:], wt[:, par], 0.0, ALU.mult,
                                                     ALU.add).then_inc(s_ws, 1)
                        dve.wait_ge(s_rc, n + 1)
                        dve.wait_ge(s_ws, n + 1)
                        wend = ws[:, par].rearrange("p (c t) -> p c t", c=CPB)[:, :, CHUNK - 1]
                        dend = dec[:, par].rearrange("p (c t) -> p c t", c=CPB)[:, :, CHUNK - 1]
                        nc.vector.tensor_tensor(fin[:, par], wend, dend, ALU.mult).then_inc(s_fin, 1)
                        dve.wait_ge(s_fin, n + 1)
                        nc.vector.tensor_tensor(fin2[:, par], fin[:, par], rc[:, par], ALU.mult).then_inc(s_fin2, 1)
                        dve.wait_ge(s_fin2, n + 1)
                        nc.vector.tensor_tensor_scan(cw[:, b, g, 1:CPB + 1], ones[:], fin2[:, par], cw[:, b, g, 0:1],
                                                     ALU.mult, ALU.add).then_inc(s_cw, 1)
                        dve.wait_ge(s_cw, n + 1)
                        nc.vector.tensor_tensor(inc[:, par], cw[:, b, g, 0:CPB], c9[:, par], ALU.mult).then_inc(s_inc, 1)
                        dve.wait_ge(s_inc, n + 1)
                        nc.vector.tensor_copy(lc[:, b, g, 0:1], lc[:, b, g, CPB:CPB + 1])
                        nc.vector.tensor_copy(cw[:, b, g, 0:1], cw[:, b, g, CPB:CPB + 1]).then_inc(s_carry, 1)

                    for s in range(US + 1):
                        if s < US:
                            clamp(s)
                        if s >= 1:
                            states(s - 1)
                        if s < US:
                            sums(s)
                        if s and s % NG == 0:
                            b = s // NG - 1
                            dve.wait_ge(s_mix, it * NB + b + 1)
                            if b:
                                dve.wait_ge(s_x, it * NB + b)
                            nc.vector.tensor_tensor(og[:], pso[:], keep["gates"][:, 0, 0, b:b + 1].broadcast_to([P, TB, D]),
                                                    ALU.mult).then_inc(s_og, 1)
                    dve.wait_ge(s_x, it * NB + NB)

            @block.tensor
            def _(pe):
                pe.wait_ge(s_w, 16 * 4)
                pe.wait_ge(s_wm, 16)
                with pe.Fori(0, NBLK) as it:
                    norm.transpose(pe, it, lambda b, k: ps[:, b, k])

                    def project(s):
                        b, g, par, n = s // NG, s % NG, s % 2, it * US + s
                        pe.wait_ge(norm.s_hT, it * NB + NB)
                        if s >= 2:
                            pe.wait_ge(s_wt, n - 1)
                        for j in range(3):
                            for k in range(KD):
                                i = nc.tensor.matmul(ps[:, par, j], w[:, k, j * REC + g * P:j * REC + (g + 1) * P],
                                                     hT[:, b, k], start=(k == 0), stop=(k == KD - 1))
                        i.then_inc(s_aiv, 1)

                    def mix(s):
                        b, g, n = s // NG, s % NG, it * US + s
                        pe.wait_ge(s_state, n + 1)
                        if g == 0 and b:
                            pe.wait_ge(s_og, it * NB + b)
                        for t in range(TB):
                            i = nc.tensor.matmul(pso[:, t], st[:, s % 3, t * P:(t + 1) * P], wmix[:, g],
                                                 start=(g == 0 and t % 2 == 0), stop=(g == NG - 1 and t % 2 == 1),
                                                 skip_group_check=True)
                        if g == NG - 1:
                            i.then_inc(s_mix, 1)

                    for s in range(US + 2):
                        if s < US:
                            project(s)
                        if s >= 2:
                            mix(s - 2)
                    pe.wait_ge(s_og, it * NB + NB)
        m.clear()


def experts(nc, a, keep):
    x, modf, ident = keep["x"], keep["modf"], keep["ident"]
    with ExitStack() as ctx:
        m = Pool(nc, ctx, "moe")
        norm = BlockNorm(m, keep, lambda b, t, it: [x[:, bass.ds(it * TB + b * TPB + t, 1)]],
                         lambda b, k: modf[:, 0, SCALE_B, NB * k + b:NB * k + b + 1],
                         lambda b, k: modf[:, 0, SHIFT_B, NB * k + b:NB * k + b + 1])
        hT = norm.hT
        w_in = m.sb("w_in", [P, EXP + 1, KD, FF])
        w_sw = m.sb("w_sw", [P, EXP + 1, KD, FF])
        w_out = m.sb("w_out", [P, EXP + 1, KF, D])
        router = m.sb("router", [P, KD, EXP])
        number = m.sb("number", [P, EXP])
        score = m.sb("score", [P, TB, EXP])
        top = m.sb("top", [P, TB, 8])
        topi = m.sb("topi", [P, TB, 8], U32)
        topf = m.sb("topf", [P, TB, 8])
        chosen = m.sb("chosen", [P, TB, EXP])
        es = m.sb("es", [P, TB, EXP])
        gate = m.sb("gate", [P, NB, TB, EXP])
        gateT = m.sb("gateT", [EXP, NB, BLK])
        routed = m.sb("routed", [P, 2, KD, BLK])
        act_f = m.sb("act_f", [P, 2, BLK])
        hid = m.sb("hid", [P, 2, KF, BLK])
        og = norm.xn[:, 0]
        ps = m.ps("ps", [P, 2, 2, BLK])
        pso = m.ps("pso", [P, TB, D])
        psg = m.ps("psg", [P, 2, BLK])
        names = ("w_load score scorecp top topi topf pick0 chosen es es1 sig gate gateTp gateT gbc routed pair silu hid "
                 "out og xadd")
        (s_w, s_score, s_scorecp, s_top, s_topi, s_topf, s_pick0, s_chosen, s_es, s_es1, s_sig, s_gate, s_gateTp,
         s_gateT, s_gbc, s_routed, s_pair, s_silu, s_hid, s_out, s_og, s_x) = (m.sem(n) for n in names.split())
        UE = NB * (EXP + 1)
        UF = UE * KF

        with nc.Block() as block:
            @block.sync
            def _(sp):
                sp.dma_start(router[:], a["L0_ffn_router_DE"].rearrange("(k p) e -> p k e", p=P)).then_inc(s_w, 16)
                sp.dma_start(number[:], on_all(a["number"], EXP)).then_inc(s_w, 16)
                for e in range(EXP):
                    sp.dma_start(w_in[:, e], a["L0_ffn_w_in_eDF"][e].rearrange("(k p) f -> p k f", p=P)).then_inc(s_w, 16)
                    sp.dma_start(w_sw[:, e], a["L0_ffn_w_swiglu_eDF"][e].rearrange("(k p) f -> p k f", p=P)).then_inc(s_w, 16)
                    sp.dma_start(w_out[:, e], a["L0_ffn_w_out_eFD"][e].rearrange("(k p) d -> p k d", p=P)).then_inc(s_w, 16)
                sp.dma_start(w_in[:, EXP], a["shared_in"].rearrange("(k p) f -> p k f", p=P)).then_inc(s_w, 16)
                sp.dma_start(w_sw[:, EXP], a["shared_sw"].rearrange("(k p) f -> p k f", p=P)).then_inc(s_w, 16)
                sp.dma_start(w_out[:, EXP], a["shared_out"].rearrange("(k p) d -> p k d", p=P)).then_inc(s_w, 16)

            @block.gpsimd
            def _(pool):
                with pool.Fori(0, NBLK) as it:
                    for b in range(NB):
                        pool.wait_ge(s_og, it * NB + b + 1)
                        xt = x[:, bass.ds(it * TB + b * TPB, TB)]
                        nc.gpsimd.tensor_tensor(xt, xt, og[:], ALU.add).then_inc(s_x, 1)

            @block.scalar
            def _(act):
                with act.Fori(0, NBLK) as it:
                    nc.scalar.preload_act_table_set(LN_SET)
                    norm.inverse_deviation(act, it)
                    norm.affine(act, it, lambda b, k: ps[:, b, k])
                    for b in range(NB):
                        act.wait_ge(s_scorecp, it * NB + b + 1)
                        if b:
                            act.wait_ge(s_sig, it * NB + b)
                        nc.scalar.activation(es[:], score[:], ACT.Exp, scale=-1.0).then_inc(s_es, 1)
                    for s in range(UE):
                        for f in range(KF):
                            n = it * UF + s * KF + f
                            act.wait_ge(s_pair, n + 1)
                            if s * KF + f >= 2:
                                act.wait_ge(s_hid, n - 1)
                            nc.scalar.activation(act_f[:, f % 2], ps[:, f % 2, 0], ACT.Silu).then_inc(s_silu, 1)

            @block.vector
            def _(dve):
                with dve.Fori(0, NBLK) as it:
                    norm.normalise(dve, it)
                    for b in range(NB):
                        u = it * NB + b + 1
                        dve.wait_ge(s_score, u)
                        if b:
                            dve.wait_ge(s_gate, u - 1)
                            dve.wait_ge(s_es, u - 1)
                        nc.vector.tensor_copy(score[:], psg[:, b, 0:TB * EXP].rearrange("p (t e) -> p t e", e=EXP)
                                              ).then_inc(s_scorecp, 1)
                        dve.wait_ge(s_scorecp, u)
                        nc.vector.memset(norm.settle[:], 0.0)
                        for t in range(TB):
                            i = nc.vector.max(top[:, t], score[:, t])
                        i.then_inc(s_top, 1)
                        dve.wait_ge(s_top, u)
                        nc.vector.memset(norm.settle[:], 0.0)
                        for t in range(TB):
                            i = nc.vector.max_index(topi[:, t], top[:, t], score[:, t])
                        i.then_inc(s_topi, 1)
                        dve.wait_ge(s_topi, u)
                        nc.vector.tensor_copy(topf[:], topi[:]).then_inc(s_topf, 1)
                        dve.wait_ge(s_topf, u)
                        for t in range(TB):
                            i = nc.vector.tensor_scalar(chosen[:, t], number[:], topf[:, t, 0:1], None, ALU.is_equal)
                        i.then_inc(s_pick0, 1)
                        dve.wait_ge(s_pick0, u)
                        for t in range(TB):
                            i = nc.vector.scalar_tensor_tensor(out=chosen[:, t], in0=number[:], scalar=topf[:, t, 1:2],
                                                               in1=chosen[:, t], op0=ALU.is_equal, op1=ALU.add)
                        i.then_inc(s_chosen, 1)
                        dve.wait_ge(s_es, u)
                        nc.vector.tensor_scalar(es[:], es[:], 1.0, None, ALU.add).then_inc(s_es1, 1)
                        dve.wait_ge(s_es1, u)
                        nc.vector.reciprocal(es[:], es[:]).then_inc(s_sig, 1)
                        dve.wait_ge(s_sig, u)
                        dve.wait_ge(s_chosen, u)
                        nc.vector.tensor_tensor(gate[:, b], chosen[:], es[:], ALU.mult).then_inc(s_gate, 1)
                    for b in range(NB):
                        dve.wait_ge(s_gateTp, it * NB + b + 1)
                        nc.vector.tensor_copy(gateT[:, b], psg[0:EXP, b]).then_inc(s_gateT, 1)

                    def route(s):
                        b, e = s // (EXP + 1), s % (EXP + 1)
                        if e == EXP:
                            return
                        n = it * NB * EXP + b * EXP + e
                        dve.wait_ge(s_gbc, n + 1)
                        if s >= 2:
                            dve.wait_ge(s_pair, it * UF + (s - 1) * KF)
                        nc.vector.tensor_tensor(routed[:, e % 2], hT[:, b],
                                                psg[:, e % 2:e % 2 + 1].broadcast_to([P, KD, BLK]),
                                                ALU.mult).then_inc(s_routed, 1)

                    route(0)
                    for s in range(UE):
                        if s + 1 < UE:
                            route(s + 1)
                        for f in range(KF):
                            n = it * UF + s * KF + f
                            dve.wait_ge(s_silu, n + 1)
                            if s >= 2 and f == 0:
                                dve.wait_ge(s_out, it * UE + s - 1)
                            nc.vector.tensor_tensor(hid[:, s % 2, f], ps[:, f % 2, 1], act_f[:, f % 2],
                                                    ALU.mult).then_inc(s_hid, 1)
                        if s % (EXP + 1) == EXP:
                            b = s // (EXP + 1)
                            dve.wait_ge(s_out, it * UE + s + 1)
                            if b:
                                dve.wait_ge(s_x, it * NB + b)
                            nc.vector.tensor_tensor(og[:], pso[:], keep["gates"][:, 0, 1, b:b + 1].broadcast_to([P, TB, D]),
                                                    ALU.mult).then_inc(s_og, 1)
                    dve.wait_ge(s_x, it * NB + NB)

            @block.tensor
            def _(pe):
                pe.wait_ge(s_w, 16 * (2 + 3 * EXP + 3))
                with pe.Fori(0, NBLK) as it:
                    norm.transpose(pe, it, lambda b, k: ps[:, b, k])
                    for b in range(NB):
                        pe.wait_ge(norm.s_hT, it * NB + b + 1)
                        for t in range(TB):
                            for k in range(KD):
                                i = nc.tensor.matmul(psg[:, b, t * EXP:(t + 1) * EXP], hT[:, b, k, t * P:(t + 1) * P],
                                                     router[:, k], start=(k == 0), stop=(k == KD - 1))
                        i.then_inc(s_score, 1)
                    for b in range(NB):
                        pe.wait_ge(s_gate, it * NB + b + 1)
                        for t in range(TB):
                            i = nc.tensor.transpose(psg[0:EXP, b, t * P:(t + 1) * P], gate[:, b, t], ident[:])
                        i.then_inc(s_gateTp, 1)

                    def spread(s):
                        b, e = s // (EXP + 1), s % (EXP + 1)
                        if e == EXP:
                            return
                        n = it * NB * EXP + b * EXP + e
                        if s == 0 or s == 1:
                            pe.wait_ge(s_gateT, it * NB + NB)
                        if b * EXP + e >= 2:
                            pe.wait_ge(s_routed, n - 1)
                        nc.tensor.matmul(psg[:, e % 2], ident[0:EXP, e:e + 1].broadcast_to([EXP, P]), gateT[:, b], start=True, stop=True).then_inc(s_gbc, 1)

                    def up(s, f):
                        b, e = s // (EXP + 1), s % (EXP + 1)
                        n = it * UF + s * KF + f
                        if f == 0 and e < EXP:
                            pe.wait_ge(s_routed, it * NB * EXP + b * EXP + e + 1)
                        if s * KF + f >= 2:
                            pe.wait_ge(s_hid, n - 1)
                        for j, wt in enumerate((w_in, w_sw)):
                            for k in range(KD):
                                src = routed[:, e % 2, k] if e < EXP else hT[:, b, k]
                                i = nc.tensor.matmul(ps[:, f % 2, j], wt[:, e, k, f * P:(f + 1) * P], src,
                                                     start=(k == 0), stop=(k == KD - 1))
                        i.then_inc(s_pair, 1)

                    def down(s):
                        b, e = s // (EXP + 1), s % (EXP + 1)
                        pe.wait_ge(s_hid, it * UF + (s + 1) * KF)
                        if e == 0 and b:
                            pe.wait_ge(s_og, it * NB + b)
                        for f in range(KF):
                            for t in range(TB):
                                i = nc.tensor.matmul(pso[:, t], hid[:, s % 2, f, t * P:(t + 1) * P], w_out[:, e, f],
                                                     start=(e == 0 and f == 0 and t % 2 == 0),
                                                     stop=(e == EXP and f == KF - 1 and t % 2 == 1),
                                                     skip_group_check=True)
                        i.then_inc(s_out, 1)

                    spread(0)
                    for s in range(UE):
                        if s + 1 < UE:
                            spread(s + 1)
                        up(s, 0)
                        up(s, 1)
                        if s >= 1:
                            down(s - 1)
                        up(s, 2)
                        up(s, 3)
                    down(UE - 1)
                    pe.wait_ge(s_og, it * NB + NB)
        m.clear()


def windowed_attention(nc, a, keep):
    x, modf, ident = keep["x"], keep["modf"], keep["ident"]
    with ExitStack() as outer:
        mo = Pool(nc, outer, "att")
        qT = mo.sb("qT", [P, KD, NT * P])
        kT = mo.sb("kT", [P, KD, (NT + 2) * P])
        v = mo.sb("v", [P, NT + 2, AKV * AHD])

        with ExitStack() as ctx:
            m = Pool(nc, ctx, "qkv")
            norm = BlockNorm(m, keep, lambda b, t, it: [x[:, bass.ds(it * TB + b * TPB + t, 1)]],
                             lambda b, k: modf[:, 1, SCALE_A, NB * k + b:NB * k + b + 1],
                             lambda b, k: modf[:, 1, SHIFT_A, NB * k + b:NB * k + b + 1])
            hT = norm.hT
            wq = m.sb("wq", [P, KD, D])
            wk = m.sb("wk", [P, KD, D])
            wv = m.sb("wv", [P, KD, AKV * AHD])
            ps = m.ps("ps", [P, 2 * KD, BLK])
            psv = m.ps("psv", [P, NB, BLK])
            s_w, s_q, s_k, s_v, s_qc, s_kc, s_vc, s_pad = (
                m.sem(n) for n in ("w_in", "q", "k", "v", "qcp", "kcp", "vcp", "pad"))
            with nc.Block() as block:
                @block.sync
                def _(sp):
                    for dst, name in ((wq, "att_wq"), (wk, "att_wk"), (wv, "att_wv")):
                        sp.dma_start(dst[:], a[name].rearrange("(k p) n -> p k n", p=P)).then_inc(s_w, 16)

                @block.gpsimd
                def _(pool):
                    for t in (0, NT + 1):
                        nc.gpsimd.memset(kT[:, :, t * P:(t + 1) * P], 0.0).then_inc(s_pad, 1)
                        nc.gpsimd.memset(v[:, t], 0.0).then_inc(s_pad, 1)
                    pool.wait_ge(s_pad, 4)

                @block.scalar
                def _(act):
                    with act.Fori(0, NBLK) as it:
                        nc.scalar.preload_act_table_set(LN_SET)
                        norm.inverse_deviation(act, it)
                        norm.affine(act, it, lambda b, k: ps[:, 2 * b + k])
                        for b in range(NB):
                            act.wait_ge(s_q, it * NB + b + 1)
                            nc.scalar.copy(qT[:, :, bass.ds(it * BLK + b * SEQ, BLK)], ps[:, 0:KD]).then_inc(s_qc, 1)

                @block.vector
                def _(dve):
                    with dve.Fori(0, NBLK) as it:
                        norm.normalise(dve, it)
                        for b in range(NB):
                            dve.wait_ge(s_k, it * NB + b + 1)
                            nc.vector.tensor_copy(kT[:, :, bass.ds(it * BLK + b * SEQ + P, BLK)],
                                                  ps[:, KD:2 * KD]).then_inc(s_kc, 1)
                            dve.wait_ge(s_v, it * NB + b + 1)
                            nc.vector.tensor_copy(v[:, bass.ds(it * TB + b * TPB + 1, TB)],
                                                  psv[:, b, 0:TB * AKV * AHD].rearrange("p (t d) -> p t d", t=TB)
                                                  ).then_inc(s_vc, 1)

                @block.tensor
                def _(pe):
                    pe.wait_ge(s_w, 48)
                    with pe.Fori(0, NBLK) as it:
                        norm.transpose(pe, it, lambda b, k: ps[:, 2 * b + k])
                        pe.wait_ge(norm.s_hT, it * NB + NB)
                        for b in range(NB):
                            for w, copied, done, at in ((wq, s_qc, s_q, 0), (wk, s_kc, s_k, KD)):
                                if b:
                                    pe.wait_ge(copied, it * NB + b)
                                for c in range(KD):
                                    for k in range(KD):
                                        i = nc.tensor.matmul(ps[:, at + c], w[:, k, c * P:(c + 1) * P], hT[:, b, k],
                                                             start=(k == 0), stop=(k == KD - 1))
                                i.then_inc(done, 1)
                            for t in range(TB):
                                for k in range(KD):
                                    i = nc.tensor.matmul(psv[:, b, t * AKV * AHD:(t + 1) * AKV * AHD],
                                                         hT[:, b, k, t * P:(t + 1) * P], wv[:, k],
                                                         start=(k == 0), stop=(k == KD - 1))
                            i.then_inc(s_v, 1)
                        pe.wait_ge(s_qc, it * NB + NB)
                        pe.wait_ge(s_kc, it * NB + NB)
                        pe.wait_ge(s_vc, it * NB + NB)

        m = Pool(nc, outer, "win")
        wo = m.sb("wo", [P, KD, D])
        mask = m.sb("mask", [P, TPB, AW], BF16)
        identb = m.sb("identb", [P, P], BF16)
        headmask = m.sb("headmask", [P, HPC])
        qm = m.sb("qm", [P, NB, AH, P])
        top = m.sb("top", [P, 3, HPR])
        nb = m.sb("nb", [P, 3, HPR])
        rs = m.sb("rs", [P, NB, AH])
        ri = m.sb("ri", [P, NB, AH])
        pr = m.sb("pr", [P, 3, HPR, AW])
        pT = m.sb("pT", [P, 3, HPR, AW])
        o = m.sb("o", [P, NB, D])
        oT = m.sb("oT", [P, NB, D])
        og = m.sb("og", [P, NB, D])
        psw = m.ps("psw", [P, 3, HPR, 512])
        pso = m.ps("pso", [P, NB, 512])
        (s_w, s_qm, s_s, s_top, s_nb, s_e, s_t, s_pT, s_pv, s_ri, s_o, s_oTp, s_oT, s_out, s_og, s_x) = (m.sem(n) for n in (
            "w_in", "qm", "scores", "top", "nb", "exp", "tp", "pT", "pv", "ri", "o", "oTp", "oT", "out", "og", "xadd"))
        s_m = m.sem("mask_in")
        RU = AH // HPR
        RI = NB * RU
        SC = float(AHD) ** -0.5
        HEAD = 1

        with nc.Block() as block:
            @block.sync
            def _(sp):
                sp.dma_start(wo[:], a["att_wo"].rearrange("(k p) n -> p k n", p=P)).then_inc(s_w, 16)
                sp.dma_start(headmask[:], a["headmask"]).then_inc(s_w, 16)

            @block.gpsimd
            def _(pool):
                pool.dma_start(mask[:], a["win_mask"]).then_inc(s_m, 16)
                pool.dma_start(identb[:], a["ident"]).then_inc(s_m, 16)
                pool.wait_ge(s_w, 32)
                with pool.Fori(0, TPB) as it:
                    for b in range(NB):
                        for c in range(KD):
                            q = qT[:, c:c + 1, bass.ds(it * P + b * SEQ, P)]
                            i = nc.gpsimd.tensor_tensor(qm[:, b, c * HPC:(c + 1) * HPC], q.broadcast_to([P, HPC, P]),
                                                        headmask[:].unsqueeze(2).broadcast_to([P, HPC, P]), ALU.mult)
                        i.then_inc(s_qm, 1)
                    pool.wait_ge(s_s, it * RI + RI)

            @block.scalar
            def _(act):
                nc.scalar.preload_act_table_set(LN_SET)
                with act.Fori(0, TPB) as it:
                    for r in range(RI):
                        n, w, b = it * RI + r, r % 3, r // RU
                        act.wait_ge(s_nb, n + 1)
                        for h in range(HPR):
                            hh = r % RU * HPR + h
                            i = nc.scalar.activation(pr[:, w, h], psw[:, w, h, 0:AW], ACT.Exp, scale=SC,
                                                     bias=nb[:, w, h:h + 1], accum_out=rs[:, b, hh:hh + 1])
                        i.then_inc(s_e, 1)
                    for b in range(NB):
                        act.wait_ge(s_oTp, it * NB + b + 1)
                        nc.scalar.copy(oT[:, b], pso[:, b, 0:D]).then_inc(s_oT, 1)

            @block.vector
            def _(dve):
                dve.sem_inc(s_og, HEAD)
                with dve.Fori(0, TPB) as it:
                    def maxima(r):
                        n, w, b = it * RI + r, r % 3, r // RU
                        dve.wait_ge(s_s, n + 1)
                        nc.vector.tensor_reduce(top[:, w], psw[:, w, :, 0:AW], AX_X, ALU.max).then_inc(s_top, 1)
                        dve.wait_ge(s_top, n + 1)
                        nc.vector.tensor_scalar(nb[:, w], top[:, w], -SC, None, ALU.mult).then_inc(s_nb, 1)

                    def move(r):
                        n, w, b = it * RI + r, r % 3, r // RU
                        dve.wait_ge(s_t, n + 1)
                        if r >= 3:
                            dve.wait_ge(s_pv, n - 2)
                        nc.vector.tensor_copy(pT[:, w], psw[:, w, :, 0:AW]).then_inc(s_pT, 1)

                    def normalise(b):
                        u = it * NB + b
                        nc.vector.reciprocal(ri[:, b], rs[:, b]).then_inc(s_ri, 1)
                        dve.wait_ge(s_ri, u + 1)
                        dve.wait_ge(s_pv, it * RI + (b + 1) * RU)
                        nc.vector.tensor_tensor(o[:, b].rearrange("p (h d) -> p h d", h=AH),
                                                pso[:, b, 0:D].rearrange("p (h d) -> p h d", h=AH),
                                                ri[:, b].unsqueeze(2).broadcast_to([P, AH, AHD]), ALU.mult).then_inc(s_o, 1)

                    for r in range(RI + 1):
                        if r < RI:
                            maxima(r)
                        if r >= 1:
                            move(r - 1)
                        if r == RU + 2:
                            normalise(0)
                    normalise(1)
                    for b in range(NB):
                        u = it * NB + b
                        dve.wait_ge(s_out, u + 1)
                        nc.vector.tensor_tensor(og[:, b], pso[:, b, D:2 * D], keep["gates"][:, 1, 0, b],
                                                ALU.mult).then_inc(s_og, 1)
                    for b in range(NB):
                        dve.wait_ge(s_og, it * NB + b + 1 + HEAD)
                        xt = x[:, bass.ds(it + b * TPB, 1)]
                        nc.vector.tensor_tensor(xt, xt, og[:, b:b + 1], ALU.add).then_inc(s_x, 1)

            @block.tensor
            def _(pe):
                pe.wait_ge(s_w, 32)
                pe.wait_ge(s_m, 32)
                with pe.Fori(0, TPB) as it:
                    def scores(r):
                        n, w, b = it * RI + r, r % 3, r // RU
                        if r % RU == 0:
                            pe.wait_ge(s_qm, it * NB + b + 1)
                        if r >= 3:
                            pe.wait_ge(s_pT, n - 2)
                        for h in range(HPR):
                            hh = r % RU * HPR + h
                            c = hh // HPC
                            nc.tensor.matmul(psw[:, w, h, 0:AW], identb[:], mask[:, bass.ds(it, 1)], start=True, stop=False)
                            i = nc.tensor.matmul(psw[:, w, h, 0:AW], qm[:, b, hh], kT[:, c, bass.ds(it * P + b * SEQ, AW)],
                                                 start=False, stop=True)
                        i.then_inc(s_s, 1)

                    def turn(r):
                        n, w, b = it * RI + r, r % 3, r // RU
                        pe.wait_ge(s_e, n + 1)
                        for h in range(HPR):
                            for kb in range(3):
                                i = nc.tensor.transpose(psw[:, w, h, kb * P:(kb + 1) * P], pr[:, w, h, kb * P:(kb + 1) * P],
                                                        ident[:])
                        i.then_inc(s_t, 1)

                    def values(r):
                        n, w, b = it * RI + r, r % 3, r // RU
                        pe.wait_ge(s_pT, n + 1)
                        if r % RU == 0:
                            pe.wait_ge(s_og, it * NB + HEAD)
                        for h in range(HPR):
                            hh = r % RU * HPR + h
                            kv = hh // AG
                            for kb in range(3):
                                i = nc.tensor.matmul(pso[:, b, hh * AHD:(hh + 1) * AHD], pT[:, w, h, kb * P:(kb + 1) * P],
                                                     v[:, bass.ds(it + b * TPB + kb, 1), kv * AHD:(kv + 1) * AHD],
                                                     start=(hh == 0 and kb == 0), stop=(hh == AH - 1 and kb == 2),
                                                     skip_group_check=True)
                        i.then_inc(s_pv, 1)

                    def turn_out(b):
                        pe.wait_ge(s_o, it * NB + b + 1)
                        for c in range(KD):
                            i = nc.tensor.transpose(pso[:, b, c * P:(c + 1) * P], o[:, b, c * P:(c + 1) * P], ident[:])
                        i.then_inc(s_oTp, 1)

                    def project_out(b):
                        pe.wait_ge(s_oT, it * NB + b + 1)
                        for c in range(KD):
                            i = nc.tensor.matmul(pso[:, b, D:2 * D], oT[:, b, c * P:(c + 1) * P], wo[:, c],
                                                 start=(c == 0), stop=(c == KD - 1))
                        i.then_inc(s_out, 1)

                    for r in range(RI + 2):
                        if r < RI:
                            scores(r)
                        if 1 <= r <= RI:
                            turn(r - 1)
                        if r >= 2:
                            values(r - 2)
                    for b in range(NB):
                        turn_out(b)
                    for b in range(NB):
                        project_out(b)


def enter_local_stack(nc, a, keep, y, xs_a, spill):
    x = keep["x"]
    with ExitStack() as ctx:
        m = Pool(nc, ctx, "ent")
        norm = BlockNorm(m, keep, lambda b, t, it: [x[:, bass.ds(it * TB + b * TPB + t, 1)]], None, None)
        s_m, s_y, s_zero, s_xs, s_sp = m.sem("mult"), m.sem("y"), m.sem("zero"), m.sem("shifted"), m.sem("spilled")
        with nc.Block() as block:
            @block.sync
            def _(sp):
                sp.dma_start(spill.rearrange("(t p) d -> p t d", p=P), x[:]).then_inc(s_sp, 16)
                sp.wait_ge(s_zero, 1)
                with sp.Fori(0, NBLK) as it:
                    for b in range(NB):
                        sp.wait_ge(s_y, it * NB + b + 1)
                        shift_tokens(sp, y, xs_a, b, it * TB, TB, s_xs)
                sp.wait_ge(s_xs, NBLK * NB * 32)

            @block.scalar
            def _(act):
                nc.scalar.preload_act_table_set(LN_SET)
                with act.Fori(0, NBLK) as it:
                    norm.inverse_deviation(act, it)

            @block.vector
            def _(dve):
                nc.vector.memset(xs_a[0:1, :, 0], 0.0).then_inc(s_zero, 1)
                with dve.Fori(0, NBLK) as it:
                    norm.normalise(dve, it)
                    dve.wait_ge(s_y, it * NB + NB)

            @block.gpsimd
            def _(pool):
                pool.wait_ge(s_sp, 16)
                with pool.Fori(0, NBLK) as it:
                    for b in range(NB):
                        pool.wait_ge(norm.s_xn, it * NB + b + 1)
                        xn = norm.xn[:, b]
                        nc.gpsimd.tensor_tensor(xn, xn, keep["scale_row"][:, b:b + 1].broadcast_to([P, TB, D]),
                                                ALU.mult).then_inc(s_m, 1)
                        pool.wait_ge(s_m, it * NB + b + 1)
                        nc.gpsimd.tensor_tensor(y[:, bass.ds(it * TB + b * TPB, TB)], xn,
                                                keep["shift_row"][:, b:b + 1].broadcast_to([P, TB, D]),
                                                ALU.add).then_inc(s_y, 1)


def shift_tokens(eng, y, xs, b, tile, n, sem):
    src = y[:, bass.ds(tile + b * TPB, n), P:D]
    eng.dma_start(xs[1:P, b, bass.ds(tile, n)], src[0:P - 1]).then_inc(sem, 16)
    eng.dma_start(xs[0:1, b, bass.ds(tile + 1, n)], src[P - 1:P]).then_inc(sem, 16)


def local_attention(nc, a, keep, y, xs_a, xs_b, tabs, layer):
    ident = keep["ident"]
    cos, sin, mask, identb = tabs
    with ExitStack() as ctx:
        m = Pool(nc, ctx, "loc")
        w = m.sb("w", [P, KD, 3 * INNER])
        wo = m.sb("wo", [P, KI, D])
        scl = m.sb("scl", [P, 2, LHD])
        tc = m.sb("tc", [P, TPB, 2, LHD])
        ts = m.sb("ts", [P, TPB, 2, LHD])
        xst = m.sb("xst", [P, NB, D])
        hT = m.sb("hT", [P, NB, D])
        sq = m.sb("sq", [P, 2 * INNER])
        ss = m.sb("ss", [P, NB, 2 * LH])
        rn = m.sb("rn", [P, NB, 2 * LH])
        t1 = m.sb("t1", [P, NB, 2 * INNER])
        t2 = m.sb("t2", [P, NB, 2 * INNER])
        v = m.sb("v", [P, NB, 2, INNER])
        qT = m.sb("qT", [P, NB, KI, P])
        kT = m.sb("kT", [P, NB, KI, 2 * P])
        top = m.sb("top", [P, NB, 4])
        nb = m.sb("nb", [P, NB, 4])
        sc8 = m.sb("sc8", [P, NB, LH])
        rs = m.sb("rs", [P, NB, LH])
        ri = m.sb("ri", [P, NB, LH])
        pr = m.sb("pr", [P, NB, 4, 2 * P])
        pT = m.sb("pT", [P, NB, 8, P])
        o = m.sb("o", [P, NB, INNER])
        oT = m.sb("oT", [P, NB, INNER])
        psa = m.ps("psa", [P, 3, 512])
        psw = m.ps("psw", [P, NB, 2, 512])
        pso1 = m.ps("pso", [P, 512])
        pso = [pso1, psa[:, 2]]
        names = ("w_in tab zero stage hTp hT qkv sq vcp ss ssm lnss rn sc8 t1 t2 rope ksc vprev kprev qkTp qT kT scores top "
                 "nb exp tp pTa pTb pv ri o oTp oT out y shifted")
        (s_w, s_tab, s_zero, s_stage, s_hTp, s_hT, s_qkv, s_sq, s_vcp, s_ss, s_ssm, s_lnss, s_rn, s_sc8, s_t1, s_t2,
         s_rope, s_ksc, s_vprev, s_kprev, s_qkTp, s_qT, s_kT, s_s, s_top, s_nb, s_e, s_tp, s_pTa, s_pTb, s_pv, s_ri,
         s_o, s_oTp, s_oT, s_out, s_y, s_xs) = (m.sem(n) for n in names.split())
        L = layer

        def heads(t):
            return t.rearrange("p (j h d) -> p j h d", j=2, h=LH)

        with nc.Block() as block:
            @block.sync
            def _(sp):
                sp.dma_start(w[:], a["wqkv"][bass.ds(L, 1)].rearrange("a (k p) n -> p (a k) n", p=P)).then_inc(s_w, 16)
                sp.dma_start(wo[:], a["loc_wo"][bass.ds(L, 1)].rearrange("a (k p) n -> p (a k) n", p=P)).then_inc(s_w, 16)
                sp.dma_start(scl[:], a["qk_scale"][bass.ds(L, 1)].broadcast_to([P, 2, LHD])).then_inc(s_w, 16)
                with sp.Fori(0, TPB) as j:
                    it = L * TPB + j
                    for b in range(NB):
                        sp.wait_ge(s_y, it * NB + b + 1)
                        shift_tokens(sp, y, xs_b, b, j, 1, s_xs)

            @block.gpsimd
            def _(pool):
                pool.wait_ge(s_w, (L + 1) * 48)
                nc.gpsimd.tensor_tensor(tc[:], cos[:], scl[:].unsqueeze(1).broadcast_to([P, TPB, 2, LHD]),
                                        ALU.mult).then_inc(s_tab, 1)
                for half in range(2):
                    d, s = slice(half * 32, half * 32 + 32), slice(32 - half * 32, 64 - half * 32)
                    nc.gpsimd.tensor_tensor(ts[:, :, :, d], sin[:, :, :, d],
                                            scl[:, :, s].unsqueeze(1).broadcast_to([P, TPB, 2, 32]),
                                            ALU.mult).then_inc(s_tab, 1)
                for t in (v[:, :, 1], kT[:, :, :, P:2 * P]):
                    nc.gpsimd.memset(t, 0.0).then_inc(s_zero, 1)
                with pool.Fori(0, TPB) as j:
                    it = L * TPB + j
                    pool.wait_ge(s_zero, 2 * L + 2)
                    for b in range(NB):
                        u = it * NB + b
                        nc.gpsimd.tensor_copy(xst[:, b, 0:P], y[:, bass.ds(j + b * TPB, 1), 0:P])
                        nc.gpsimd.tensor_copy(xst[:, b, P:D], xs_a[:, b, bass.ds(j, 1)]).then_inc(s_stage, 1)
                    for b in range(NB):
                        u = it * NB + b
                        nc.gpsimd.tensor_copy(v[:, b, 0], v[:, b, 1]).then_inc(s_vprev, 1)
                        nc.gpsimd.tensor_copy(kT[:, b, :, 0:P], kT[:, b, :, P:2 * P]).then_inc(s_kprev, 1)
                    for b in range(NB):
                        u = it * NB + b
                        pool.wait_ge(s_t2, u + 1)
                        nc.gpsimd.tensor_tensor(t1[:, b], t1[:, b], t2[:, b], ALU.add).then_inc(s_rope, 1)
                        pool.wait_ge(s_rope, u + 1)
                        pool.wait_ge(s_rn, u + 1)
                        kk = t1[:, b, INNER:].rearrange("p (h d) -> p h d", h=LH)
                        nc.gpsimd.tensor_tensor(kk, kk, rn[:, b, LH:].unsqueeze(2).broadcast_to([P, LH, LHD]),
                                                ALU.mult).then_inc(s_ksc, 1)
                    pool.wait_ge(s_pv, it * NB * 2 + NB * 2)
                pool.wait_ge(s_xs, (L + 1) * (TPB * NB * 32))

            @block.scalar
            def _(act):
                nc.scalar.preload_act_table_set(LN_SET)
                with act.Fori(0, TPB) as j:
                    it = L * TPB + j
                    for b in range(NB):
                        u = it * NB + b
                        act.wait_ge(s_hTp, u + 1)
                        nc.scalar.copy(hT[:, b], psw[:, b, 0, 0:D]).then_inc(s_hT, 1)
                    for b in range(NB):
                        u = it * NB + b
                        act.wait_ge(s_qkv, u + 1)
                        if b:
                            act.wait_ge(s_ss, u)
                        nc.scalar.activation(sq[:], psa[:, 0:2].rearrange("p a n -> p (a n)"), ACT.Square).then_inc(s_sq, 1)
                        act.wait_ge(s_vprev, u + 1)
                        nc.scalar.copy(v[:, b, 1], psa[:, 2]).then_inc(s_vcp, 1)
                        act.wait_ge(s_ssm, u + 1)
                        nc.scalar.activation(rn[:, b], ss[:, b], ACT.Ln, scale=SS_SCALE).then_inc(s_lnss, 1)
                        act.wait_ge(s_lnss, u + 1)
                        nc.scalar.activation(rn[:, b], rn[:, b], ACT.Exp, scale=-0.5,
                                             bias=keep["ss_log"][:, 0:1]).then_inc(s_rn, 1)
                    for b in range(NB):
                        u = it * NB + b
                        act.wait_ge(s_qkTp, u + 1)
                        nc.scalar.copy(qT[:, b].rearrange("p k n -> p (k n)"), psw[:, b, 0]).then_inc(s_qT, 1)

                    def exps(b, hf):
                        n = (it * NB * 2) + hf * NB + b
                        act.wait_ge(s_nb, n + 1)
                        for h in range(4):
                            hh = hf * 4 + h % 2 * 2 + h // 2
                            i = nc.scalar.activation(pr[:, b, h], psw[:, b, h // 2, h % 2 * 256:h % 2 * 256 + 256], ACT.Exp,
                                                     scale=sc8[:, b, hh:hh + 1], bias=nb[:, b, h:h + 1],
                                                     accum_out=rs[:, b, hh:hh + 1])
                        i.then_inc(s_e, 1)

                    def move(b, hf):
                        n = (it * NB * 2) + hf * NB + b
                        act.wait_ge(s_tp, n + 1)
                        nc.scalar.copy(pT[:, b, 4:8].rearrange("p k n -> p (k n)"), psw[:, b, 1]).then_inc(s_pTb, 1)

                    for hf in range(2):
                        for b in range(NB):
                            exps(b, hf)
                        for b in range(NB):
                            move(b, hf)
                    for b in range(NB):
                        u = it * NB + b
                        act.wait_ge(s_oTp, u + 1)
                        nc.scalar.copy(oT[:, b], psw[:, b, 0]).then_inc(s_oT, 1)

            @block.vector
            def _(dve):
                nc.vector.memset(xs_b[0:1, :, 0], 0.0)
                with dve.Fori(0, TPB) as j:
                    it = L * TPB + j
                    dve.wait_ge(s_tab, (L + 1) * 3)
                    for b in range(NB):
                        u = it * NB + b
                        dve.wait_ge(s_sq, u + 1)
                        qk = heads(psa[:, 0:2].rearrange("p a n -> p (a n)"))
                        for q in range(2):
                            cosq = tc[:, bass.ds(j, 1), q].broadcast_to([P, LH, LHD])
                            i = nc.vector.tensor_tensor(heads(t1[:, b])[:, q], qk[:, q], cosq, ALU.mult)
                        i.then_inc(s_t1, 1)
                        for q in range(2):
                            for half in range(2):
                                d, s = slice(half * 32, half * 32 + 32), slice(32 - half * 32, 64 - half * 32)
                                i = nc.vector.tensor_tensor(heads(t2[:, b])[:, q, :, d], qk[:, q, :, s],
                                                            ts[:, bass.ds(j, 1), q, d].broadcast_to([P, LH, 32]), ALU.mult)
                        i.then_inc(s_t2, 1)
                        nc.vector.tensor_reduce(ss[:, b], sq[:].rearrange("p (h d) -> p h d", d=LHD), AX_X,
                                                ALU.add).then_inc(s_ss, 1)
                        dve.wait_ge(s_ss, u + 1)
                        nc.vector.tensor_scalar(ss[:, b], ss[:, b], 1e-24, None, ALU.max).then_inc(s_ssm, 1)
                        dve.wait_ge(s_rn, u + 1)
                        nc.vector.tensor_scalar(sc8[:, b], rn[:, b, 0:LH], QK_SCALE, None, ALU.mult).then_inc(s_sc8, 1)
                    for b in range(NB):
                        u = it * NB + b
                        dve.wait_ge(s_qkTp, u + 1)
                        dve.wait_ge(s_kprev, u + 1)
                        nc.vector.tensor_copy(kT[:, b, :, P:2 * P], psw[:, b, 1].rearrange("p (k n) -> p k n", k=KI)
                                              ).then_inc(s_kT, 1)

                    def maxima(b, hf):
                        n = (it * NB * 2) + hf * NB + b
                        dve.wait_ge(s_s, n + 1)
                        nc.vector.tensor_reduce(top[:, b], psw[:, b].rearrange("p a (h n) -> p (a h) n", h=2), AX_X,
                                                ALU.max).then_inc(s_top, 1)
                        dve.wait_ge(s_top, n + 1)
                        dve.wait_ge(s_sc8, it * NB + b + 1)
                        nc.vector.scalar_tensor_tensor(
                            out=nb[:, b].rearrange("p (r s) -> p r s", r=2),
                            in0=top[:, b].rearrange("p (r s) -> p r s", r=2), scalar=-1.0,
                            in1=sc8[:, b, hf * 4:hf * 4 + 4].rearrange("p (s r) -> p r s", r=2), op0=ALU.mult,
                            op1=ALU.mult).then_inc(s_nb, 1)

                    def move(b, hf):
                        n = (it * NB * 2) + hf * NB + b
                        dve.wait_ge(s_tp, n + 1)
                        nc.vector.tensor_copy(pT[:, b, 0:4].rearrange("p k n -> p (k n)"), psw[:, b, 0]).then_inc(s_pTa, 1)

                    for hf in range(2):
                        for b in range(NB):
                            maxima(b, hf)
                        for b in range(NB):
                            move(b, hf)
                    for b in range(NB):
                        u = it * NB + b
                        nc.vector.reciprocal(ri[:, b], rs[:, b]).then_inc(s_ri, 1)
                        dve.wait_ge(s_ri, u + 1)
                        dve.wait_ge(s_pv, it * NB * 2 + NB + b + 1)
                        nc.vector.tensor_tensor(o[:, b].rearrange("p (h d) -> p h d", h=LH),
                                                pso[b].rearrange("p (h d) -> p h d", h=LH) if b else
                                                pso1[:].rearrange("p (h d) -> p h d", h=LH),
                                                ri[:, b].unsqueeze(2).broadcast_to([P, LH, LHD]), ALU.mult).then_inc(s_o, 1)
                    for b in range(NB):
                        u = it * NB + b
                        dve.wait_ge(s_out, u + 1)
                        yt = y[:, bass.ds(j + b * TPB, 1)]
                        nc.vector.tensor_tensor(yt, psw[:, b, 1:2, 0:D], yt, ALU.add).then_inc(s_y, 1)

            @block.tensor
            def _(pe):
                with pe.Fori(0, TPB) as j:
                    it = L * TPB + j
                    pe.wait_ge(s_w, (L + 1) * 48)
                    for b in range(NB):
                        u = it * NB + b
                        pe.wait_ge(s_stage, u + 1)
                        for k in range(KD):
                            i = nc.tensor.transpose(psw[:, b, 0, k * P:(k + 1) * P], xst[:, b, k * P:(k + 1) * P], ident[:])
                        i.then_inc(s_hTp, 1)
                    for b in range(NB):
                        u = it * NB + b
                        pe.wait_ge(s_hT, u + 1)
                        if b:
                            pe.wait_ge(s_t2, u)
                            pe.wait_ge(s_sq, u)
                            pe.wait_ge(s_vcp, u)
                        for c in range(3):
                            for k in range(KD):
                                i = nc.tensor.matmul(psa[:, c], hT[:, b, k * P:(k + 1) * P], w[:, k, c * 512:(c + 1) * 512],
                                                     start=(k == 0), stop=(k == KD - 1))
                        i.then_inc(s_qkv, 1)
                    for b in range(NB):
                        u = it * NB + b
                        pe.wait_ge(s_ksc, u + 1)
                        for q in range(2):
                            for c in range(KI):
                                i = nc.tensor.transpose(psw[:, b, q, c * P:(c + 1) * P],
                                                        t1[:, b, q * INNER + c * P:q * INNER + (c + 1) * P], ident[:])
                        i.then_inc(s_qkTp, 1)

                    def scores(b, hf):
                        n = (it * NB * 2) + hf * NB + b
                        if hf == 0:
                            pe.wait_ge(s_qT, it * NB + b + 1)
                            pe.wait_ge(s_kT, it * NB + b + 1)
                        else:
                            pe.wait_ge(s_pTa, n - 1)
                            pe.wait_ge(s_pTb, n - 1)
                        for i2 in range(2):
                            out = psw[:, b, i2].rearrange("p (h w n) -> p h w n", h=2, w=2)
                            nc.tensor.matmul(out[:, :, 0], identb[:], mask[:, bass.ds(j, 1), 0:P].broadcast_to([P, 2, P]),
                                             start=True, stop=False, skip_group_check=True)
                            nc.tensor.matmul(out[:, :, 1], identb[:], mask[:, 0:1, P:2 * P].broadcast_to([P, 2, P]),
                                             start=False, stop=False, skip_group_check=True)
                        for h in range(2):
                            for i2 in range(2):
                                hh, r = hf * 4 + h * 2 + i2, i2 * LHD
                                i = nc.tensor.matmul(psw[:, b, i2, h * 256:(h + 1) * 256], qT[r:r + LHD, b, hh // 2],
                                                     kT[r:r + LHD, b, hh // 2], start=False, stop=(h == 1),
                                                     skip_group_check=True)
                        i.then_inc(s_s, 1)

                    def turn(b, hf):
                        n = (it * NB * 2) + hf * NB + b
                        pe.wait_ge(s_e, n + 1)
                        for h in range(4):
                            for kb in range(2):
                                i = nc.tensor.transpose(psw[:, b, h // 2, (h % 2 * 2 + kb) * P:(h % 2 * 2 + kb + 1) * P],
                                                        pr[:, b, h, kb * P:(kb + 1) * P], ident[:])
                        i.then_inc(s_tp, 1)

                    def values(b, hf):
                        n = (it * NB * 2) + hf * NB + b
                        pe.wait_ge(s_pTa, n + 1)
                        pe.wait_ge(s_pTb, n + 1)
                        if b:
                            pe.wait_ge(s_vcp, it * NB + NB)
                        for h in range(4):
                            hh = hf * 4 + h % 2 * 2 + h // 2
                            for kb in range(2):
                                i = nc.tensor.matmul(pso[b][:, hh * LHD:(hh + 1) * LHD], pT[:, b, h * 2 + kb],
                                                     v[:, b, kb, hh * LHD:(hh + 1) * LHD], start=(hh == 0 and kb == 0),
                                                     stop=(hh == LH - 1 and kb == 1), skip_group_check=True)
                        i.then_inc(s_pv, 1)

                    scores(0, 0)
                    scores(1, 0)
                    for hf in range(2):
                        turn(0, hf)
                        turn(1, hf)
                        for b in range(NB):
                            values(b, hf)
                            if hf == 0:
                                scores(b, 1)
                    for b in range(NB):
                        u = it * NB + b
                        pe.wait_ge(s_o, u + 1)
                        for c in range(KI):
                            i = nc.tensor.transpose(psw[:, b, 0, c * P:(c + 1) * P], o[:, b, c * P:(c + 1) * P], ident[:])
                        i.then_inc(s_oTp, 1)
                    for b in range(NB):
                        u = it * NB + b
                        pe.wait_ge(s_oT, u + 1)
                        for c in range(KI):
                            i = nc.tensor.matmul(psw[:, b, 1, 0:D], oT[:, b, c * P:(c + 1) * P], wo[:, c],
                                                 start=(c == 0), stop=(c == KI - 1))
                        i.then_inc(s_out, 1)
                    pe.wait_ge(s_y, it * NB + NB)


def gated_mlp(nc, a, keep, y, xs_a, xs_b, layer):
    L = layer
    with ExitStack() as ctx:
        m = Pool(nc, ctx, "mlp")
        col = m.sb("col", [P, 2 * KD + 2 * KH])
        norm = BlockNorm(m, keep, lambda b, t, j: [y[:, bass.ds(j * TB + b * TPB + t, 1), 0:P],
                                                   xs_b[:, b, bass.ds(j * TB + t, 1)]],
                         lambda b, k: col[:, k:k + 1], lambda b, k: col[:, KD + k:KD + k + 1])
        hT = norm.hT
        w1 = m.sb("w1", [P, KD, 2 * HID])
        w2 = m.sb("w2", [P, KH, D])
        b2 = m.sb("b2", [P, 1, D])
        gl = m.sb("gl", [P, 2, BLK])
        hid = m.sb("hid", [P, 2, KH, BLK])
        ps = m.ps("ps", [P, 2, 2, BLK])
        pso = m.ps("pso", [P, TB, D])
        s_w, s_pair, s_gl, s_hid, s_out, s_yo, s_y, s_xs = (
            m.sem(n) for n in ("w_in", "pair", "gelu", "hid", "out", "yo", "y", "shifted"))
        UF = NB * KH

        with nc.Block() as block:
            @block.sync
            def _(sp):
                sp.dma_start(w1[:], a["w1"][bass.ds(L, 1)].rearrange("a (k p) n -> p (a k) n", p=P)).then_inc(s_w, 16)
                full = (KH - 1) * P
                sp.dma_start(w2[:, 0:KH - 1], a["w2"][bass.ds(L, 1), 0:full].rearrange("a (k p) n -> p (a k) n", p=P)
                             ).then_inc(s_w, 16)
                sp.dma_start(w2[0:HTAIL, KH - 1:KH], a["w2"][bass.ds(L, 1), full:HID].rearrange("a p n -> p a n")
                             ).then_inc(s_w, 16)
                sp.dma_start(b2[:], a["b2"][bass.ds(L, 1)].unsqueeze(0).broadcast_to([P, 1, D])).then_inc(s_w, 16)
                sp.dma_start(col[:], a["mlp_col"][bass.ds(L, 1)].rearrange("a p n -> p (a n)")).then_inc(s_w, 16)
                with sp.Fori(0, NBLK) as j:
                    it = L * NBLK + j
                    for b in range(NB):
                        sp.wait_ge(s_y, it * NB + b + 1)
                        shift_tokens(sp, y, xs_a, b, j * TB, TB, s_xs)

            @block.gpsimd
            def _(pool):
                with pool.Fori(0, NBLK) as j:
                    it = L * NBLK + j
                    pool.wait_ge(s_w, (L + 1) * 80)
                    for b in range(NB):
                        pool.wait_ge(s_yo, it * NB + b + 1)
                        yt = y[:, bass.ds(j * TB + b * TPB, TB)]
                        nc.gpsimd.tensor_tensor(yt, yt, b2[:].broadcast_to([P, TB, D]), ALU.add).then_inc(s_y, 1)
                pool.wait_ge(s_xs, (L + 1) * (NBLK * NB * 32))

            @block.scalar
            def _(act):
                with act.Fori(0, NBLK) as j:
                    it = L * NBLK + j
                    nc.scalar.preload_act_table_set(LN_SET)
                    act.wait_ge(s_w, (L + 1) * 80)
                    norm.inverse_deviation(act, it)
                    norm.affine(act, it, lambda b, k: ps[:, b, k])
                    for q in range(UF):
                        n, f = it * UF + q, q % KH
                        M = P if f < KH - 1 else HTAIL
                        act.wait_ge(s_pair, n + 1)
                        if q >= 2:
                            act.wait_ge(s_hid, n - 1)
                        c = 2 * KD + KH + f
                        nc.scalar.activation(gl[0:M, q % 2], ps[0:M, q % 2, 1], ACT.Gelu,
                                             bias=col[0:M, c:c + 1]).then_inc(s_gl, 1)

            @block.vector
            def _(dve):
                with dve.Fori(0, NBLK) as j:
                    it = L * NBLK + j
                    dve.wait_ge(s_w, (L + 1) * 80)
                    norm.normalise(dve, it, j)
                    for q in range(UF):
                        n, f, b = it * UF + q, q % KH, q // KH
                        M = P if f < KH - 1 else HTAIL
                        dve.wait_ge(s_gl, n + 1)
                        c = 2 * KD + f
                        nc.vector.scalar_tensor_tensor(out=hid[0:M, b, f], in0=ps[0:M, q % 2, 0], scalar=col[0:M, c:c + 1],
                                                       in1=gl[0:M, q % 2], op0=ALU.add, op1=ALU.mult).then_inc(s_hid, 1)
                        if q == KH + 3 or q == UF - 1:
                            bb = 0 if q == KH + 3 else 1
                            dve.wait_ge(s_out, it * NB + bb + 1)
                            yt = y[:, bass.ds(j * TB + bb * TPB, TB)]
                            nc.vector.tensor_tensor(yt, pso[:], yt, ALU.add).then_inc(s_yo, 1)
                    dve.wait_ge(s_y, it * NB + NB)

            @block.tensor
            def _(pe):
                with pe.Fori(0, NBLK) as j:
                    it = L * NBLK + j
                    pe.wait_ge(s_w, (L + 1) * 80)
                    norm.transpose(pe, it, lambda b, k: ps[:, b, k])
                    pe.wait_ge(norm.s_hT, it * NB + NB)

                    def up(q):
                        n, f, b = it * UF + q, q % KH, q // KH
                        M = P if f < KH - 1 else HTAIL
                        if q >= 2:
                            pe.wait_ge(s_hid, n - 1)
                        for i2 in range(2):
                            for k in range(KD):
                                i = nc.tensor.matmul(ps[0:M, q % 2, i2], w1[:, k, i2 * HID + f * P:i2 * HID + f * P + M],
                                                     hT[:, b, k], start=(k == 0), stop=(k == KD - 1))
                        i.then_inc(s_pair, 1)

                    def down(b):
                        pe.wait_ge(s_hid, it * UF + (b + 1) * KH)
                        if b:
                            pe.wait_ge(s_yo, it * NB + b)
                        for f in range(KH):
                            M = P if f < KH - 1 else HTAIL
                            for t in range(TB):
                                i = nc.tensor.matmul(pso[:, t], hid[0:M, b, f, t * P:(t + 1) * P], w2[0:M, f],
                                                     start=(f == 0 and t % 2 == 0), stop=(f == KH - 1 and t % 2 == 1),
                                                     skip_group_check=True)
                        i.then_inc(s_out, 1)

                    for q in range(UF):
                        up(q)
                        if q == KH + 1:
                            down(0)
                    down(1)
                    pe.wait_ge(s_yo, it * NB + NB)


def leave_local_stack(nc, a, keep, y, spill):
    with ExitStack() as ctx:
        m = Pool(nc, ctx, "fin")
        xr = m.sb("xr", [P, NT, D])
        s_g, s_r, s_o = m.sem("gated"), m.sem("ready"), m.sem("stored")
        s_x = [m.sem(f"x_in{n}") for n in range(NT // TB)]
        with nc.Block() as block:
            @block.vector
            def _(dve):
                for n in range(NT // TB):
                    t = slice(n * TB, (n + 1) * TB)
                    g = keep["gates"][:, 1, 1, n // NBLK:n // NBLK + 1].broadcast_to([P, TB, D])
                    nc.vector.tensor_tensor(y[:, t], y[:, t], g, ALU.mult).then_inc(s_g, 1)

            @block.gpsimd
            def _(pool):
                for n in range(NT // TB):
                    t = slice(n * TB, (n + 1) * TB)
                    pool.wait_ge(s_g, n + 1)
                    pool.wait_ge(s_x[n], 16)
                    nc.gpsimd.tensor_tensor(y[:, t], xr[:, t], y[:, t], ALU.add).then_inc(s_r, 1)

            @block.sync
            def _(sp):
                back = spill.rearrange("(t p) d -> p t d", p=P)
                out = a["y"].rearrange("(t p) d -> p t d", p=P)
                for n in range(NT // TB):
                    t = slice(n * TB, (n + 1) * TB)
                    sp.dma_start(xr[:, t], back[:, t]).then_inc(s_x[n], 16)
                for n in range(NT // TB):
                    t = slice(n * TB, (n + 1) * TB)
                    sp.wait_ge(s_r, n + 1)
                    sp.dma_start(out[:, t], y[:, t]).then_inc(s_o, 16)
                sp.wait_ge(s_o, 16 * (NT // TB))


def local_stack(nc, a, keep):
    with ExitStack() as ctx:
        m = Pool(nc, ctx, "stk")
        y = keep["x"]
        spill = nc.dram_tensor("x_aside", [NT * P, D], F32).ap()
        xs_a = m.sb("xs_a", [P, NB, TPB + 1, P])
        xs_b = m.sb("xs_b", [P, NB, TPB + 1, P])
        cos = m.sb("cos", [P, TPB, 2, LHD])
        sin = m.sb("sin", [P, TPB, 2, LHD])
        mask = m.sb("mask", [P, TPB, 2 * P], BF16)
        identb = m.sb("identb", [P, P], BF16)
        s_t, s_mk = m.sem("tables"), m.sem("masks")
        with nc.Block() as block:
            @block.sync
            def _(sp):
                for dst, name in ((cos, "cos"), (sin, "sin")):
                    sp.dma_start(dst[:], a[name]).then_inc(s_t, 16)
                sp.wait_ge(s_t, 32)

            @block.gpsimd
            def _(pool):
                for dst, name in ((mask, "loc_mask"), (identb, "ident")):
                    pool.dma_start(dst[:], a[name]).then_inc(s_mk, 16)
                pool.wait_ge(s_mk, 32)
        enter_local_stack(nc, a, keep, y, xs_a, spill)
        with nc.Fori(0, DEPTH) as layer:
            local_attention(nc, a, keep, y, xs_a, xs_b, (cos, sin, mask, identb), layer)
            gated_mlp(nc, a, keep, y, xs_a, xs_b, layer)
        leave_local_stack(nc, a, keep, y, spill)


def write_out(nc, a, keep):
    with ExitStack() as ctx:
        m = Pool(nc, ctx, "out")
        s_o = m.sem("stored")
        with nc.Block() as block:
            @block.sync
            def _(sp):
                sp.dma_start(a["y"].rearrange("(t p) d -> p t d", p=P), keep["x"][:]).then_inc(s_o, 16)
                sp.wait_ge(s_o, 16)


def build_program(nc, a, stages=(1, 2, 3, 4)):
    with ExitStack() as ctx:
        m = Pool(nc, ctx, "keep")
        keep = {
            "x": m.sb("x", [P, NT, D]),
            "ident": m.sb("ident", [P, P]),
            "modf": m.sb("modf", [P, 2, 6, KD * NB]),
            "gates": m.sb("gates", [P, 2, 2, NB, D]),
            "scale_row": m.sb("scale_row", [P, NB, D]),
            "shift_row": m.sb("shift_row", [P, NB, D]),
            "bmix_gated": m.sb("bmix_gated", [P, NB, D]),
            "eps": m.sb("eps", [P, 1]),
            "u_log": m.sb("u_log", [P, 1]),
            "ss_log": m.sb("ss_log", [P, 1]),
        }
        s_c = m.sem("consts")
        with nc.Block() as block:
            @block.vector
            def _(dve):
                nc.vector.memset(keep["eps"][:], EPS).then_inc(s_c, 1)
                nc.vector.memset(keep["u_log"][:], U_LOG).then_inc(s_c, 1)
                nc.vector.memset(keep["ss_log"][:], SS_LOG).then_inc(s_c, 1)
                dve.wait_ge(s_c, 3)
        load_and_modulate(nc, a, keep)
        if 1 in stages:
            gated_recurrence(nc, a, keep)
        if 2 in stages:
            experts(nc, a, keep)
        if 3 in stages:
            windowed_attention(nc, a, keep)
        if 4 in stages:
            local_stack(nc, a, keep)
        else:
            write_out(nc, a, keep)


def lay_out(inputs):
    c = np.ascontiguousarray
    out = {k: c(inputs[k]) for k in (
        "L0_attn_W_aiv", "L0_attn_decay_bias", "L0_attn_W_mix", "L0_attn_b_mix", "L0_wmod", "L1_wmod",
        "L0_ffn_router_DE", "L0_ffn_w_in_eDF", "L0_ffn_w_swiglu_eDF", "L0_ffn_w_out_eFD")}
    out["L0_c"], out["L1_c"] = c(np.asarray(inputs["L0_c"]).T), c(np.asarray(inputs["L1_c"]).T)
    out["x"] = c(inputs["L0_attn_x"]).reshape(NB * SEQ, D)
    out["L0_attn_decay_bias"] = c(c(inputs["L0_attn_decay_bias"]).reshape(NG, P).T)
    out["shared_in"] = c(np.asarray(inputs["L0_ffn_w_in_shared_FD"]).T)
    out["shared_sw"] = c(np.asarray(inputs["L0_ffn_w_swiglu_FD"]).T)
    out["shared_out"] = c(np.asarray(inputs["L0_ffn_w_out_shared_DF"]).T)
    out["number"] = np.arange(EXP, dtype=np.float32)
    out["ident"] = np.eye(P, dtype=np.float32)
    out["keepmask"] = (np.arange(BLK) % CHUNK != 0).astype(np.float32)
    out["att_wq"] = c(np.asarray(inputs["L1_attn_Wq"]).T)
    wk = np.asarray(inputs["L1_attn_Wk"]).T.reshape(D, AKV, 1, AHD)
    out["att_wk"] = c(np.broadcast_to(wk, (D, AKV, AG, AHD)).reshape(D, D))
    out["att_wv"] = c(np.asarray(inputs["L1_attn_Wv"]).T)
    out["att_wo"] = c(np.asarray(inputs["L1_attn_Wo"]).T)
    out.update(shape_constants())
    out["wqkv"] = c(inputs["L1_ffn_wqkv"])
    out["loc_wo"] = c(inputs["L1_ffn_wo"])
    out["qk_scale"] = np.stack([np.asarray(inputs["L1_ffn_q_scale"]), np.asarray(inputs["L1_ffn_k_scale"])], axis=1)
    out["w1"] = c(inputs["L1_ffn_w1"])
    out["w2"] = c(inputs["L1_ffn_w2"])
    out["b2"] = c(inputs["L1_ffn_b2"])
    col = np.zeros((DEPTH, 2 * KD + 2 * KH, P), np.float32)
    col[:, 0:KD] = np.asarray(inputs["L1_ffn_ln_g"]).reshape(DEPTH, KD, P)
    col[:, KD:2 * KD] = np.asarray(inputs["L1_ffn_ln_b"]).reshape(DEPTH, KD, P)
    b1 = np.asarray(inputs["L1_ffn_b1"])
    for half in range(2):
        part = np.zeros((DEPTH, KH * P), np.float32)
        part[:, :HID] = b1[:, half * HID:(half + 1) * HID]
        col[:, 2 * KD + half * KH:2 * KD + (half + 1) * KH] = part.reshape(DEPTH, KH, P)
    out["mlp_col"] = c(col.transpose(0, 2, 1))
    return out


def shape_constants():
    far = np.float32(-1e30)
    q, key = np.arange(P)[:, None], np.arange(P)[None, :]
    before = np.where(key >= q, 0, far)
    after = np.where(key <= q, 0, far)
    never = np.full((P, P), far)
    win = np.zeros((P, TPB, AW), np.float32)
    loc = np.zeros((P, TPB, 2 * P), np.float32)
    for t in range(TPB):
        win[:, t, 0:P] = loc[:, t, 0:P] = before if t else never
        win[:, t, 2 * P:] = after if t < TPB - 1 else never
        loc[:, t, P:] = after
    half = np.arange(0, LHD, 2, dtype=np.float32)
    inv_freq = np.float32(1.0) / np.float32(10000.0) ** (half / np.float32(LHD))
    t = np.arange(SEQ, dtype=np.float32)
    freqs = t[:, None] * inv_freq[None]
    base = (half + np.float32(0.4 * LHD)) / np.float32(1.4 * LHD)
    scale = (base[None].astype(np.float64) ** ((t - SEQ // 2) / 64.0)[:, None])
    cosf, sinf = np.cos(freqs.astype(np.float64)), np.sin(freqs.astype(np.float64))
    cos, sin = np.zeros((SEQ, 2, LHD)), np.zeros((SEQ, 2, LHD))
    for i, s in enumerate((scale, 1 / scale)):
        cos[:, i] = np.concatenate([cosf * s, cosf * s], axis=1)
        sin[:, i] = np.concatenate([-sinf * s, sinf * s], axis=1)
    tile = lambda x: np.ascontiguousarray(x.reshape(TPB, P, 2, LHD).transpose(1, 0, 2, 3).astype(np.float32))
    return {
        "win_mask": win, "loc_mask": loc,
        "headmask": (np.arange(P)[:, None] // AHD == np.arange(HPC)[None]).astype(np.float32),
        "cos": tile(cos), "sin": tile(sin),
    }


def kernel(**inputs):
    import concourse.bacc as bacc
    from concourse.bass_utils import run_bass_kernel_spmd

    nc = bacc.Bacc("TRN2", target_bir_lowering=False, num_devices=1)
    arrays = {f"in_{name}": value for name, value in lay_out(inputs).items()}
    aps = {name[3:]: nc.dram_tensor(name, value.shape, mybir.dt.from_np(value.dtype), kind="ExternalInput").ap()
           for name, value in arrays.items()}
    aps["y"] = nc.dram_tensor("out_y", (NB * SEQ, D), F32, kind="ExternalOutput").ap()
    build_program(nc, aps)
    result = run_bass_kernel_spmd(nc, [arrays], core_ids=[0])
    return result.results[0]["out_y"].reshape(NB, SEQ, D)
```

```python
from contextlib import ExitStack

import numpy as np

import concourse.bass as bass
from concourse import mybir

F32 = mybir.dt.float32
BF16 = mybir.dt.bfloat16
U32 = mybir.dt.uint32
I32 = mybir.dt.int32
ALU = mybir.AluOpType
ACT = mybir.ActivationFunctionType
AX_X = mybir.AxisListType.X

P = 128
D = 256
KD = D // P
NB = 2
SEQ = 2048
TPB = SEQ // P
NT = NB * TPB
BLK = 512
TB = BLK // P
NBLK = SEQ // BLK
EPS = 1e-5
MODS = ("shift_a", "scale_a", "gate_a", "shift_b", "scale_b", "gate_b")
SHIFT_A, SCALE_A, GATE_A, SHIFT_B, SCALE_B, GATE_B = range(6)
LN_SET = "natural_log_exp_and_others"

REC = 1024
NG = REC // P
CHUNK = 64
CPB = BLK // CHUNK
LN_TINY = float(np.log(1e-10))
U_SCALE = 2.0 ** -10
U_LOG = float(10 * np.log(2.0) / 2)
SIG_FLOOR = float(0.5 * np.log(1e-8)) - U_LOG

AH = 16
AHD = 16
AKV = 4
AG = AH // AKV
HPC = P // AHD
AW = 3 * P
HPR = 2

DEPTH = 2
LH = 8
LHD = 64
INNER = LH * LHD
KI = INNER // P
HID = 682
KH = -(-HID // P)
HTAIL = HID - (KH - 1) * P
QK_SCALE = 8.0
SS_SCALE = 2.0 ** 20
SS_LOG = float(10 * np.log(2.0))

EXP = 8
FF = 512
KF = FF // P
CHOICES = 2
REGION = NB * SEQ + P
XBLOCKS = CHOICES * NB * TPB + EXP
SPARE = EXP
LAST_ROW = EXP * REGION + (SPARE - 1) * P


def on_all(vector, n):
    return vector.rearrange("(a n) -> a n", a=1).broadcast_to([P, n])


class Pool:

    def __init__(self, nc, ctx, name):
        self.nc, self.ctx, self.name = nc, ctx, name
        self.sems = []

    def sb(self, name, shape, dt=F32):
        return self.ctx.enter_context(self.nc.sbuf_tensor(f"sb_{self.name}_{name}", shape, dt))

    def ps(self, name, shape, dt=F32):
        return self.ctx.enter_context(self.nc.psum_tensor(f"ps_{self.name}_{name}", shape, dt))

    def sem(self, name):
        self.sems.append(self.ctx.enter_context(self.nc.semaphore(f"{self.name}_{name}")))
        return self.sems[-1]

    def clear(self):
        with self.nc.Block() as block:
            @block.gpsimd
            def _(pool):
                for sem in self.sems:
                    pool.sem_clear(sem)


class BlockNorm:

    def __init__(self, m, keep, halves, scale, shift):
        self.nc, self.keep, self.halves, self.scale, self.shift = m.nc, keep, halves, scale, shift
        self.stats = m.sb("stats", [P, NB, TB, KD, 6])
        self.mv = m.sb("mv", [P, NB, TB, 2])
        self.settle = m.sb("settle", [P, 1])
        self.lnv = m.sb("lnv", [P, NB, TB])
        self.rstd = m.sb("rstd", [P, NB, TB])
        self.nmr = m.sb("nmr", [P, NB, TB])
        self.xn = m.sb("xn", [P, NB, TB, D])
        self.hT = m.sb("hT", [P, NB, KD, BLK])
        (self.s_st, self.s_mv, self.s_ln, self.s_rstd, self.s_nmr, self.s_xn, self.s_tr, self.s_hT) = (
            m.sem(n) for n in ("stats", "mv", "lnv", "rstd", "nmr", "xn", "tr", "hT"))

    def normalise(self, dve, it, j=None):
        nc = self.nc
        j = it if j is None else j
        for b in range(NB):
            for t in range(TB):
                parts = self.halves(b, t, j)
                for k, part in enumerate(parts):
                    i = nc.vector.bn_stats(self.stats[:, b, t, k], part)
            i.then_inc(self.s_st, 1)
        dve.wait_ge(self.s_st, it * NB + NB)
        nc.vector.memset(self.settle[:], 0.0)
        for b in range(NB):
            for t in range(TB):
                i = nc.vector.bn_aggr(self.mv[:, b, t], self.stats[:, b, t, 0:len(self.halves(b, t, j))])
            i.then_inc(self.s_mv, 1)
        for b in range(NB):
            dve.wait_ge(self.s_rstd, it * NB + b + 1)
            dve.wait_ge(self.s_mv, it * NB + b + 1)
            nc.vector.scalar_tensor_tensor(out=self.nmr[:, b], in0=self.mv[:, b, :, 0], scalar=-1.0,
                                           in1=self.rstd[:, b], op0=ALU.mult, op1=ALU.mult).then_inc(self.s_nmr, 1)
            dve.wait_ge(self.s_nmr, it * NB + b + 1)
            for t in range(TB):
                parts = self.halves(b, t, j)
                w = D // len(parts)
                for k, part in enumerate(parts):
                    i = nc.vector.tensor_scalar(self.xn[:, b, t, k * w:(k + 1) * w], part, self.rstd[:, b, t:t + 1],
                                                self.nmr[:, b, t:t + 1], ALU.mult, ALU.add)
            i.then_inc(self.s_xn, 1)

    def inverse_deviation(self, act, it):
        nc = self.nc
        for b in range(NB):
            act.wait_ge(self.s_mv, it * NB + b + 1)
            nc.scalar.activation(self.lnv[:, b], self.mv[:, b, :, 1], ACT.Ln,
                                 bias=self.keep["eps"][:, 0:1]).then_inc(self.s_ln, 1)
            act.wait_ge(self.s_ln, it * NB + b + 1)
            nc.scalar.activation(self.rstd[:, b], self.lnv[:, b], ACT.Exp, scale=-0.5).then_inc(self.s_rstd, 1)

    def transpose(self, pe, it, psum):
        for b in range(NB):
            pe.wait_ge(self.s_xn, it * NB + b + 1)
            for k in range(KD):
                for t in range(TB):
                    i = self.nc.tensor.transpose(psum(b, k)[:, t * P:(t + 1) * P],
                                                 self.xn[:, b, t, k * P:(k + 1) * P], self.keep["ident"][:])
            i.then_inc(self.s_tr, 1)

    def affine(self, act, it, psum):
        for b in range(NB):
            act.wait_ge(self.s_tr, it * NB + b + 1)
            for k in range(KD):
                i = self.nc.scalar.activation(self.hT[:, b, k], psum(b, k), ACT.Identity,
                                              scale=self.scale(b, k), bias=self.shift(b, k))
            i.then_inc(self.s_hT, 1)


def load_and_modulate(nc, a, keep):
    with ExitStack() as ctx:
        m = Pool(nc, ctx, "mod")
        cT = m.sb("cT", [P, 2, KD, NB])
        cs = m.sb("cs", [P, 2, KD, NB])
        cwide = m.sb("cwide", [P, 2, KD, NB, P])
        wmod = m.sb("wmod", [P, 2, KD, 6 * D])
        rows = m.sb("rows", [P, 2, NB, 6 * D])
        sign = m.sb("sign", [P, 4, D])
        size = m.sb("size", [P, 4, D])
        ps_row = m.ps("ps_row", [P, 2, 512])
        ps_col = m.ps("ps_col", [P, 2, 512])
        s_c, s_w, s_x, s_k, s_bm = (m.sem(n) for n in ("c_in", "wmod_in", "x_in", "const_in", "bmix_in"))
        s_silu, s_wide, s_row, s_rowcp, s_col, s_colcp = (
            m.sem(n) for n in ("silu", "wide", "row", "rowcp", "col", "colcp"))
        s_g = m.sem("guard")

        with nc.Block() as block:
            @block.sync
            def _(sp):
                for l, name in enumerate(("L0_c", "L1_c")):
                    sp.dma_start(cT[:, l], a[name].rearrange("(k p) b -> p k b", p=P)).then_inc(s_c, 16)
                for l, name in enumerate(("L0_wmod", "L1_wmod")):
                    sp.dma_start(wmod[:, l], a[name].rearrange("(k p) n -> p k n", p=P)).then_inc(s_w, 16)
                sp.dma_start(keep["ident"][:], a["ident"]).then_inc(s_k, 16)
                sp.dma_start(keep["bmix_gated"][:, 0], on_all(a["L0_attn_b_mix"], D)).then_inc(s_bm, 16)
                sp.dma_start(keep["x"][:], a["x"].rearrange("(t p) d -> p t d", p=P)).then_inc(s_x, 16)
                sp.wait_ge(s_k, 16)
                sp.wait_ge(s_x, 16)

            @block.scalar
            def _(act):
                act.wait_ge(s_c, 32)
                nc.scalar.activation(cs[:], cT[:], ACT.Silu).then_inc(s_silu, 1)
                for n in range(12):
                    act.wait_ge(s_row, n + 1)
                    l, b, c = n // 6, n // 3 % 2, n % 3
                    nc.scalar.copy(rows[:, l, b, c * 512:(c + 1) * 512], ps_row[:, n % 2]).then_inc(s_rowcp, 1)

            @block.tensor
            def _(pe):
                pe.wait_ge(s_w, 32)
                pe.wait_ge(s_silu, 1)
                for l in range(2):
                    for c in range(6 * KD):
                        for k in range(KD):
                            mm = nc.tensor.matmul(ps_col[:, l, 2 * c:2 * c + 2], wmod[:, l, k, c * P:(c + 1) * P],
                                                  cs[:, l, k], start=(k == 0), stop=(k == KD - 1))
                mm.then_inc(s_col, 1)
                pe.wait_ge(s_wide, 1)
                for n in range(12):
                    l, b, c = n // 6, n // 3 % 2, n % 3
                    if n >= 2:
                        pe.wait_ge(s_rowcp, n - 1)
                    for k in range(KD):
                        mm = nc.tensor.matmul(ps_row[:, n % 2], cwide[:, l, k, b],
                                              wmod[:, l, k, c * 512:(c + 1) * 512], start=(k == 0), stop=(k == KD - 1))
                    mm.then_inc(s_row, 1)

            @block.vector
            def _(dve):
                dve.wait_ge(s_silu, 1)
                for l in range(2):
                    for k in range(KD):
                        i = nc.vector.tensor_copy(cwide[:, l, k], cs[:, l, k].unsqueeze(2).broadcast_to([P, NB, P]))
                i.then_inc(s_wide, 1)
                dve.wait_ge(s_col, 1)
                nc.vector.tensor_copy(keep["modf"][:], ps_col[:, :, 0:24].rearrange("p l (j n) -> p l j n", n=2 * KD)
                                      ).then_inc(s_colcp, 1)
                dve.wait_ge(s_colcp, 1)
                for j in (SCALE_A, SCALE_B):
                    nc.vector.tensor_scalar(keep["modf"][:, :, j], keep["modf"][:, :, j], 1.0, None,
                                            ALU.add).then_inc(s_colcp, 1)
                dve.wait_ge(s_rowcp, 12)
                n = 0
                for l in range(2):
                    for w, j in enumerate((GATE_A, GATE_B)):
                        g = rows[:, l, :, j * D:(j + 1) * D]
                        sg = sign[:, 2 * w:2 * w + 2]
                        sz = size[:, 2 * w:2 * w + 2]
                        nc.vector.tensor_scalar(sg, g, 0.0, 2.0, ALU.is_ge, ALU.mult).then_inc(s_g, 1)
                        nc.vector.scalar_tensor_tensor(out=sz, in0=g, scalar=-1.0, in1=g, op0=ALU.mult,
                                                       op1=ALU.max).then_inc(s_g, 1)
                        dve.wait_ge(s_g, n + 2)
                        nc.vector.tensor_scalar(sz, sz, 0.25, None, ALU.max).then_inc(s_g, 1)
                        dve.wait_ge(s_g, n + 3)
                        nc.vector.scalar_tensor_tensor(out=keep["gates"][:, l, w], in0=sg, scalar=-1.0, in1=sz,
                                                       op0=ALU.add, op1=ALU.mult).then_inc(s_g, 1)
                        n += 4
                        dve.wait_ge(s_g, n)
                nc.vector.tensor_scalar(keep["moe_scale_row"][:], rows[:, 0, :, SCALE_B * D:(SCALE_B + 1) * D], 1.0, None,
                                        ALU.add)
                nc.vector.tensor_copy(keep["moe_shift_row"][:], rows[:, 0, :, SHIFT_B * D:(SHIFT_B + 1) * D])
                nc.vector.tensor_scalar(keep["scale_row"][:], rows[:, 1, :, SCALE_B * D:(SCALE_B + 1) * D], 1.0, None,
                                        ALU.add).then_inc(s_g, 1)
                nc.vector.tensor_copy(keep["shift_row"][:], rows[:, 1, :, SHIFT_B * D:(SHIFT_B + 1) * D]).then_inc(s_g, 1)
                dve.wait_ge(s_bm, 16)
                bm = keep["bmix_gated"]
                nc.vector.tensor_tensor(bm[:, 1], bm[:, 0], keep["gates"][:, 0, 0, 1], ALU.mult).then_inc(s_g, 1)
                dve.wait_ge(s_g, n + 3)
                nc.vector.tensor_tensor(bm[:, 0], bm[:, 0], keep["gates"][:, 0, 0, 0], ALU.mult).then_inc(s_g, 1)
                dve.wait_ge(s_g, n + 4)
                dve.wait_ge(s_colcp, 3)
        m.clear()


def gated_recurrence(nc, a, keep):
    x, modf, ident = keep["x"], keep["modf"], keep["ident"]
    with ExitStack() as ctx:
        m = Pool(nc, ctx, "rec")
        w = m.sb("w", [P, KD, 3 * REC])
        wmix = m.sb("wmix", [P, NG, D])
        nbias = m.sb("nbias", [P, NG])
        keepmask = m.sb("keepmask", [P, BLK])
        ones = m.sb("ones", [P, CPB])
        norm = BlockNorm(m, keep, lambda b, t, it: [x[:, bass.ds(it * TB + b * TPB + t, 1)]],
                         lambda b, k: modf[:, 0, SCALE_A, NB * k + b:NB * k + b + 1],
                         lambda b, k: modf[:, 0, SHIFT_A, NB * k + b:NB * k + b + 1])
        hT = norm.hT
        e = m.sb("e", [P, 2, 2, BLK])
        u = m.sb("u", [P, 2, BLK])
        l = m.sb("l", [P, 2, 2, BLK])
        lu = m.sb("lu", [P, 2, BLK])
        cum = m.sb("cum", [P, 2, BLK])
        q = m.sb("q", [P, 2, BLK])
        z = m.sb("z", [P, 2, BLK])
        ez = m.sb("ez", [P, 2, BLK])
        dec = m.sb("dec", [P, 2, BLK])
        wt = m.sb("wt", [P, 2, BLK])
        ws = m.sb("ws", [P, 2, BLK])
        st = m.sb("st", [P, 3, BLK])
        last = m.sb("last", [P, 2, CPB])
        lc = m.sb("lc", [P, NB, NG, CPB + 1])
        lcm = m.sb("lcm", [P, 2, CPB])
        c9 = m.sb("c9", [P, 2, CPB])
        rc = m.sb("rc", [P, 2, CPB])
        fin = m.sb("fin", [P, 2, CPB])
        fin2 = m.sb("fin2", [P, 2, CPB])
        cw = m.sb("cw", [P, NB, NG, CPB + 1])
        inc = m.sb("inc", [P, 2, CPB])
        og = m.sb("og", [P, TB, D])
        ps = m.ps("ps", [P, 2, 3, BLK])
        pso = m.ps("pso", [P, TB, D])

        s_w, s_wm = m.sem("w_in"), m.sem("wmix_in")
        (s_aiv, s_e, s_ec, s_u, s_l, s_lu, s_cum, s_q, s_q2, s_z, s_last, s_lc, s_lcm, s_ez, s_rc) = (
            m.sem(n) for n in ("aiv", "e", "ec", "u", "l", "lu", "cum", "q", "q2", "z", "last", "lc", "lcm", "ez", "rc"))
        (s_wt, s_ws, s_fin, s_fin2, s_cw, s_inc, s_carry, s_wi, s_state, s_mix, s_og, s_ogb, s_x) = (
            m.sem(n) for n in ("wt", "ws", "fin", "fin2", "cw", "inc", "carry", "wi", "state", "mix", "og", "ogb", "x"))
        s_init = m.sem("init")
        US = NB * NG

        with nc.Block() as block:
            @block.sync
            def _(sp):
                for k in range(KD):
                    sp.dma_start(w[:, k], a["L0_attn_W_aiv"][k * P:(k + 1) * P]).then_inc(s_w, 16)
                sp.dma_start(nbias[:], a["L0_attn_decay_bias"]).then_inc(s_w, 16)
                sp.dma_start(keepmask[:], on_all(a["keepmask"], BLK)).then_inc(s_w, 16)
                sp.dma_start(wmix[:], a["L0_attn_W_mix"].rearrange("(g p) d -> p g d", p=P)).then_inc(s_wm, 16)

            @block.gpsimd
            def _(pool):
                with pool.Fori(0, NBLK) as it:
                    for s in range(US + 1):
                        if s >= 1:
                            b, g, par, n = (s - 1) // NG, (s - 1) % NG, (s - 1) % 2, it * US + s
                            pool.wait_ge(s_inc, n)
                            nc.gpsimd.tensor_tensor(ws[:, par].rearrange("p (c t) -> p c t", c=CPB),
                                                    ws[:, par].rearrange("p (c t) -> p c t", c=CPB),
                                                    inc[:, par].unsqueeze(2).broadcast_to([P, CPB, CHUNK]),
                                                    ALU.add).then_inc(s_wi, 1)
                            pool.wait_ge(s_wi, n)
                            nc.gpsimd.tensor_tensor(st[:, (s - 1) % 3], ws[:, par], dec[:, par],
                                                    ALU.mult).then_inc(s_state, 1)
                        if s and s % NG == 0:
                            b = s // NG - 1
                            pool.wait_ge(s_og, it * NB + b + 1)
                            nc.gpsimd.tensor_tensor(og[:], og[:], keep["bmix_gated"][:, b:b + 1].broadcast_to([P, TB, D]),
                                                    ALU.add).then_inc(s_ogb, 1)
                            pool.wait_ge(s_ogb, it * NB + b + 1)
                            xt = x[:, bass.ds(it * TB + b * TPB, TB)]
                            nc.gpsimd.tensor_tensor(xt, xt, og[:], ALU.add).then_inc(s_x, 1)

            @block.scalar
            def _(act):
                nc.scalar.preload_act_table_set(LN_SET)
                act.wait_ge(s_init, 1)
                with act.Fori(0, NBLK) as it:
                    norm.inverse_deviation(act, it)
                    norm.affine(act, it, lambda b, k: ps[:, b, k])

                    def first(s):
                        b, g, par, n = s // NG, s % NG, s % 2, it * US + s
                        act.wait_ge(s_aiv, n + 1)
                        nc.scalar.activation(e[:, par, 0], ps[:, par, 0], ACT.Exp, scale=-1.0, bias=nbias[:, g:g + 1])
                        nc.scalar.activation(e[:, par, 1], ps[:, par, 1], ACT.Exp, scale=-1.0).then_inc(s_e, 1)

                    def logs(s):
                        par, n = s % 2, it * US + s
                        act.wait_ge(s_ec, n + 1)
                        nc.scalar.activation(l[:, par], e[:, par], ACT.Ln, bias=1.0).then_inc(s_l, 1)
                        act.wait_ge(s_u, n + 1)
                        nc.scalar.activation(lu[:, par], u[:, par], ACT.Ln, scale=U_SCALE).then_inc(s_lu, 1)

                    def exps(s):
                        b, g, par, n = s // NG, s % NG, s % 2, it * US + s
                        act.wait_ge(s_z, n + 1)
                        nc.scalar.activation(ez[:, par], z[:, par], ACT.Exp, scale=-1.0,
                                             bias=keep["u_log"][:, 0:1]).then_inc(s_ez, 1)
                        act.wait_ge(s_lcm, n + 1)
                        if s >= 2:
                            act.wait_ge(s_state, n - 1)
                        nc.scalar.activation(dec[:, par], cum[:, par], ACT.Exp)
                        nc.scalar.activation(c9[:, par], lc[:, b, g, 0:CPB], ACT.Exp)
                        nc.scalar.activation(rc[:, par], lcm[:, par], ACT.Exp, scale=-1.0).then_inc(s_rc, 1)

                    for s in range(US + 1):
                        if s < US:
                            first(s)
                        if s >= 1:
                            exps(s - 1)
                        if s < US:
                            logs(s)

            @block.vector
            def _(dve):
                nc.vector.memset(lc[:], 0.0)
                nc.vector.memset(cw[:], 0.0)
                nc.vector.memset(ones[:], 1.0)
                dve.wait_ge(s_w, 16 * 4)
                nc.vector.tensor_scalar(nbias[:], nbias[:], -1.0, None, ALU.mult).then_inc(s_init, 1)
                dve.wait_ge(s_init, 1)
                with dve.Fori(0, NBLK) as it:
                    norm.normalise(dve, it)

                    def clamp(s):
                        par, n = s % 2, it * US + s
                        dve.wait_ge(s_e, n + 1)
                        nc.vector.tensor_scalar(e[:, par, 0], e[:, par, 0], 1e-12, 1e10, ALU.max, ALU.min)
                        nc.vector.tensor_scalar(e[:, par, 1], e[:, par, 1], 1e19, None, ALU.min).then_inc(s_ec, 1)
                        dve.wait_ge(s_ec, n + 1)
                        nc.vector.scalar_tensor_tensor(out=u[:, par], in0=e[:, par, 0], scalar=2.0, in1=e[:, par, 0],
                                                       op0=ALU.add, op1=ALU.mult).then_inc(s_u, 1)

                    def sums(s):
                        b, g, par, n = s // NG, s % NG, s % 2, it * US + s
                        dve.wait_ge(s_l, n + 1)
                        nc.vector.tensor_tensor_scan(cum[:, par], keepmask[:], l[:, par, 0], 0.0, ALU.mult,
                                                     ALU.subtract).then_inc(s_cum, 1)
                        dve.wait_ge(s_lu, n + 1)
                        nc.vector.scalar_tensor_tensor(out=q[:, par], in0=lu[:, par], scalar=0.5, in1=l[:, par, 0],
                                                       op0=ALU.mult, op1=ALU.subtract).then_inc(s_q, 1)
                        dve.wait_ge(s_q, n + 1)
                        nc.vector.scalar_tensor_tensor(out=q[:, par], in0=q[:, par], scalar=SIG_FLOOR, in1=l[:, par, 1],
                                                       op0=ALU.max, op1=ALU.subtract).then_inc(s_q2, 1)
                        dve.wait_ge(s_q2, n + 1)
                        nc.vector.scalar_tensor_tensor(out=z[:, par], in0=cum[:, par], scalar=LN_TINY, in1=q[:, par],
                                                       op0=ALU.max, op1=ALU.subtract).then_inc(s_z, 1)
                        ends = cum[:, par].rearrange("p (c t) -> p c t", c=CPB)[:, :, CHUNK - 1]
                        nc.vector.tensor_scalar(last[:, par], ends, LN_TINY, None, ALU.max).then_inc(s_last, 1)
                        dve.wait_ge(s_last, n + 1)
                        nc.vector.tensor_tensor_scan(lc[:, b, g, 1:CPB + 1], ones[:], last[:, par], lc[:, b, g, 0:1],
                                                     ALU.mult, ALU.add).then_inc(s_lc, 1)
                        dve.wait_ge(s_lc, n + 1)
                        nc.vector.tensor_scalar(lcm[:, par], lc[:, b, g, 1:CPB + 1], LN_TINY, None,
                                                ALU.max).then_inc(s_lcm, 1)

                    def states(s):
                        b, g, par, n = s // NG, s % NG, s % 2, it * US + s
                        dve.wait_ge(s_ez, n + 1)
                        nc.vector.tensor_tensor(wt[:, par], ps[:, par, 2], ez[:, par], ALU.mult).then_inc(s_wt, 1)
                        dve.wait_ge(s_wt, n + 1)
                        if s >= 2:
                            dve.wait_ge(s_state, n - 1)
                        nc.vector.tensor_tensor_scan(ws[:, par], keepmask[:], wt[:, par], 0.0, ALU.mult,
                                                     ALU.add).then_inc(s_ws, 1)
                        dve.wait_ge(s_rc, n + 1)
                        dve.wait_ge(s_ws, n + 1)
                        wend = ws[:, par].rearrange("p (c t) -> p c t", c=CPB)[:, :, CHUNK - 1]
                        dend = dec[:, par].rearrange("p (c t) -> p c t", c=CPB)[:, :, CHUNK - 1]
                        nc.vector.tensor_tensor(fin[:, par], wend, dend, ALU.mult).then_inc(s_fin, 1)
                        dve.wait_ge(s_fin, n + 1)
                        nc.vector.tensor_tensor(fin2[:, par], fin[:, par], rc[:, par], ALU.mult).then_inc(s_fin2, 1)
                        dve.wait_ge(s_fin2, n + 1)
                        nc.vector.tensor_tensor_scan(cw[:, b, g, 1:CPB + 1], ones[:], fin2[:, par], cw[:, b, g, 0:1],
                                                     ALU.mult, ALU.add).then_inc(s_cw, 1)
                        dve.wait_ge(s_cw, n + 1)
                        nc.vector.tensor_tensor(inc[:, par], cw[:, b, g, 0:CPB], c9[:, par], ALU.mult).then_inc(s_inc, 1)
                        dve.wait_ge(s_inc, n + 1)
                        nc.vector.tensor_copy(lc[:, b, g, 0:1], lc[:, b, g, CPB:CPB + 1])
                        nc.vector.tensor_copy(cw[:, b, g, 0:1], cw[:, b, g, CPB:CPB + 1]).then_inc(s_carry, 1)

                    for s in range(US + 1):
                        if s < US:
                            clamp(s)
                        if s >= 1:
                            states(s - 1)
                        if s < US:
                            sums(s)
                        if s and s % NG == 0:
                            b = s // NG - 1
                            dve.wait_ge(s_mix, it * NB + b + 1)
                            if b:
                                dve.wait_ge(s_x, it * NB + b)
                            nc.vector.tensor_tensor(og[:], pso[:], keep["gates"][:, 0, 0, b:b + 1].broadcast_to([P, TB, D]),
                                                    ALU.mult).then_inc(s_og, 1)
                    dve.wait_ge(s_x, it * NB + NB)

            @block.tensor
            def _(pe):
                pe.wait_ge(s_w, 16 * 4)
                pe.wait_ge(s_wm, 16)
                with pe.Fori(0, NBLK) as it:
                    norm.transpose(pe, it, lambda b, k: ps[:, b, k])

                    def project(s):
                        b, g, par, n = s // NG, s % NG, s % 2, it * US + s
                        pe.wait_ge(norm.s_hT, it * NB + NB)
                        if s >= 2:
                            pe.wait_ge(s_wt, n - 1)
                        for j in range(3):
                            for k in range(KD):
                                i = nc.tensor.matmul(ps[:, par, j], w[:, k, j * REC + g * P:j * REC + (g + 1) * P],
                                                     hT[:, b, k], start=(k == 0), stop=(k == KD - 1))
                        i.then_inc(s_aiv, 1)

                    def mix(s):
                        b, g, n = s // NG, s % NG, it * US + s
                        pe.wait_ge(s_state, n + 1)
                        if g == 0 and b:
                            pe.wait_ge(s_og, it * NB + b)
                        for t in range(TB):
                            i = nc.tensor.matmul(pso[:, t], st[:, s % 3, t * P:(t + 1) * P], wmix[:, g],
                                                 start=(g == 0 and t % 2 == 0), stop=(g == NG - 1 and t % 2 == 1),
                                                 skip_group_check=True)
                        if g == NG - 1:
                            i.then_inc(s_mix, 1)

                    for s in range(US + 2):
                        if s < US:
                            project(s)
                        if s >= 2:
                            mix(s - 2)
                    pe.wait_ge(s_og, it * NB + NB)
        m.clear()


def experts(nc, a, keep):
    with ExitStack() as ctx:
        m = Pool(nc, ctx, "moe")
        soft = {name: keep["soft"].sem(name) for name in ("before_in", "sorted", "padded", "got0", "got1")}
        t = {
            "w_in": m.sb("w_in", [P, EXP + 1, KD, FF]),
            "w_sw": m.sb("w_sw", [P, EXP + 1, KD, FF]),
            "row": m.sb("row", [P, NBLK, NB * TB, 2], U32),
            "block_expert": m.sb("block_expert", [1, XBLOCKS], I32),
            "block_row": m.sb("block_row", [1, XBLOCKS], I32),
            "sorted": nc.dram_tensor("sorted_tokens", [(EXP + 1) * REGION, D], F32).ap(),
            "results": nc.dram_tensor("expert_results", [XBLOCKS * P, D], F32).ap(),
            "w_here": m.sem("weights_in"),
            "soft": soft,
        }
        route_tokens(nc, a, keep, t)
        run_experts(nc, a, keep, t)
        collect_experts(nc, a, keep, t)
        m.clear()


def route_tokens(nc, a, keep, t):
    x, modf, ident = keep["x"], keep["modf"], keep["ident"]
    w_in, w_sw = t["w_in"], t["w_sw"]
    TI = NB * TB
    UF = NB * KF
    with ExitStack() as ctx:
        m = Pool(nc, ctx, "route")
        norm = BlockNorm(m, keep, lambda b, t, it: [x[:, bass.ds(it * TB + b * TPB + t, 1)]],
                         lambda b, k: modf[:, 0, SCALE_B, NB * k + b:NB * k + b + 1],
                         lambda b, k: modf[:, 0, SHIFT_B, NB * k + b:NB * k + b + 1])
        hT = norm.hT
        w_out = m.sb("w_out", [P, KF, D])
        router = m.sb("router", [P, KD, EXP])
        number = m.sb("number", [P, EXP])
        region = m.sb("region", [P, EXP])
        iota = m.sb("iota", [P, 1])
        steps = m.sb("steps", [P, SEQ * NB // P])
        block_no = m.sb("block_no", [1, XBLOCKS])
        before = m.sb("before", [P, P], BF16)
        ones = m.sb("ones", [P, P], BF16)
        zeros = m.sb("zeros", [P, D])
        score = m.sb("score", [P, TI, EXP])
        top = m.sb("top", [P, TI, 8])
        topi = m.sb("topi", [P, TI, 8], U32)
        topf = m.sb("topf", [P, TI, 8])
        pick = m.sb("pick", [P, 2, TI, EXP])
        chosen = m.sb("chosen", [P, TI, EXP], BF16)
        run = m.sb("run", [P, EXP])
        place = m.sb("place", [P, 2, TI, EXP])
        rowf = m.sb("rowf", [P, TI, 2])
        rowu = m.sb("rowu", [P, TI, 2], U32)
        rows = m.sb("rows", [P, NBLK, TI, 2])
        gate = m.sb("gate", [P, TI, 2])
        gated = m.sb("gated", [P, TI, 2, D])
        act_f = m.sb("act_f", [P, 2, BLK])
        hid = m.sb("hid", [P, 2, KF, BLK])
        og = m.sb("og", [P, TB, D])
        settle = m.sb("settle1", [P, 1])
        padf = m.sb("padf", [P, EXP])
        padu = m.sb("padu", [P, EXP], U32)
        count = m.sb("count", [P, EXP])
        over = m.sb("over", [P, EXP, SEQ * NB // P])
        blocks = m.sb("blocks", [P, EXP])
        end = m.sb("end", [P, EXP])
        past = m.sb("past", [1, 2, XBLOCKS, EXP])
        bexp = m.sb("bexp", [1, XBLOCKS])
        brow = m.sb("brow", [1, 2, XBLOCKS])
        shift = m.sb("shift", [P, 3, EXP])
        above = m.sb("above", [P, 2, NBLK * TI * 2, EXP])
        moved = m.sb("moved", [P, NBLK * TI * 2])
        ps = m.ps("ps", [P, 2, 2, BLK])
        pso = m.ps("pso", [P, TB, D])
        psg = m.ps("psg", [P, BLK])
        psr = m.ps("psr", [P, BLK])
        s_b, s_sorted, s_padded = (t["soft"][n] for n in ("before_in", "sorted", "padded"))
        names = ("w_load ones score scorecp top topi topf pick chosen es es1 gate rank run place placed rowf rowu row "
                 "hmul h gated pair silu hid out og xadd pad padzero table settle")
        (s_w, s_ones, s_score, s_scorecp, s_top, s_topi, s_topf, s_pick, s_chosen, s_es, s_es1, s_gate, s_rank, s_run,
         s_place, s_placed, s_rowf, s_rowu, s_row, s_hmul, s_h, s_gated, s_pair, s_silu, s_hid, s_out, s_og, s_x,
         s_pad, s_padzero, s_table, s_settle) = (m.sem(n) for n in names.split())
        ROUTED = TI * 2

        with nc.Block() as block:
            @block.sync
            def _(sp):
                sp.dma_start(router[:], a["L0_ffn_router_DE"].rearrange("(k p) e -> p k e", p=P)).then_inc(s_w, 16)
                sp.dma_start(number[:], on_all(a["number"], EXP)).then_inc(s_w, 16)
                sp.dma_start(region[:], on_all(a["region"], EXP)).then_inc(s_w, 16)
                sp.dma_start(iota[:], a["iota"]).then_inc(s_w, 16)
                sp.dma_start(steps[:], on_all(a["steps"], SEQ * NB // P)).then_inc(s_w, 16)
                sp.dma_start(block_no[:], a["block_no"].unsqueeze(0)).then_inc(s_w, 16)
                sp.dma_start(w_in[:, EXP], a["shared_in"].rearrange("(k p) f -> p k f", p=P)).then_inc(s_w, 16)
                sp.dma_start(w_sw[:, EXP], a["shared_sw"].rearrange("(k p) f -> p k f", p=P)).then_inc(s_w, 16)
                sp.dma_start(w_out[:], a["shared_out"].rearrange("(k p) d -> p k d", p=P)).then_inc(s_w, 16)
                for e in range(EXP):
                    for dst, name in ((w_in, "L0_ffn_w_in_eDF"), (w_sw, "L0_ffn_w_swiglu_eDF")):
                        sp.dma_start(dst[:, e], a[name][e].rearrange("(k p) f -> p k f", p=P)).then_inc(t["w_here"], 16)
                sp.wait_ge(s_ones, 3)
                spare = t["sorted"][EXP * REGION:EXP * REGION + SPARE * P]
                sp.dma_start(spare.rearrange("(n p) d -> p n d", p=P), zeros[:].unsqueeze(1).broadcast_to([P, SPARE, D])
                             ).then_inc(s_padzero, 16)

            @block.gpsimd
            def _(pool):
                pool.dma_start(before[:], a["before"]).then_inc(s_b, 16)
                pool.wait_ge(s_w, 16 * 9)
                with pool.Fori(0, NBLK) as it:
                    for b in range(NB):
                        u = it * NB + b + 1
                        pool.wait_ge(norm.s_tr, u)
                        xn = norm.xn[:, b]
                        nc.gpsimd.tensor_tensor(xn, xn, keep["moe_scale_row"][:, b:b + 1].broadcast_to([P, TB, D]),
                                                ALU.mult).then_inc(s_hmul, 1)
                        pool.wait_ge(s_hmul, u)
                        nc.gpsimd.tensor_tensor(xn, xn, keep["moe_shift_row"][:, b:b + 1].broadcast_to([P, TB, D]),
                                                ALU.add).then_inc(s_h, 1)
                    pool.wait_ge(s_gated, it + 1)
                    pool.wait_ge(s_rowu, it + 1)
                    nc.gpsimd.tensor_tensor(settle[:], keep["one"][:], keep["one"][:], ALU.mult).then_inc(s_settle, 1)
                    for n in range(TI):
                        for c in range(2):
                            pool.indirect_dma_start(t["sorted"], bass.IndirectOffsetOnAxis(ap=rowu[:, n, c:c + 1], axis=0),
                                                    gated[:, n, c], None).then_inc(s_sorted, 16)
                    pool.wait_ge(s_settle, it + 1)
                    for b in range(NB):
                        pool.wait_ge(s_og, it * NB + b + 1)
                        xt = x[:, bass.ds(it * TB + b * TPB, TB)]
                        nc.gpsimd.tensor_tensor(xt, xt, og[:], ALU.add).then_inc(s_x, 1)
                pool.wait_ge(s_pad, 2)
                pool.wait_ge(s_sorted, NBLK * ROUTED * 16)
                for e in range(EXP):
                    pool.indirect_dma_start(t["sorted"], bass.IndirectOffsetOnAxis(ap=padu[:, e:e + 1], axis=0),
                                            zeros[:], None).then_inc(s_padded, 16)
                pool.wait_ge(s_padded, EXP * 16)
                pool.wait_ge(s_padzero, 16)

            @block.scalar
            def _(act):
                with act.Fori(0, NBLK) as it:
                    nc.scalar.preload_act_table_set(LN_SET)
                    norm.inverse_deviation(act, it)
                    norm.affine(act, it, lambda b, k: ps[:, b, k])
                    act.wait_ge(s_top, it + 1)
                    nc.scalar.activation(gate[:], top[:, :, 0:2], ACT.Exp, scale=-1.0).then_inc(s_es, 1)
                    for q in range(UF):
                        n = it * UF + q
                        act.wait_ge(s_pair, n + 1)
                        if q >= 2:
                            act.wait_ge(s_hid, n - 1)
                        nc.scalar.activation(act_f[:, q % 2], ps[:, q % 2, 0], ACT.Silu).then_inc(s_silu, 1)

            @block.vector
            def _(dve):
                nc.vector.memset(ones[:], 1.0).then_inc(s_ones, 1)
                nc.vector.memset(zeros[:], 0.0).then_inc(s_ones, 2)
                dve.wait_ge(s_w, 16 * 9)
                nc.vector.tensor_copy(run[:], region[:]).then_inc(s_run, 1)
                with dve.Fori(0, NBLK) as it:
                    u = it + 1
                    norm.normalise(dve, it)
                    dve.wait_ge(s_score, u)
                    nc.vector.tensor_copy(score[:], psg[:, 0:TI * EXP].rearrange("p (t e) -> p t e", e=EXP)
                                          ).then_inc(s_scorecp, 1)
                    dve.wait_ge(s_scorecp, u)
                    nc.vector.memset(norm.settle[:], 0.0)
                    for n in range(TI):
                        i = nc.vector.max(top[:, n], score[:, n])
                    i.then_inc(s_top, 1)
                    dve.wait_ge(s_top, u)
                    nc.vector.memset(norm.settle[:], 0.0)
                    for n in range(TI):
                        i = nc.vector.max_index(topi[:, n], top[:, n], score[:, n])
                    i.then_inc(s_topi, 1)
                    dve.wait_ge(s_topi, u)
                    nc.vector.tensor_copy(topf[:], topi[:]).then_inc(s_topf, 1)
                    dve.wait_ge(s_topf, u)
                    for c in range(2):
                        i = nc.vector.tensor_tensor(pick[:, c], number[:].unsqueeze(1).broadcast_to([P, TI, EXP]),
                                                    topf[:, :, c:c + 1].broadcast_to([P, TI, EXP]), ALU.is_equal)
                    i.then_inc(s_pick, 1)
                    dve.wait_ge(s_pick, u)
                    nc.vector.tensor_tensor(chosen[:], pick[:, 0], pick[:, 1], ALU.add).then_inc(s_chosen, 1)
                    dve.wait_ge(s_es, u)
                    nc.vector.tensor_scalar(gate[:], gate[:], 1.0, None, ALU.add).then_inc(s_es1, 1)
                    dve.wait_ge(s_es1, u)
                    nc.vector.reciprocal(gate[:], gate[:]).then_inc(s_gate, 1)

                    def product(q):
                        n = it * UF + q
                        dve.wait_ge(s_silu, n + 1)
                        nc.vector.tensor_tensor(hid[:, q // KF, q % KF], ps[:, q % 2, 1], act_f[:, q % 2],
                                                ALU.mult).then_inc(s_hid, 1)

                    def output(b):
                        dve.wait_ge(s_out, it * NB + b + 1)
                        if b:
                            dve.wait_ge(s_x, it * NB + b)
                        nc.vector.tensor_tensor(og[:], pso[:], keep["gates"][:, 0, 1, b:b + 1].broadcast_to([P, TB, D]),
                                                ALU.mult).then_inc(s_og, 1)

                    product(0)
                    product(1)
                    dve.wait_ge(s_rank, u)
                    dve.wait_ge(s_run, u)
                    nc.vector.tensor_tensor(place[:, 0], psr[:, 0:TI * EXP].rearrange("p (t e) -> p t e", e=EXP),
                                            run[:].unsqueeze(1).broadcast_to([P, TI, EXP]), ALU.add).then_inc(s_place, 1)
                    dve.wait_ge(s_place, u)
                    nc.vector.tensor_tensor(run[:], run[:], psr[:, TI * EXP:(TI + 1) * EXP], ALU.add).then_inc(s_run, 1)
                    product(2)
                    for c in (1, 0):
                        i = nc.vector.tensor_tensor(place[:, c], place[:, 0], pick[:, c], ALU.mult)
                        i.then_inc(s_placed, 1)
                        dve.wait_ge(s_placed, 2 * it + 2 - c)
                    for c in range(2):
                        i = nc.vector.tensor_reduce(rowf[:, :, c:c + 1], place[:, c], AX_X, ALU.add)
                    i.then_inc(s_rowf, 1)
                    product(3)
                    dve.wait_ge(s_rowf, u)
                    nc.vector.tensor_copy(rowu[:], rowf[:]).then_inc(s_rowu, 1)
                    nc.vector.tensor_copy(rows[:, bass.ds(it, 1)], rowf[:].unsqueeze(1)).then_inc(s_row, 1)
                    dve.wait_ge(s_gate, u)
                    dve.wait_ge(s_h, it * NB + NB)
                    for n in range(TI):
                        for c in range(2):
                            i = nc.vector.tensor_scalar(gated[:, n, c], norm.xn[:, n // TB, n % TB], gate[:, n, c:c + 1],
                                                        None, ALU.mult)
                        if n % 2:
                            if n == TI - 1:
                                i.then_inc(s_gated, 1)
                            product(KF + n // 2)
                        if n == 3:
                            output(0)
                    output(1)
                    dve.wait_ge(s_x, it * NB + NB)
                    dve.wait_ge(s_sorted, it * ROUTED * 16 + ROUTED * 16)
                dve.wait_ge(s_run, NBLK + 1)
                nc.vector.tensor_scalar(padf[:], run[:], iota[:, 0:1], None, ALU.add).then_inc(s_pad, 1)
                dve.wait_ge(s_pad, 1)
                nc.vector.tensor_copy(padu[:], padf[:]).then_inc(s_pad, 1)
                n = [0]

                def one(instruction):
                    n[0] += 1
                    instruction.then_inc(s_table, 1)
                    dve.wait_ge(s_table, n[0])

                one(nc.vector.tensor_tensor(count[:], run[:], region[:], ALU.subtract))
                shape = [P, EXP, SEQ * NB // P]
                one(nc.vector.tensor_tensor(over[:], count[:].unsqueeze(2).broadcast_to(shape),
                                            steps[:].unsqueeze(1).broadcast_to(shape), ALU.is_gt))
                one(nc.vector.tensor_reduce(blocks[:], over[:], AX_X, ALU.add))
                one(nc.vector.tensor_tensor_scan(end[:], keep["one"][:].broadcast_to([P, EXP]), blocks[:], 0.0,
                                                 ALU.mult, ALU.add))
                shape = [1, XBLOCKS, EXP]
                one(nc.vector.tensor_tensor(past[:, 0], block_no[:].unsqueeze(2).broadcast_to(shape),
                                            end[0:1].unsqueeze(1).broadcast_to(shape), ALU.is_ge))
                one(nc.vector.tensor_tensor(past[:, 1], past[:, 0], blocks[0:1].unsqueeze(1).broadcast_to(shape), ALU.mult))
                one(nc.vector.tensor_reduce(bexp[:], past[:, 0], AX_X, ALU.add))
                one(nc.vector.tensor_reduce(brow[:, 0], past[:, 1], AX_X, ALU.add))
                one(nc.vector.tensor_tensor(brow[:, 1], block_no[:], brow[:, 0], ALU.subtract))
                one(nc.vector.tensor_scalar(brow[:, 0], brow[:, 1], float(P), None, ALU.mult))
                one(nc.vector.scalar_tensor_tensor(out=brow[:, 1], in0=bexp[:], scalar=float(REGION), in1=brow[:, 0],
                                                   op0=ALU.mult, op1=ALU.add))
                one(nc.vector.tensor_copy(t["block_expert"][:], bexp[:]))
                one(nc.vector.tensor_copy(t["block_row"][:], brow[:, 1]))
                one(nc.vector.tensor_tensor(shift[:, 0], end[:], blocks[:], ALU.subtract))
                one(nc.vector.scalar_tensor_tensor(out=shift[:, 1], in0=shift[:, 0], scalar=-float(P), in1=region[:],
                                                   op0=ALU.mult, op1=ALU.add))
                one(nc.vector.tensor_copy(shift[:, 2, 0:1], shift[:, 1, 0:1]))
                one(nc.vector.tensor_tensor(shift[:, 2, 1:EXP], shift[:, 1, 1:EXP], shift[:, 1, 0:EXP - 1], ALU.subtract))
                dve.wait_ge(s_row, NBLK)
                shape = [P, NBLK * TI * 2, EXP]
                flat = rows[:].rearrange("p i n c -> p (i n c)")
                one(nc.vector.tensor_tensor(above[:, 0], flat.unsqueeze(2).broadcast_to(shape),
                                            region[:].unsqueeze(1).broadcast_to(shape), ALU.is_ge))
                one(nc.vector.tensor_tensor(above[:, 1], above[:, 0], shift[:, 2].unsqueeze(1).broadcast_to(shape), ALU.mult))
                one(nc.vector.tensor_reduce(moved[:], above[:, 1], AX_X, ALU.add))
                one(nc.vector.tensor_tensor(moved[:], flat, moved[:], ALU.subtract))
                one(nc.vector.tensor_copy(t["row"][:].rearrange("p i n c -> p (i n c)"), moved[:]))

            @block.tensor
            def _(pe):
                pe.wait_ge(s_w, 16 * 9)
                pe.wait_ge(s_ones, 1)
                pe.wait_ge(s_b, 16)
                with pe.Fori(0, NBLK) as it:
                    norm.transpose(pe, it, lambda b, k: ps[:, b, k])
                    for b in range(NB):
                        pe.wait_ge(norm.s_hT, it * NB + b + 1)
                        for n in range(TB):
                            at = (b * TB + n) * EXP
                            for k in range(KD):
                                i = nc.tensor.matmul(psg[:, at:at + EXP], hT[:, b, k, n * P:(n + 1) * P],
                                                     router[:, k], start=(k == 0), stop=(k == KD - 1))
                    i.then_inc(s_score, 1)

                    def up(q):
                        n, b, f = it * UF + q, q // KF, q % KF
                        if q >= 2:
                            pe.wait_ge(s_hid, n - 1)
                        for j, wt in enumerate((w_in, w_sw)):
                            for k in range(KD):
                                i = nc.tensor.matmul(ps[:, q % 2, j], wt[:, EXP, k, f * P:(f + 1) * P], hT[:, b, k],
                                                     start=(k == 0), stop=(k == KD - 1))
                        i.then_inc(s_pair, 1)

                    def ranks():
                        pe.wait_ge(s_chosen, it + 1)
                        nc.tensor.matmul(psr[:, 0:TI * EXP], before[:], chosen[:].rearrange("p t e -> p (t e)"),
                                         start=True, stop=False, skip_group_check=True)
                        for n in range(TI - 1):
                            nc.tensor.matmul(psr[:, (n + 1) * EXP:TI * EXP].rearrange("p (t e) -> p t e", e=EXP), ones[:],
                                             chosen[:, n:n + 1].broadcast_to([P, TI - 1 - n, EXP]), start=False,
                                             stop=False, skip_group_check=True)
                        for n in range(TI):
                            i = nc.tensor.matmul(psr[:, TI * EXP:(TI + 1) * EXP], ones[:], chosen[:, n], start=False,
                                                 stop=(n == TI - 1), skip_group_check=True)
                        i.then_inc(s_rank, 1)

                    def down(b):
                        pe.wait_ge(s_hid, it * UF + (b + 1) * KF)
                        if b:
                            pe.wait_ge(s_og, it * NB + b)
                        for f in range(KF):
                            for n in range(TB):
                                i = nc.tensor.matmul(pso[:, n], hid[:, b, f, n * P:(n + 1) * P], w_out[:, f],
                                                     start=(f == 0 and n % 2 == 0), stop=(f == KF - 1 and n % 2 == 1),
                                                     skip_group_check=True)
                        i.then_inc(s_out, 1)

                    for q in range(UF):
                        up(q)
                        if q == 1:
                            ranks()
                        if q == KF + 1:
                            down(0)
                    down(1)
                    pe.wait_ge(s_og, it * NB + NB)
        m.clear()


def run_experts(nc, a, keep, t):
    w_in, w_sw, ident = t["w_in"], t["w_sw"], keep["ident"]
    FIRST, UNROLL = 5, 4
    with ExitStack() as ctx:
        m = Pool(nc, ctx, "exp")
        w_out = m.sb("w_out", [P, EXP + 1, KF, D])
        rows = m.sb("rows", [P, UNROLL, D])
        xT = m.sb("xT", [P, 2, KD, P])
        act_f = m.sb("act_f", [P, 2, FF])
        hid = m.sb("hid", [P, 2, FF])
        hidT = m.sb("hidT", [P, 2, FF])
        res = m.sb("res", [P, UNROLL, D])
        psx = m.ps("psx", [P, 512])
        ps = m.ps("ps", [P, 2, 2, FF])
        psh = m.ps("psh", [P, FF])
        pso = m.ps("pso", [P, 512])
        s_turned, s_xT, s_mid, s_sw, s_silu, s_hid, s_hturned, s_hidT, s_out, s_res = (
            m.sem(n) for n in "turned xT mid sw silu hid hturned hidT out res".split())
        s_wo = m.sem("w_out_in")
        s_in = [m.sem(f"rows_in{n}") for n in range(UNROLL)]
        s_st = [m.sem(f"stored{n}") for n in range(UNROLL)]

        def pipeline(eng, step):
            for n in range(1, FIRST):
                step(0, n)
            rounds = (XBLOCKS - FIRST) // UNROLL
            with eng.Fori(0, rounds) as r:
                for k in range(UNROLL):
                    step(r * UNROLL, FIRST + k)
            for n in range(FIRST + rounds * UNROLL, XBLOCKS):
                step(0, n)

        with nc.Block() as block:
            @block.sync
            def _(sp):
                def load(base, k):
                    row = sp.value_load(t["block_row"][0:1, bass.ds(base + k, 1)], min_val=0, max_val=LAST_ROW)
                    sp.dma_start(rows[:, k % UNROLL], t["sorted"][bass.ds(row, P)]).then_inc(s_in[k % UNROLL], 16)

                def store(base, k):
                    sp.dma_start(t["results"][bass.ds((base + k) * P, P)], res[:, k % UNROLL]).then_inc(s_st[k % UNROLL], 16)

                for n in range(UNROLL):
                    load(0, n)
                for e in range(EXP + 1):
                    src = a["L0_ffn_w_out_eFD"][e] if e < EXP else a["shared_out"]
                    sp.dma_start(w_out[:, e], src.rearrange("(k p) d -> p k d", p=P)).then_inc(s_wo, 16)

                def step(base, k):
                    if not (isinstance(base, int) and k + 3 >= XBLOCKS):
                        sp.wait_ge(s_turned, base + k)
                        load(base, k + 3)
                    if k >= 2:
                        sp.wait_ge(s_res, base + k - 1)
                        store(base, k - 2)

                pipeline(sp, step)
                for n in (XBLOCKS - 2, XBLOCKS - 1):
                    sp.wait_ge(s_res, n + 1)
                    store(0, n)
                for n in range(UNROLL):
                    sp.wait_ge(s_st[n], 16 * (XBLOCKS // UNROLL))

            @block.scalar
            def _(act):
                def rows_in(base, k):
                    act.wait_ge(s_turned, base + k + 1)
                    nc.scalar.copy(xT[:, k % 2].rearrange("p k n -> p (k n)"), psx[:, 0:D]).then_inc(s_xT, 1)

                def silu(base, k):
                    act.wait_ge(s_mid, base + k + 1)
                    nc.scalar.activation(act_f[:, k % 2], ps[:, k % 2, 0], ACT.Silu).then_inc(s_silu, 1)

                def hidden(base, k):
                    act.wait_ge(s_hturned, base + k + 1)
                    nc.scalar.copy(hidT[:, k % 2], psh[:]).then_inc(s_hidT, 1)

                rows_in(0, 0)
                rows_in(0, 1)
                silu(0, 0)

                def step(base, k):
                    hidden(base, k - 1)
                    if not (isinstance(base, int) and k + 1 >= XBLOCKS):
                        rows_in(base, k + 1)
                    silu(base, k)

                pipeline(act, step)
                hidden(0, XBLOCKS - 1)

            @block.vector
            def _(dve):
                def product(base, k):
                    dve.wait_ge(s_silu, base + k + 1)
                    dve.wait_ge(s_sw, base + k + 1)
                    nc.vector.tensor_tensor(hid[:, k % 2], ps[:, k % 2, 1], act_f[:, k % 2], ALU.mult).then_inc(s_hid, 1)

                def result(base, k):
                    dve.wait_ge(s_out, base + k + 1)
                    if k >= UNROLL:
                        dve.wait_ge(s_st[k % UNROLL], base * (16 // UNROLL) + k // UNROLL * 16)
                    nc.vector.tensor_copy(res[:, k % UNROLL], pso[:, 0:D]).then_inc(s_res, 1)

                product(0, 0)

                def step(base, k):
                    product(base, k)
                    result(base, k - 1)

                pipeline(dve, step)
                result(0, XBLOCKS - 1)

            @block.tensor
            def _(pe):
                def turn(base, k):
                    pe.wait_ge(s_in[k % UNROLL], base * (16 // UNROLL) + k // UNROLL * 16 + 16)
                    if k:
                        pe.wait_ge(s_xT, base + k)
                    for c in range(KD):
                        i = nc.tensor.transpose(psx[:, c * P:(c + 1) * P], rows[:, k % UNROLL, c * P:(c + 1) * P], ident[:])
                    i.then_inc(s_turned, 1)

                def up(base, k):
                    e = pe.value_load(t["block_expert"][0:1, bass.ds(base + k, 1)], min_val=0, max_val=EXP)
                    pe.wait_ge(s_xT, base + k + 1)
                    for j, (wt, done) in enumerate(((w_in, s_mid), (w_sw, s_sw))):
                        for c in range(KD):
                            i = nc.tensor.matmul(ps[:, k % 2, j], xT[:, k % 2, c],
                                                 wt[:, bass.ds(e, 1), c].rearrange("p a f -> p (a f)"),
                                                 start=(c == 0), stop=(c == KD - 1))
                        i.then_inc(done, 1)

                def turn_hidden(base, k):
                    pe.wait_ge(s_hid, base + k + 1)
                    for f in range(KF):
                        i = nc.tensor.transpose(psh[:, f * P:(f + 1) * P], hid[:, k % 2, f * P:(f + 1) * P], ident[:])
                    i.then_inc(s_hturned, 1)

                def down(base, k):
                    e = pe.value_load(t["block_expert"][0:1, bass.ds(base + k, 1)], min_val=0, max_val=EXP)
                    pe.wait_ge(s_hidT, base + k + 1)
                    if k:
                        pe.wait_ge(s_res, base + k)
                    else:
                        pe.wait_ge(s_wo, 16 * (EXP + 1))
                    for f in range(KF):
                        i = nc.tensor.matmul(pso[:, 0:D], hidT[:, k % 2, f * P:(f + 1) * P],
                                             w_out[:, bass.ds(e, 1), f].rearrange("p a f -> p (a f)"),
                                             start=(f == 0), stop=(f == KF - 1))
                    i.then_inc(s_out, 1)

                pe.wait_ge(t["w_here"], 16 * 2 * EXP)
                turn(0, 0)
                turn(0, 1)
                up(0, 0)

                def step(base, k):
                    turn_hidden(base, k - 1)
                    if not (isinstance(base, int) and k + 1 >= XBLOCKS):
                        turn(base, k + 1)
                    up(base, k)
                    down(base, k - 1)

                pipeline(pe, step)
                turn_hidden(0, XBLOCKS - 1)
                down(0, XBLOCKS - 1)
        m.clear()


def collect_experts(nc, a, keep, t):
    x = keep["x"]
    TI = NB * TB
    with ExitStack() as ctx:
        m = Pool(nc, ctx, "col")
        rowu = m.sb("rowu", [P, 2, TI, 2], U32)
        got = m.sb("got", [P, 2, TI, 2, D])
        total = m.sb("total", [P, TI, D])
        s_row, s_sum, s_gated, s_x = (m.sem(n) for n in "row sum gated xadd".split())
        s_got = [t["soft"][f"got{n}"] for n in range(2)]
        with nc.Block() as block:
            @block.gpsimd
            def _(pool):
                for it in range(NBLK):
                    pool.wait_ge(s_row, it + 1)
                    if it >= 2:
                        pool.wait_ge(s_sum, it - 1)
                    for n in range(TI):
                        for c in range(2):
                            pool.indirect_dma_start(got[:, it % 2, n, c], None, t["results"],
                                                    bass.IndirectOffsetOnAxis(ap=rowu[:, it % 2, n, c:c + 1], axis=0)
                                                    ).then_inc(s_got[it % 2], 16)

            @block.vector
            def _(dve):
                def number(it):
                    nc.vector.tensor_copy(rowu[:, it % 2], t["row"][:, it]).then_inc(s_row, 1)

                number(0)
                number(1)
                for it in range(NBLK):
                    dve.wait_ge(s_got[it % 2], (it // 2 + 1) * TI * 2 * 16)
                    if it + 2 < NBLK:
                        number(it + 2)
                    nc.vector.tensor_tensor(total[:], got[:, it % 2, :, 0], got[:, it % 2, :, 1], ALU.add).then_inc(s_sum, 1)
                    dve.wait_ge(s_sum, it + 1)
                    for b in range(NB):
                        part = total[:, b * TB:(b + 1) * TB]
                        i = nc.vector.tensor_tensor(part, part, keep["gates"][:, 0, 1, b:b + 1].broadcast_to([P, TB, D]),
                                                    ALU.mult)
                    i.then_inc(s_gated, 1)
                    dve.wait_ge(s_gated, it + 1)
                    for b in range(NB):
                        xt = x[:, it * TB + b * TPB:it * TB + b * TPB + TB]
                        i = nc.vector.tensor_tensor(xt, xt, total[:, b * TB:(b + 1) * TB], ALU.add)
                    i.then_inc(s_x, 1)
                    dve.wait_ge(s_x, it + 1)
        m.clear()


def windowed_attention(nc, a, keep):
    x, modf, ident = keep["x"], keep["modf"], keep["ident"]
    with ExitStack() as outer:
        mo = Pool(nc, outer, "att")
        qT = mo.sb("qT", [P, KD, NT * P])
        kT = mo.sb("kT", [P, KD, (NT + 2) * P])
        v = mo.sb("v", [P, NT + 2, AKV * AHD])

        with ExitStack() as ctx:
            m = Pool(nc, ctx, "qkv")
            norm = BlockNorm(m, keep, lambda b, t, it: [x[:, bass.ds(it * TB + b * TPB + t, 1)]],
                             lambda b, k: modf[:, 1, SCALE_A, NB * k + b:NB * k + b + 1],
                             lambda b, k: modf[:, 1, SHIFT_A, NB * k + b:NB * k + b + 1])
            hT = norm.hT
            wq = m.sb("wq", [P, KD, D])
            wk = m.sb("wk", [P, KD, D])
            wv = m.sb("wv", [P, KD, AKV * AHD])
            ps = m.ps("ps", [P, 2 * KD, BLK])
            psv = m.ps("psv", [P, NB, BLK])
            s_w, s_q, s_k, s_v, s_qc, s_kc, s_vc, s_pad = (
                m.sem(n) for n in ("w_in", "q", "k", "v", "qcp", "kcp", "vcp", "pad"))
            with nc.Block() as block:
                @block.sync
                def _(sp):
                    for dst, name in ((wq, "att_wq"), (wk, "att_wk"), (wv, "att_wv")):
                        sp.dma_start(dst[:], a[name].rearrange("(k p) n -> p k n", p=P)).then_inc(s_w, 16)

                @block.gpsimd
                def _(pool):
                    for t in (0, NT + 1):
                        nc.gpsimd.memset(kT[:, :, t * P:(t + 1) * P], 0.0).then_inc(s_pad, 1)
                        nc.gpsimd.memset(v[:, t], 0.0).then_inc(s_pad, 1)
                    pool.wait_ge(s_pad, 4)

                @block.scalar
                def _(act):
                    with act.Fori(0, NBLK) as it:
                        nc.scalar.preload_act_table_set(LN_SET)
                        norm.inverse_deviation(act, it)
                        norm.affine(act, it, lambda b, k: ps[:, 2 * b + k])
                        for b in range(NB):
                            act.wait_ge(s_q, it * NB + b + 1)
                            nc.scalar.copy(qT[:, :, bass.ds(it * BLK + b * SEQ, BLK)], ps[:, 0:KD]).then_inc(s_qc, 1)

                @block.vector
                def _(dve):
                    with dve.Fori(0, NBLK) as it:
                        norm.normalise(dve, it)
                        for b in range(NB):
                            dve.wait_ge(s_k, it * NB + b + 1)
                            nc.vector.tensor_copy(kT[:, :, bass.ds(it * BLK + b * SEQ + P, BLK)],
                                                  ps[:, KD:2 * KD]).then_inc(s_kc, 1)
                            dve.wait_ge(s_v, it * NB + b + 1)
                            nc.vector.tensor_copy(v[:, bass.ds(it * TB + b * TPB + 1, TB)],
                                                  psv[:, b, 0:TB * AKV * AHD].rearrange("p (t d) -> p t d", t=TB)
                                                  ).then_inc(s_vc, 1)

                @block.tensor
                def _(pe):
                    pe.wait_ge(s_w, 48)
                    with pe.Fori(0, NBLK) as it:
                        norm.transpose(pe, it, lambda b, k: ps[:, 2 * b + k])
                        pe.wait_ge(norm.s_hT, it * NB + NB)
                        for b in range(NB):
                            for w, copied, done, at in ((wq, s_qc, s_q, 0), (wk, s_kc, s_k, KD)):
                                if b:
                                    pe.wait_ge(copied, it * NB + b)
                                for c in range(KD):
                                    for k in range(KD):
                                        i = nc.tensor.matmul(ps[:, at + c], w[:, k, c * P:(c + 1) * P], hT[:, b, k],
                                                             start=(k == 0), stop=(k == KD - 1))
                                i.then_inc(done, 1)
                            for t in range(TB):
                                for k in range(KD):
                                    i = nc.tensor.matmul(psv[:, b, t * AKV * AHD:(t + 1) * AKV * AHD],
                                                         hT[:, b, k, t * P:(t + 1) * P], wv[:, k],
                                                         start=(k == 0), stop=(k == KD - 1))
                            i.then_inc(s_v, 1)
                        pe.wait_ge(s_qc, it * NB + NB)
                        pe.wait_ge(s_kc, it * NB + NB)
                        pe.wait_ge(s_vc, it * NB + NB)

        m = Pool(nc, outer, "win")
        wo = m.sb("wo", [P, KD, D])
        mask = m.sb("mask", [P, TPB, AW], BF16)
        identb = m.sb("identb", [P, P], BF16)
        headmask = m.sb("headmask", [P, HPC])
        qm = m.sb("qm", [P, NB, AH, P])
        top = m.sb("top", [P, 3, HPR])
        nb = m.sb("nb", [P, 3, HPR])
        rs = m.sb("rs", [P, NB, AH])
        ri = m.sb("ri", [P, NB, AH])
        pr = m.sb("pr", [P, 3, HPR, AW])
        pT = m.sb("pT", [P, 3, HPR, AW])
        o = m.sb("o", [P, NB, D])
        oT = m.sb("oT", [P, NB, D])
        og = m.sb("og", [P, NB, D])
        psw = m.ps("psw", [P, 3, HPR, 512])
        pso = m.ps("pso", [P, NB, 512])
        (s_w, s_qm, s_s, s_top, s_nb, s_e, s_t, s_pT, s_pv, s_ri, s_o, s_oTp, s_oT, s_out, s_og, s_x) = (m.sem(n) for n in (
            "w_in", "qm", "scores", "top", "nb", "exp", "tp", "pT", "pv", "ri", "o", "oTp", "oT", "out", "og", "xadd"))
        s_m = keep["soft"].sem("mask_in")
        RU = AH // HPR
        RI = NB * RU
        SC = float(AHD) ** -0.5
        HEAD = 1

        with nc.Block() as block:
            @block.sync
            def _(sp):
                sp.dma_start(wo[:], a["att_wo"].rearrange("(k p) n -> p k n", p=P)).then_inc(s_w, 16)
                sp.dma_start(headmask[:], a["headmask"]).then_inc(s_w, 16)

            @block.gpsimd
            def _(pool):
                pool.dma_start(mask[:], a["win_mask"]).then_inc(s_m, 16)
                pool.dma_start(identb[:], a["ident"]).then_inc(s_m, 16)
                pool.wait_ge(s_w, 32)
                with pool.Fori(0, TPB) as it:
                    for b in range(NB):
                        for c in range(KD):
                            q = qT[:, c:c + 1, bass.ds(it * P + b * SEQ, P)]
                            i = nc.gpsimd.tensor_tensor(qm[:, b, c * HPC:(c + 1) * HPC], q.broadcast_to([P, HPC, P]),
                                                        headmask[:].unsqueeze(2).broadcast_to([P, HPC, P]), ALU.mult)
                        i.then_inc(s_qm, 1)
                    pool.wait_ge(s_s, it * RI + RI)

            @block.scalar
            def _(act):
                nc.scalar.preload_act_table_set(LN_SET)
                with act.Fori(0, TPB) as it:
                    for r in range(RI):
                        n, w, b = it * RI + r, r % 3, r // RU
                        act.wait_ge(s_nb, n + 1)
                        for h in range(HPR):
                            hh = r % RU * HPR + h
                            i = nc.scalar.activation(pr[:, w, h], psw[:, w, h, 0:AW], ACT.Exp, scale=SC,
                                                     bias=nb[:, w, h:h + 1], accum_out=rs[:, b, hh:hh + 1])
                        i.then_inc(s_e, 1)
                    for b in range(NB):
                        act.wait_ge(s_oTp, it * NB + b + 1)
                        nc.scalar.copy(oT[:, b], pso[:, b, 0:D]).then_inc(s_oT, 1)

            @block.vector
            def _(dve):
                dve.sem_inc(s_og, HEAD)
                with dve.Fori(0, TPB) as it:
                    def maxima(r):
                        n, w, b = it * RI + r, r % 3, r // RU
                        dve.wait_ge(s_s, n + 1)
                        nc.vector.tensor_reduce(top[:, w], psw[:, w, :, 0:AW], AX_X, ALU.max).then_inc(s_top, 1)
                        dve.wait_ge(s_top, n + 1)
                        nc.vector.tensor_scalar(nb[:, w], top[:, w], -SC, None, ALU.mult).then_inc(s_nb, 1)

                    def move(r):
                        n, w, b = it * RI + r, r % 3, r // RU
                        dve.wait_ge(s_t, n + 1)
                        if r >= 3:
                            dve.wait_ge(s_pv, n - 2)
                        nc.vector.tensor_copy(pT[:, w], psw[:, w, :, 0:AW]).then_inc(s_pT, 1)

                    def normalise(b):
                        u = it * NB + b
                        nc.vector.reciprocal(ri[:, b], rs[:, b]).then_inc(s_ri, 1)
                        dve.wait_ge(s_ri, u + 1)
                        dve.wait_ge(s_pv, it * RI + (b + 1) * RU)
                        nc.vector.tensor_tensor(o[:, b].rearrange("p (h d) -> p h d", h=AH),
                                                pso[:, b, 0:D].rearrange("p (h d) -> p h d", h=AH),
                                                ri[:, b].unsqueeze(2).broadcast_to([P, AH, AHD]), ALU.mult).then_inc(s_o, 1)

                    for r in range(RI + 1):
                        if r < RI:
                            maxima(r)
                        if r >= 1:
                            move(r - 1)
                        if r == RU + 2:
                            normalise(0)
                    normalise(1)
                    for b in range(NB):
                        u = it * NB + b
                        dve.wait_ge(s_out, u + 1)
                        nc.vector.tensor_tensor(og[:, b], pso[:, b, D:2 * D], keep["gates"][:, 1, 0, b],
                                                ALU.mult).then_inc(s_og, 1)
                    for b in range(NB):
                        dve.wait_ge(s_og, it * NB + b + 1 + HEAD)
                        xt = x[:, bass.ds(it + b * TPB, 1)]
                        nc.vector.tensor_tensor(xt, xt, og[:, b:b + 1], ALU.add).then_inc(s_x, 1)

            @block.tensor
            def _(pe):
                pe.wait_ge(s_w, 32)
                pe.wait_ge(s_m, 32)
                with pe.Fori(0, TPB) as it:
                    def scores(r):
                        n, w, b = it * RI + r, r % 3, r // RU
                        if r % RU == 0:
                            pe.wait_ge(s_qm, it * NB + b + 1)
                        if r >= 3:
                            pe.wait_ge(s_pT, n - 2)
                        for h in range(HPR):
                            hh = r % RU * HPR + h
                            c = hh // HPC
                            nc.tensor.matmul(psw[:, w, h, 0:AW], identb[:], mask[:, bass.ds(it, 1)], start=True, stop=False)
                            i = nc.tensor.matmul(psw[:, w, h, 0:AW], qm[:, b, hh], kT[:, c, bass.ds(it * P + b * SEQ, AW)],
                                                 start=False, stop=True)
                        i.then_inc(s_s, 1)

                    def turn(r):
                        n, w, b = it * RI + r, r % 3, r // RU
                        pe.wait_ge(s_e, n + 1)
                        for h in range(HPR):
                            for kb in range(3):
                                i = nc.tensor.transpose(psw[:, w, h, kb * P:(kb + 1) * P], pr[:, w, h, kb * P:(kb + 1) * P],
                                                        ident[:])
                        i.then_inc(s_t, 1)

                    def values(r):
                        n, w, b = it * RI + r, r % 3, r // RU
                        pe.wait_ge(s_pT, n + 1)
                        if r % RU == 0:
                            pe.wait_ge(s_og, it * NB + HEAD)
                        for h in range(HPR):
                            hh = r % RU * HPR + h
                            kv = hh // AG
                            for kb in range(3):
                                i = nc.tensor.matmul(pso[:, b, hh * AHD:(hh + 1) * AHD], pT[:, w, h, kb * P:(kb + 1) * P],
                                                     v[:, bass.ds(it + b * TPB + kb, 1), kv * AHD:(kv + 1) * AHD],
                                                     start=(hh == 0 and kb == 0), stop=(hh == AH - 1 and kb == 2),
                                                     skip_group_check=True)
                        i.then_inc(s_pv, 1)

                    def turn_out(b):
                        pe.wait_ge(s_o, it * NB + b + 1)
                        for c in range(KD):
                            i = nc.tensor.transpose(pso[:, b, c * P:(c + 1) * P], o[:, b, c * P:(c + 1) * P], ident[:])
                        i.then_inc(s_oTp, 1)

                    def project_out(b):
                        pe.wait_ge(s_oT, it * NB + b + 1)
                        for c in range(KD):
                            i = nc.tensor.matmul(pso[:, b, D:2 * D], oT[:, b, c * P:(c + 1) * P], wo[:, c],
                                                 start=(c == 0), stop=(c == KD - 1))
                        i.then_inc(s_out, 1)

                    for r in range(RI + 2):
                        if r < RI:
                            scores(r)
                        if 1 <= r <= RI:
                            turn(r - 1)
                        if r >= 2:
                            values(r - 2)
                    for b in range(NB):
                        turn_out(b)
                    for b in range(NB):
                        project_out(b)


def enter_local_stack(nc, a, keep, y, xs_a, spill):
    x = keep["x"]
    with ExitStack() as ctx:
        m = Pool(nc, ctx, "ent")
        norm = BlockNorm(m, keep, lambda b, t, it: [x[:, bass.ds(it * TB + b * TPB + t, 1)]], None, None)
        s_m, s_y, s_zero, s_xs, s_sp = m.sem("mult"), m.sem("y"), m.sem("zero"), m.sem("shifted"), m.sem("spilled")
        with nc.Block() as block:
            @block.sync
            def _(sp):
                sp.dma_start(spill.rearrange("(t p) d -> p t d", p=P), x[:]).then_inc(s_sp, 16)
                sp.wait_ge(s_zero, 1)
                with sp.Fori(0, NBLK) as it:
                    for b in range(NB):
                        sp.wait_ge(s_y, it * NB + b + 1)
                        shift_tokens(sp, y, xs_a, b, it * TB, TB, s_xs)
                sp.wait_ge(s_xs, NBLK * NB * 32)

            @block.scalar
            def _(act):
                nc.scalar.preload_act_table_set(LN_SET)
                with act.Fori(0, NBLK) as it:
                    norm.inverse_deviation(act, it)

            @block.vector
            def _(dve):
                nc.vector.memset(xs_a[0:1, :, 0], 0.0).then_inc(s_zero, 1)
                with dve.Fori(0, NBLK) as it:
                    norm.normalise(dve, it)
                    dve.wait_ge(s_y, it * NB + NB)

            @block.gpsimd
            def _(pool):
                pool.wait_ge(s_sp, 16)
                with pool.Fori(0, NBLK) as it:
                    for b in range(NB):
                        pool.wait_ge(norm.s_xn, it * NB + b + 1)
                        xn = norm.xn[:, b]
                        nc.gpsimd.tensor_tensor(xn, xn, keep["scale_row"][:, b:b + 1].broadcast_to([P, TB, D]),
                                                ALU.mult).then_inc(s_m, 1)
                        pool.wait_ge(s_m, it * NB + b + 1)
                        nc.gpsimd.tensor_tensor(y[:, bass.ds(it * TB + b * TPB, TB)], xn,
                                                keep["shift_row"][:, b:b + 1].broadcast_to([P, TB, D]),
                                                ALU.add).then_inc(s_y, 1)


def shift_tokens(eng, y, xs, b, tile, n, sem):
    src = y[:, bass.ds(tile + b * TPB, n), P:D]
    eng.dma_start(xs[1:P, b, bass.ds(tile, n)], src[0:P - 1]).then_inc(sem, 16)
    eng.dma_start(xs[0:1, b, bass.ds(tile + 1, n)], src[P - 1:P]).then_inc(sem, 16)


def local_attention(nc, a, keep, y, xs_a, xs_b, tabs, layer):
    ident = keep["ident"]
    cos, sin, mask, identb = tabs
    with ExitStack() as ctx:
        m = Pool(nc, ctx, "loc")
        w = m.sb("w", [P, KD, 3 * INNER])
        wo = m.sb("wo", [P, KI, D])
        scl = m.sb("scl", [P, 2, LHD])
        tc = m.sb("tc", [P, TPB, 2, LHD])
        ts = m.sb("ts", [P, TPB, 2, LHD])
        xst = m.sb("xst", [P, NB, D])
        hT = m.sb("hT", [P, NB, D])
        sq = m.sb("sq", [P, 2 * INNER])
        ss = m.sb("ss", [P, NB, 2 * LH])
        rn = m.sb("rn", [P, NB, 2 * LH])
        t1 = m.sb("t1", [P, NB, 2 * INNER])
        t2 = m.sb("t2", [P, NB, 2 * INNER])
        v = m.sb("v", [P, NB, 2, INNER])
        qT = m.sb("qT", [P, NB, KI, P])
        kT = m.sb("kT", [P, NB, KI, 2 * P])
        top = m.sb("top", [P, 2, 4])
        nb = m.sb("nb", [P, 2, 4])
        sc8 = m.sb("sc8", [P, NB, LH])
        rs = m.sb("rs", [P, NB, LH])
        ri = m.sb("ri", [P, NB, LH])
        pr = m.sb("pr", [P, 2, 4, 2 * P])
        pT = m.sb("pT", [P, 2, 8, P])
        o = m.sb("o", [P, INNER])
        oT = m.sb("oT", [P, INNER])
        psa = m.ps("psa", [P, 3, 512])
        psw = m.ps("psw", [P, 2, 2, 512])
        pso = m.ps("pso", [P, 512])
        names = ("w_in tab stage hTp hT qk vproj sq vcp ss ssm lnss rn sc8 t1 t2 rope krope ksc vprev kprev qkTp qT kT scores top "
                 "nb exp tp pTa pTb pv ri o oTp oT out y shifted")
        (s_w, s_tab, s_stage, s_hTp, s_hT, s_qk, s_v, s_sq, s_vcp, s_ss, s_ssm, s_lnss, s_rn, s_sc8, s_t1, s_t2,
         s_rope, s_krope, s_ksc, s_vprev, s_kprev, s_qkTp, s_qT, s_kT, s_s, s_top, s_nb, s_e, s_tp, s_pTa, s_pTb, s_pv, s_ri,
         s_o, s_oTp, s_oT, s_out, s_y, s_xs) = (m.sem(n) for n in names.split())
        L = layer

        def tile_of(j, b, ahead):
            jj, bb = j + (b + ahead) // NB, (b + ahead) % NB
            return jj, bb, L * (TPB * NB) + jj * NB + bb

        def pipeline(eng, step):
            with eng.Fori(0, TPB - 1) as j:
                for b in range(NB):
                    step(j, b, True, True)
            step(TPB - 1, 0, True, False)
            step(TPB - 1, 1, False, False)

        def heads(t):
            return t.rearrange("p (j h d) -> p j h d", j=2, h=LH)

        with nc.Block() as block:
            @block.sync
            def _(sp):
                sp.dma_start(w[:], a["wqkv"][bass.ds(L, 1)].rearrange("a (k p) n -> p (a k) n", p=P)).then_inc(s_w, 16)
                sp.dma_start(wo[:], a["loc_wo"][bass.ds(L, 1)].rearrange("a (k p) n -> p (a k) n", p=P)).then_inc(s_w, 16)
                sp.dma_start(scl[:], a["qk_scale"][bass.ds(L, 1)].broadcast_to([P, 2, LHD])).then_inc(s_w, 16)
                with sp.Fori(0, TPB) as j:
                    for b in range(NB):
                        u = L * (TPB * NB) + j * NB + b
                        sp.wait_ge(s_y, u + 2 + L)
                        shift_tokens(sp, y, xs_b, b, j, 1, s_xs)

            @block.gpsimd
            def _(pool):
                def copy(dst, src):
                    one = keep["one"][:]
                    for _ in range(len(src.shape) - 2):
                        one = one.unsqueeze(1)
                    return nc.gpsimd.tensor_tensor(dst, src, one.broadcast_to(list(src.shape)), ALU.mult)

                def stage(j, b):
                    copy(xst[:, b, 0:P].unsqueeze(1), y[:, bass.ds(j + b * TPB, 1), 0:P])
                    copy(xst[:, b, P:D].unsqueeze(1), xs_a[:, b, bass.ds(j, 1)]).then_inc(s_stage, 1)

                def rotate(b, u):
                    pool.wait_ge(s_t2, u + 1)
                    qq = t1[:, b, 0:INNER]
                    nc.gpsimd.tensor_tensor(qq, qq, t2[:, b, 0:INNER], ALU.add).then_inc(s_rope, 1)
                    pool.wait_ge(s_krope, u + 1)
                    pool.wait_ge(s_rn, u + 1)
                    kk = t1[:, b, INNER:].rearrange("p (h d) -> p h d", h=LH)
                    nc.gpsimd.tensor_tensor(kk, kk, rn[:, b, LH:].unsqueeze(2).broadcast_to([P, LH, LHD]),
                                            ALU.mult).then_inc(s_ksc, 1)

                for b in range(NB):
                    stage(0, b)
                    nc.gpsimd.memset(v[:, b, 0], 0.0).then_inc(s_vprev, 1)
                    nc.gpsimd.memset(kT[:, b, :, 0:P], 0.0).then_inc(s_kprev, 1)
                pool.wait_ge(s_w, (L + 1) * 48)
                nc.gpsimd.tensor_tensor(tc[:], cos[:], scl[:].unsqueeze(1).broadcast_to([P, TPB, 2, LHD]),
                                        ALU.mult).then_inc(s_tab, 1)
                for half in range(2):
                    d, s = slice(half * 32, half * 32 + 32), slice(32 - half * 32, 64 - half * 32)
                    nc.gpsimd.tensor_tensor(ts[:, :, :, d], sin[:, :, :, d],
                                            scl[:, :, s].unsqueeze(1).broadcast_to([P, TPB, 2, 32]),
                                            ALU.mult).then_inc(s_tab, 1)
                rotate(0, L * (TPB * NB))

                def step(j, b, ahead1, ahead2):
                    _, _, u = tile_of(j, b, 0)
                    if ahead2:
                        j2, b2, u2 = tile_of(j, b, 2)
                        pool.wait_ge(s_hTp, u2)
                        stage(j2, b2)
                        pool.wait_ge(s_s, 2 * u + 2)
                        copy(kT[:, b, :, 0:P], kT[:, b, :, P:2 * P]).then_inc(s_kprev, 1)
                    if ahead1:
                        _, b1, u1 = tile_of(j, b, 1)
                        rotate(b1, u1)
                    if ahead2:
                        pool.wait_ge(s_pv, 2 * u + 2)
                        copy(v[:, b, 0], v[:, b, 1]).then_inc(s_vprev, 1)

                pipeline(pool, step)
                pool.wait_ge(s_xs, (L + 1) * (TPB * NB * 32))

            @block.scalar
            def _(act):
                def copy_input(b, u):
                    act.wait_ge(s_hTp, u + 1)
                    nc.scalar.copy(hT[:, b], psa[:, 2, 0:D]).then_inc(s_hT, 1)

                def squares(b, u):
                    act.wait_ge(s_qk, u + 1)
                    nc.scalar.activation(sq[:], psa[:, 0:2].rearrange("p a n -> p (a n)"), ACT.Square).then_inc(s_sq, 1)

                def copy_values(b, u):
                    act.wait_ge(s_v, u + 1)
                    act.wait_ge(s_vprev, u + 1)
                    nc.scalar.copy(v[:, b, 1], psa[:, 2]).then_inc(s_vcp, 1)

                def inverse_norms(b, u):
                    act.wait_ge(s_ssm, u + 1)
                    nc.scalar.activation(rn[:, b], ss[:, b], ACT.Ln, scale=SS_SCALE).then_inc(s_lnss, 1)
                    act.wait_ge(s_lnss, u + 1)
                    nc.scalar.activation(rn[:, b], rn[:, b], ACT.Exp, scale=-0.5,
                                         bias=keep["ss_log"][:, 0:1]).then_inc(s_rn, 1)

                def copy_queries(b, u):
                    act.wait_ge(s_qkTp, u + 1)
                    nc.scalar.copy(qT[:, b].rearrange("p k n -> p (k n)"), psa[:, 0]).then_inc(s_qT, 1)

                def exps(b, u, hf):
                    act.wait_ge(s_nb, 2 * u + hf + 1)
                    for h in range(4):
                        hh = hf * 4 + h % 2 * 2 + h // 2
                        i = nc.scalar.activation(pr[:, hf, h], psw[:, hf, h // 2, h % 2 * 256:h % 2 * 256 + 256], ACT.Exp,
                                                 scale=sc8[:, b, hh:hh + 1], bias=nb[:, hf, h:h + 1],
                                                 accum_out=rs[:, b, hh:hh + 1])
                    i.then_inc(s_e, 1)

                def move(b, u, hf):
                    act.wait_ge(s_tp, 2 * u + hf + 1)
                    nc.scalar.copy(pT[:, hf, 4:8].rearrange("p k n -> p (k n)"), psw[:, hf, 1]).then_inc(s_pTb, 1)

                nc.scalar.preload_act_table_set(LN_SET)
                first = L * (TPB * NB)
                copy_input(0, first)
                squares(0, first)
                copy_values(0, first)
                inverse_norms(0, first)
                copy_input(1, first + 1)
                copy_queries(0, first)

                def step(j, b, ahead1, ahead2):
                    _, _, u = tile_of(j, b, 0)
                    _, b1, u1 = tile_of(j, b, 1)
                    exps(b, u, 0)
                    exps(b, u, 1)
                    if ahead1:
                        squares(b1, u1)
                        copy_values(b1, u1)
                    move(b, u, 0)
                    move(b, u, 1)
                    if ahead1:
                        inverse_norms(b1, u1)
                    if ahead2:
                        _, b2, u2 = tile_of(j, b, 2)
                        copy_input(b2, u2)
                    act.wait_ge(s_oTp, u + 1)
                    nc.scalar.copy(oT[:], pso[:]).then_inc(s_oT, 1)
                    if ahead1:
                        copy_queries(b1, u1)

                pipeline(act, step)

            @block.vector
            def _(dve):
                def rotate_cos(j, b, u):
                    dve.wait_ge(s_sq, u + 1)
                    qk = heads(psa[:, 0:2].rearrange("p a n -> p (a n)"))
                    for q in range(2):
                        cosq = tc[:, bass.ds(j, 1), q].broadcast_to([P, LH, LHD])
                        i = nc.vector.tensor_tensor(heads(t1[:, b])[:, q], qk[:, q], cosq, ALU.mult)
                    i.then_inc(s_t1, 1)

                def rotate_sin(j, b, u):
                    qk = heads(psa[:, 0:2].rearrange("p a n -> p (a n)"))
                    for q in range(2):
                        for half in range(2):
                            d, s = slice(half * 32, half * 32 + 32), slice(32 - half * 32, 64 - half * 32)
                            i = nc.vector.tensor_tensor(heads(t2[:, b])[:, q, :, d], qk[:, q, :, s],
                                                        ts[:, bass.ds(j, 1), q, d].broadcast_to([P, LH, 32]), ALU.mult)
                    i.then_inc(s_t2, 1)
                    dve.wait_ge(s_t2, u + 1)
                    kk = t1[:, b, INNER:]
                    nc.vector.tensor_tensor(kk, kk, t2[:, b, INNER:], ALU.add).then_inc(s_krope, 1)

                def sum_squares(b, u):
                    nc.vector.tensor_reduce(ss[:, b], sq[:].rearrange("p (h d) -> p h d", d=LHD), AX_X,
                                            ALU.add).then_inc(s_ss, 1)
                    dve.wait_ge(s_ss, u + 1)
                    nc.vector.tensor_scalar(ss[:, b], ss[:, b], 1e-24, None, ALU.max).then_inc(s_ssm, 1)

                def query_scale(b, u):
                    dve.wait_ge(s_rn, u + 1)
                    nc.vector.tensor_scalar(sc8[:, b], rn[:, b, 0:LH], QK_SCALE, None, ALU.mult).then_inc(s_sc8, 1)

                def copy_keys(b, u):
                    dve.wait_ge(s_qkTp, u + 1)
                    dve.wait_ge(s_kprev, u + 1)
                    nc.vector.tensor_copy(kT[:, b, :, P:2 * P], psa[:, 1].rearrange("p (k n) -> p k n", k=KI)
                                          ).then_inc(s_kT, 1)

                def maxima(b, u, hf):
                    dve.wait_ge(s_s, 2 * u + hf + 1)
                    nc.vector.tensor_reduce(top[:, hf], psw[:, hf].rearrange("p a (h n) -> p (a h) n", h=2), AX_X,
                                            ALU.max).then_inc(s_top, 1)
                    dve.wait_ge(s_top, 2 * u + hf + 1)
                    dve.wait_ge(s_sc8, u + 1)
                    nc.vector.scalar_tensor_tensor(
                        out=nb[:, hf].rearrange("p (r s) -> p r s", r=2),
                        in0=top[:, hf].rearrange("p (r s) -> p r s", r=2), scalar=-1.0,
                        in1=sc8[:, b, hf * 4:hf * 4 + 4].rearrange("p (s r) -> p r s", r=2), op0=ALU.mult,
                        op1=ALU.mult).then_inc(s_nb, 1)

                def move(b, u, hf):
                    dve.wait_ge(s_tp, 2 * u + hf + 1)
                    nc.vector.tensor_copy(pT[:, hf, 0:4].rearrange("p k n -> p (k n)"), psw[:, hf, 0]).then_inc(s_pTa, 1)

                nc.vector.memset(xs_b[0:1, :, 0], 0.0).then_inc(s_y, 1)
                dve.wait_ge(s_tab, (L + 1) * 3)
                first = L * (TPB * NB)
                rotate_cos(0, 0, first)
                rotate_sin(0, 0, first)
                sum_squares(0, first)
                query_scale(0, first)
                copy_keys(0, first)

                def step(j, b, ahead1, ahead2):
                    _, _, u = tile_of(j, b, 0)
                    j1, b1, u1 = tile_of(j, b, 1)
                    maxima(b, u, 0)
                    maxima(b, u, 1)
                    if ahead1:
                        rotate_cos(j1, b1, u1)
                    move(b, u, 0)
                    move(b, u, 1)
                    if ahead1:
                        rotate_sin(j1, b1, u1)
                        sum_squares(b1, u1)
                    nc.vector.reciprocal(ri[:, b], rs[:, b]).then_inc(s_ri, 1)
                    dve.wait_ge(s_ri, u + 1)
                    dve.wait_ge(s_pv, 2 * u + 2)
                    nc.vector.tensor_tensor(o[:].rearrange("p (h d) -> p h d", h=LH),
                                            pso[:].rearrange("p (h d) -> p h d", h=LH),
                                            ri[:, b].unsqueeze(2).broadcast_to([P, LH, LHD]), ALU.mult).then_inc(s_o, 1)
                    if ahead1:
                        query_scale(b1, u1)
                        copy_keys(b1, u1)
                    dve.wait_ge(s_out, u + 1)
                    yt = y[:, bass.ds(j + b * TPB, 1)]
                    nc.vector.tensor_tensor(yt, pso[:, 0:D].unsqueeze(1), yt, ALU.add).then_inc(s_y, 1)

                pipeline(dve, step)

            @block.tensor
            def _(pe):
                def turn_input(b, u):
                    pe.wait_ge(s_stage, u + 1)
                    for k in range(KD):
                        i = nc.tensor.transpose(psa[:, 2, k * P:(k + 1) * P], xst[:, b, k * P:(k + 1) * P], ident[:])
                    i.then_inc(s_hTp, 1)

                def project(b, u):
                    pe.wait_ge(s_hT, u + 1)
                    for c, done in ((0, None), (1, s_qk), (2, s_v)):
                        for k in range(KD):
                            i = nc.tensor.matmul(psa[:, c], hT[:, b, k * P:(k + 1) * P], w[:, k, c * 512:(c + 1) * 512],
                                                 start=(k == 0), stop=(k == KD - 1))
                        if done is not None:
                            i.then_inc(done, 1)

                def turn_queries_keys(b, u):
                    for q, turned in enumerate((s_rope, s_ksc)):
                        pe.wait_ge(turned, u + 1)
                        for c in range(KI):
                            i = nc.tensor.transpose(psa[:, q, c * P:(c + 1) * P],
                                                    t1[:, b, q * INNER + c * P:q * INNER + (c + 1) * P], ident[:])
                    i.then_inc(s_qkTp, 1)

                def scores(j, b, u, hf):
                    if hf == 0:
                        pe.wait_ge(s_qT, u + 1)
                        pe.wait_ge(s_kT, u + 1)
                    for i2 in range(2):
                        out = psw[:, hf, i2].rearrange("p (h w n) -> p h w n", h=2, w=2)
                        nc.tensor.matmul(out[:, :, 0], identb[:], mask[:, bass.ds(j, 1), 0:P].broadcast_to([P, 2, P]),
                                         start=True, stop=False, skip_group_check=True)
                        nc.tensor.matmul(out[:, :, 1], identb[:], mask[:, 0:1, P:2 * P].broadcast_to([P, 2, P]),
                                         start=False, stop=False, skip_group_check=True)
                    for h in range(2):
                        for i2 in range(2):
                            hh, r = hf * 4 + h * 2 + i2, i2 * LHD
                            i = nc.tensor.matmul(psw[:, hf, i2, h * 256:(h + 1) * 256], qT[r:r + LHD, b, hh // 2],
                                                 kT[r:r + LHD, b, hh // 2], start=False, stop=(h == 1),
                                                 skip_group_check=True)
                    i.then_inc(s_s, 1)

                def turn(b, u, hf):
                    pe.wait_ge(s_e, 2 * u + hf + 1)
                    for h in range(4):
                        for kb in range(2):
                            i = nc.tensor.transpose(psw[:, hf, h // 2, (h % 2 * 2 + kb) * P:(h % 2 * 2 + kb + 1) * P],
                                                    pr[:, hf, h, kb * P:(kb + 1) * P], ident[:])
                    i.then_inc(s_tp, 1)

                def values(b, u, hf):
                    if hf == 0:
                        pe.wait_ge(s_y, u + 1 + L)
                        pe.wait_ge(s_vcp, u + 1)
                    pe.wait_ge(s_pTa, 2 * u + hf + 1)
                    pe.wait_ge(s_pTb, 2 * u + hf + 1)
                    for h in range(4):
                        hh = hf * 4 + h % 2 * 2 + h // 2
                        for kb in range(2):
                            i = nc.tensor.matmul(pso[:, hh * LHD:(hh + 1) * LHD], pT[:, hf, h * 2 + kb],
                                                 v[:, b, kb, hh * LHD:(hh + 1) * LHD], start=(hh == 0 and kb == 0),
                                                 stop=(hh == LH - 1 and kb == 1), skip_group_check=True)
                    i.then_inc(s_pv, 1)

                first = L * (TPB * NB)
                turn_input(0, first)
                pe.wait_ge(s_w, (L + 1) * 48)
                project(0, first)
                pe.wait_ge(s_vcp, first + 1)
                turn_input(1, first + 1)
                turn_queries_keys(0, first)

                def step(j, b, ahead1, ahead2):
                    _, _, u = tile_of(j, b, 0)
                    _, b1, u1 = tile_of(j, b, 1)
                    scores(j, b, u, 0)
                    scores(j, b, u, 1)
                    if ahead1:
                        project(b1, u1)
                    turn(b, u, 0)
                    turn(b, u, 1)
                    values(b, u, 0)
                    values(b, u, 1)
                    if ahead2:
                        _, b2, u2 = tile_of(j, b, 2)
                        pe.wait_ge(s_vcp, u1 + 1)
                        turn_input(b2, u2)
                    pe.wait_ge(s_o, u + 1)
                    for c in range(KI):
                        i = nc.tensor.transpose(pso[:, c * P:(c + 1) * P], o[:, c * P:(c + 1) * P], ident[:])
                    i.then_inc(s_oTp, 1)
                    if ahead1:
                        turn_queries_keys(b1, u1)
                    pe.wait_ge(s_oT, u + 1)
                    for c in range(KI):
                        i = nc.tensor.matmul(pso[:, 0:D], oT[:, c * P:(c + 1) * P], wo[:, c],
                                             start=(c == 0), stop=(c == KI - 1))
                    i.then_inc(s_out, 1)

                pipeline(pe, step)


def gated_mlp(nc, a, keep, y, xs_a, xs_b, layer):
    L = layer
    with ExitStack() as ctx:
        m = Pool(nc, ctx, "mlp")
        col = m.sb("col", [P, 2 * KD + 2 * KH])
        norm = BlockNorm(m, keep, lambda b, t, j: [y[:, bass.ds(j * TB + b * TPB + t, 1), 0:P],
                                                   xs_b[:, b, bass.ds(j * TB + t, 1)]],
                         lambda b, k: col[:, k:k + 1], lambda b, k: col[:, KD + k:KD + k + 1])
        hT = norm.hT
        w1 = m.sb("w1", [P, KD, 2 * HID])
        w2 = m.sb("w2", [P, KH, D])
        b2 = m.sb("b2", [P, 1, D])
        gl = m.sb("gl", [P, 2, BLK])
        hid = m.sb("hid", [P, 2, KH, BLK])
        ps = m.ps("ps", [P, 2, 2, BLK])
        pso = m.ps("pso", [P, TB, D])
        s_w, s_pair, s_gl, s_hid, s_out, s_yo, s_y, s_xs = (
            m.sem(n) for n in ("w_in", "pair", "gelu", "hid", "out", "yo", "y", "shifted"))
        UF = NB * KH

        with nc.Block() as block:
            @block.sync
            def _(sp):
                sp.dma_start(w1[:], a["w1"][bass.ds(L, 1)].rearrange("a (k p) n -> p (a k) n", p=P)).then_inc(s_w, 16)
                full = (KH - 1) * P
                sp.dma_start(w2[:, 0:KH - 1], a["w2"][bass.ds(L, 1), 0:full].rearrange("a (k p) n -> p (a k) n", p=P)
                             ).then_inc(s_w, 16)
                sp.dma_start(w2[0:HTAIL, KH - 1:KH], a["w2"][bass.ds(L, 1), full:HID].rearrange("a p n -> p a n")
                             ).then_inc(s_w, 16)
                sp.dma_start(b2[:], a["b2"][bass.ds(L, 1)].unsqueeze(0).broadcast_to([P, 1, D])).then_inc(s_w, 16)
                sp.dma_start(col[:], a["mlp_col"][bass.ds(L, 1)].rearrange("a p n -> p (a n)")).then_inc(s_w, 16)
                with sp.Fori(0, NBLK) as j:
                    it = L * NBLK + j
                    for b in range(NB):
                        sp.wait_ge(s_y, it * NB + b + 1)
                        shift_tokens(sp, y, xs_a, b, j * TB, TB, s_xs)

            @block.gpsimd
            def _(pool):
                with pool.Fori(0, NBLK) as j:
                    it = L * NBLK + j
                    pool.wait_ge(s_w, (L + 1) * 80)
                    for b in range(NB):
                        pool.wait_ge(s_yo, it * NB + b + 1)
                        yt = y[:, bass.ds(j * TB + b * TPB, TB)]
                        nc.gpsimd.tensor_tensor(yt, yt, b2[:].broadcast_to([P, TB, D]), ALU.add).then_inc(s_y, 1)
                pool.wait_ge(s_xs, (L + 1) * (NBLK * NB * 32))

            @block.scalar
            def _(act):
                with act.Fori(0, NBLK) as j:
                    it = L * NBLK + j
                    nc.scalar.preload_act_table_set(LN_SET)
                    act.wait_ge(s_w, (L + 1) * 80)
                    norm.inverse_deviation(act, it)
                    norm.affine(act, it, lambda b, k: ps[:, b, k])
                    for q in range(UF):
                        n, f = it * UF + q, q % KH
                        M = P if f < KH - 1 else HTAIL
                        act.wait_ge(s_pair, n + 1)
                        if q >= 2:
                            act.wait_ge(s_hid, n - 1)
                        c = 2 * KD + KH + f
                        nc.scalar.activation(gl[0:M, q % 2], ps[0:M, q % 2, 1], ACT.Gelu,
                                             bias=col[0:M, c:c + 1]).then_inc(s_gl, 1)

            @block.vector
            def _(dve):
                with dve.Fori(0, NBLK) as j:
                    it = L * NBLK + j
                    dve.wait_ge(s_w, (L + 1) * 80)
                    norm.normalise(dve, it, j)
                    for q in range(UF):
                        n, f, b = it * UF + q, q % KH, q // KH
                        M = P if f < KH - 1 else HTAIL
                        dve.wait_ge(s_gl, n + 1)
                        c = 2 * KD + f
                        nc.vector.scalar_tensor_tensor(out=hid[0:M, b, f], in0=ps[0:M, q % 2, 0], scalar=col[0:M, c:c + 1],
                                                       in1=gl[0:M, q % 2], op0=ALU.add, op1=ALU.mult).then_inc(s_hid, 1)
                        if q == KH + 3 or q == UF - 1:
                            bb = 0 if q == KH + 3 else 1
                            dve.wait_ge(s_out, it * NB + bb + 1)
                            yt = y[:, bass.ds(j * TB + bb * TPB, TB)]
                            nc.vector.tensor_tensor(yt, pso[:], yt, ALU.add).then_inc(s_yo, 1)
                    dve.wait_ge(s_y, it * NB + NB)

            @block.tensor
            def _(pe):
                with pe.Fori(0, NBLK) as j:
                    it = L * NBLK + j
                    pe.wait_ge(s_w, (L + 1) * 80)
                    norm.transpose(pe, it, lambda b, k: ps[:, b, k])
                    pe.wait_ge(norm.s_hT, it * NB + NB)

                    def up(q):
                        n, f, b = it * UF + q, q % KH, q // KH
                        M = P if f < KH - 1 else HTAIL
                        if q >= 2:
                            pe.wait_ge(s_hid, n - 1)
                        for i2 in range(2):
                            for k in range(KD):
                                i = nc.tensor.matmul(ps[0:M, q % 2, i2], w1[:, k, i2 * HID + f * P:i2 * HID + f * P + M],
                                                     hT[:, b, k], start=(k == 0), stop=(k == KD - 1))
                        i.then_inc(s_pair, 1)

                    def down(b):
                        pe.wait_ge(s_hid, it * UF + (b + 1) * KH)
                        if b:
                            pe.wait_ge(s_yo, it * NB + b)
                        for f in range(KH):
                            M = P if f < KH - 1 else HTAIL
                            for t in range(TB):
                                i = nc.tensor.matmul(pso[:, t], hid[0:M, b, f, t * P:(t + 1) * P], w2[0:M, f],
                                                     start=(f == 0 and t % 2 == 0), stop=(f == KH - 1 and t % 2 == 1),
                                                     skip_group_check=True)
                        i.then_inc(s_out, 1)

                    for q in range(UF):
                        up(q)
                        if q == KH + 1:
                            down(0)
                    down(1)
                    pe.wait_ge(s_yo, it * NB + NB)


def leave_local_stack(nc, a, keep, y, spill):
    with ExitStack() as ctx:
        m = Pool(nc, ctx, "fin")
        xr = m.sb("xr", [P, NT, D])
        s_g, s_r, s_o = m.sem("gated"), m.sem("ready"), m.sem("stored")
        s_x = [m.sem(f"x_in{n}") for n in range(NT // TB)]
        with nc.Block() as block:
            @block.vector
            def _(dve):
                for n in range(NT // TB):
                    t = slice(n * TB, (n + 1) * TB)
                    g = keep["gates"][:, 1, 1, n // NBLK:n // NBLK + 1].broadcast_to([P, TB, D])
                    nc.vector.tensor_tensor(y[:, t], y[:, t], g, ALU.mult).then_inc(s_g, 1)

            @block.gpsimd
            def _(pool):
                for n in range(NT // TB):
                    t = slice(n * TB, (n + 1) * TB)
                    pool.wait_ge(s_g, n + 1)
                    pool.wait_ge(s_x[n], 16)
                    nc.gpsimd.tensor_tensor(y[:, t], xr[:, t], y[:, t], ALU.add).then_inc(s_r, 1)

            @block.sync
            def _(sp):
                back = spill.rearrange("(t p) d -> p t d", p=P)
                out = a["y"].rearrange("(t p) d -> p t d", p=P)
                for n in range(NT // TB):
                    t = slice(n * TB, (n + 1) * TB)
                    sp.dma_start(xr[:, t], back[:, t]).then_inc(s_x[n], 16)
                for n in range(NT // TB):
                    t = slice(n * TB, (n + 1) * TB)
                    sp.wait_ge(s_r, n + 1)
                    sp.dma_start(out[:, t], y[:, t]).then_inc(s_o, 16)
                sp.wait_ge(s_o, 16 * (NT // TB))


def local_stack(nc, a, keep):
    with ExitStack() as ctx:
        m = Pool(nc, ctx, "stk")
        y = keep["x"]
        spill = nc.dram_tensor("x_aside", [NT * P, D], F32).ap()
        xs_a = m.sb("xs_a", [P, NB, TPB + 1, P])
        xs_b = m.sb("xs_b", [P, NB, TPB + 1, P])
        cos = m.sb("cos", [P, TPB, 2, LHD])
        sin = m.sb("sin", [P, TPB, 2, LHD])
        mask = m.sb("mask", [P, TPB, 2 * P], BF16)
        identb = m.sb("identb", [P, P], BF16)
        s_t, s_mk = m.sem("tables"), keep["soft"].sem("masks")
        with nc.Block() as block:
            @block.sync
            def _(sp):
                for dst, name in ((cos, "cos"), (sin, "sin")):
                    sp.dma_start(dst[:], a[name]).then_inc(s_t, 16)
                sp.wait_ge(s_t, 32)

            @block.gpsimd
            def _(pool):
                for dst, name in ((mask, "loc_mask"), (identb, "ident")):
                    pool.dma_start(dst[:], a[name]).then_inc(s_mk, 16)
                pool.wait_ge(s_mk, 32)
        enter_local_stack(nc, a, keep, y, xs_a, spill)
        with nc.Fori(0, DEPTH) as layer:
            local_attention(nc, a, keep, y, xs_a, xs_b, (cos, sin, mask, identb), layer)
            gated_mlp(nc, a, keep, y, xs_a, xs_b, layer)
        leave_local_stack(nc, a, keep, y, spill)


def write_out(nc, a, keep):
    with ExitStack() as ctx:
        m = Pool(nc, ctx, "out")
        s_o = m.sem("stored")
        with nc.Block() as block:
            @block.sync
            def _(sp):
                sp.dma_start(a["y"].rearrange("(t p) d -> p t d", p=P), keep["x"][:]).then_inc(s_o, 16)
                sp.wait_ge(s_o, 16)


def build_program(nc, a, stages=(1, 2, 3, 4)):
    with ExitStack() as ctx:
        m = Pool(nc, ctx, "keep")
        keep = {
            "x": m.sb("x", [P, NT, D]),
            "ident": m.sb("ident", [P, P]),
            "modf": m.sb("modf", [P, 2, 6, KD * NB]),
            "gates": m.sb("gates", [P, 2, 2, NB, D]),
            "moe_scale_row": m.sb("moe_scale_row", [P, NB, D]),
            "moe_shift_row": m.sb("moe_shift_row", [P, NB, D]),
            "scale_row": m.sb("scale_row", [P, NB, D]),
            "shift_row": m.sb("shift_row", [P, NB, D]),
            "bmix_gated": m.sb("bmix_gated", [P, NB, D]),
            "eps": m.sb("eps", [P, 1]),
            "one": m.sb("one", [P, 1]),
            "u_log": m.sb("u_log", [P, 1]),
            "ss_log": m.sb("ss_log", [P, 1]),
        }
        keep["soft"] = Pool(nc, ctx, "soft")
        s_c = m.sem("consts")
        with nc.Block() as block:
            @block.vector
            def _(dve):
                nc.vector.memset(keep["eps"][:], EPS).then_inc(s_c, 1)
                nc.vector.memset(keep["one"][:], 1.0).then_inc(s_c, 1)
                nc.vector.memset(keep["u_log"][:], U_LOG).then_inc(s_c, 1)
                nc.vector.memset(keep["ss_log"][:], SS_LOG).then_inc(s_c, 1)
                dve.wait_ge(s_c, 4)
        load_and_modulate(nc, a, keep)
        if 1 in stages:
            gated_recurrence(nc, a, keep)
        if 2 in stages:
            experts(nc, a, keep)
        if 3 in stages:
            windowed_attention(nc, a, keep)
        if 4 in stages:
            local_stack(nc, a, keep)
        else:
            write_out(nc, a, keep)


def lay_out(inputs):
    c = np.ascontiguousarray
    out = {k: c(inputs[k]) for k in (
        "L0_attn_W_aiv", "L0_attn_decay_bias", "L0_attn_W_mix", "L0_attn_b_mix", "L0_wmod", "L1_wmod",
        "L0_ffn_router_DE", "L0_ffn_w_in_eDF", "L0_ffn_w_swiglu_eDF", "L0_ffn_w_out_eFD")}
    out["L0_c"], out["L1_c"] = c(np.asarray(inputs["L0_c"]).T), c(np.asarray(inputs["L1_c"]).T)
    out["x"] = c(inputs["L0_attn_x"]).reshape(NB * SEQ, D)
    out["L0_attn_decay_bias"] = c(c(inputs["L0_attn_decay_bias"]).reshape(NG, P).T)
    out["shared_in"] = c(np.asarray(inputs["L0_ffn_w_in_shared_FD"]).T)
    out["shared_sw"] = c(np.asarray(inputs["L0_ffn_w_swiglu_FD"]).T)
    out["shared_out"] = c(np.asarray(inputs["L0_ffn_w_out_shared_DF"]).T)
    out["number"] = np.arange(EXP, dtype=np.float32)
    out["region"] = (np.arange(EXP) * REGION).astype(np.float32)
    out["iota"] = np.arange(P, dtype=np.float32)[:, None]
    out["steps"] = (np.arange(NB * TPB) * P).astype(np.float32)
    out["block_no"] = np.arange(XBLOCKS, dtype=np.float32)
    out["before"] = np.triu(np.ones((P, P), np.float32), 1)
    out["ident"] = np.eye(P, dtype=np.float32)
    out["keepmask"] = (np.arange(BLK) % CHUNK != 0).astype(np.float32)
    out["att_wq"] = c(np.asarray(inputs["L1_attn_Wq"]).T)
    wk = np.asarray(inputs["L1_attn_Wk"]).T.reshape(D, AKV, 1, AHD)
    out["att_wk"] = c(np.broadcast_to(wk, (D, AKV, AG, AHD)).reshape(D, D))
    out["att_wv"] = c(np.asarray(inputs["L1_attn_Wv"]).T)
    out["att_wo"] = c(np.asarray(inputs["L1_attn_Wo"]).T)
    out.update(shape_constants())
    out["wqkv"] = c(inputs["L1_ffn_wqkv"])
    out["loc_wo"] = c(inputs["L1_ffn_wo"])
    out["qk_scale"] = np.stack([np.asarray(inputs["L1_ffn_q_scale"]), np.asarray(inputs["L1_ffn_k_scale"])], axis=1)
    out["w1"] = c(inputs["L1_ffn_w1"])
    out["w2"] = c(inputs["L1_ffn_w2"])
    out["b2"] = c(inputs["L1_ffn_b2"])
    col = np.zeros((DEPTH, 2 * KD + 2 * KH, P), np.float32)
    col[:, 0:KD] = np.asarray(inputs["L1_ffn_ln_g"]).reshape(DEPTH, KD, P)
    col[:, KD:2 * KD] = np.asarray(inputs["L1_ffn_ln_b"]).reshape(DEPTH, KD, P)
    b1 = np.asarray(inputs["L1_ffn_b1"])
    for half in range(2):
        part = np.zeros((DEPTH, KH * P), np.float32)
        part[:, :HID] = b1[:, half * HID:(half + 1) * HID]
        col[:, 2 * KD + half * KH:2 * KD + (half + 1) * KH] = part.reshape(DEPTH, KH, P)
    out["mlp_col"] = c(col.transpose(0, 2, 1))
    return out


def shape_constants():
    far = np.float32(-1e30)
    q, key = np.arange(P)[:, None], np.arange(P)[None, :]
    before = np.where(key >= q, 0, far)
    after = np.where(key <= q, 0, far)
    never = np.full((P, P), far)
    win = np.zeros((P, TPB, AW), np.float32)
    loc = np.zeros((P, TPB, 2 * P), np.float32)
    for t in range(TPB):
        win[:, t, 0:P] = loc[:, t, 0:P] = before if t else never
        win[:, t, 2 * P:] = after if t < TPB - 1 else never
        loc[:, t, P:] = after
    half = np.arange(0, LHD, 2, dtype=np.float32)
    inv_freq = np.float32(1.0) / np.float32(10000.0) ** (half / np.float32(LHD))
    t = np.arange(SEQ, dtype=np.float32)
    freqs = t[:, None] * inv_freq[None]
    base = (half + np.float32(0.4 * LHD)) / np.float32(1.4 * LHD)
    scale = (base[None].astype(np.float64) ** ((t - SEQ // 2) / 64.0)[:, None])
    cosf, sinf = np.cos(freqs.astype(np.float64)), np.sin(freqs.astype(np.float64))
    cos, sin = np.zeros((SEQ, 2, LHD)), np.zeros((SEQ, 2, LHD))
    for i, s in enumerate((scale, 1 / scale)):
        cos[:, i] = np.concatenate([cosf * s, cosf * s], axis=1)
        sin[:, i] = np.concatenate([-sinf * s, sinf * s], axis=1)
    tile = lambda x: np.ascontiguousarray(x.reshape(TPB, P, 2, LHD).transpose(1, 0, 2, 3).astype(np.float32))
    return {
        "win_mask": win, "loc_mask": loc,
        "headmask": (np.arange(P)[:, None] // AHD == np.arange(HPC)[None]).astype(np.float32),
        "cos": tile(cos), "sin": tile(sin),
    }


def kernel(**inputs):
    import concourse.bacc as bacc
    from concourse.bass_utils import run_bass_kernel_spmd

    nc = bacc.Bacc("TRN2", target_bir_lowering=False, num_devices=1)
    arrays = {f"in_{name}": value for name, value in lay_out(inputs).items()}
    aps = {name[3:]: nc.dram_tensor(name, value.shape, mybir.dt.from_np(value.dtype), kind="ExternalInput").ap()
           for name, value in arrays.items()}
    aps["y"] = nc.dram_tensor("out_y", (NB * SEQ, D), F32, kind="ExternalOutput").ap()
    build_program(nc, aps)
    result = run_bass_kernel_spmd(nc, [arrays], core_ids=[0])
    return result.results[0]["out_y"].reshape(NB, SEQ, D)
```

```python
from contextlib import ExitStack

import numpy as np

import concourse.bass as bass
from concourse import mybir

F32 = mybir.dt.float32
F32R = mybir.dt.float32r
BF16 = mybir.dt.bfloat16
U32 = mybir.dt.uint32
I32 = mybir.dt.int32
ALU = mybir.AluOpType
ACT = mybir.ActivationFunctionType
AX_X = mybir.AxisListType.X

P = 128
D = 256
KD = D // P
NB = 2
SEQ = 2048
TPB = SEQ // P
NT = NB * TPB
BLK = 512
TB = BLK // P
NBLK = SEQ // BLK
EPS = 1e-5
MODS = ("shift_a", "scale_a", "gate_a", "shift_b", "scale_b", "gate_b")
SHIFT_A, SCALE_A, GATE_A, SHIFT_B, SCALE_B, GATE_B = range(6)
LN_SET = "natural_log_exp_and_others"

REC = 1024
NG = REC // P
CHUNK = 64
CPB = BLK // CHUNK
LN_TINY = float(np.log(1e-10))
U_SCALE = 2.0 ** -10
U_LOG = float(10 * np.log(2.0) / 2)
SIG_FLOOR = float(0.5 * np.log(1e-8)) - U_LOG

AH = 16
AHD = 16
AKV = 4
AG = AH // AKV
AW = 3 * P
HPR = 2

DEPTH = 2
LH = 8
LHD = 64
INNER = LH * LHD
KI = INNER // P
HID = 682
KH = -(-HID // P)
HTAIL = HID - (KH - 1) * P
QK_SCALE = 8.0
SS_SCALE = 2.0 ** 20
SS_LOG = float(10 * np.log(2.0))

EXP = 8
FF = 512
KF = FF // P
CHOICES = 2
REGION = NB * SEQ + P
XBLOCKS = CHOICES * NB * TPB + EXP
SPARE = EXP
LAST_ROW = EXP * REGION + (SPARE - 1) * P


def on_all(vector, n):
    return vector.rearrange("(a n) -> a n", a=1).broadcast_to([P, n])


class Pool:

    def __init__(self, nc, ctx, name):
        self.nc, self.ctx, self.name = nc, ctx, name
        self.sems = []

    def sb(self, name, shape, dt=F32):
        return self.ctx.enter_context(self.nc.sbuf_tensor(f"sb_{self.name}_{name}", shape, dt))

    def ps(self, name, shape, dt=F32):
        return self.ctx.enter_context(self.nc.psum_tensor(f"ps_{self.name}_{name}", shape, dt))

    def sem(self, name):
        self.sems.append(self.ctx.enter_context(self.nc.semaphore(f"{self.name}_{name}")))
        return self.sems[-1]

    def clear(self):
        with self.nc.Block() as block:
            @block.gpsimd
            def _(pool):
                for sem in self.sems:
                    pool.sem_clear(sem)


class BlockNorm:

    def __init__(self, m, keep, halves, scale, shift, banks=1):
        self.banks = banks
        self.nc, self.keep, self.halves, self.scale, self.shift = m.nc, keep, halves, scale, shift
        self.stats = m.sb("stats", [P, NB, TB, KD, 6])
        self.mv = m.sb("mv", [P, NB, TB, 2])
        self.settle = m.sb("settle", [P, 1])
        self.lnv = m.sb("lnv", [P, NB, TB])
        self.rstd = m.sb("rstd", [P, NB, TB])
        self.nmr = m.sb("nmr", [P, NB, TB])
        self.xn = m.sb("xn", [P, NB, TB, D])
        self.hT = m.sb("hT", [P, NB, KD, BLK])
        (self.s_st, self.s_mv, self.s_ln, self.s_rstd, self.s_nmr, self.s_xn, self.s_tr, self.s_hT) = (
            m.sem(n) for n in ("stats", "mv", "lnv", "rstd", "nmr", "xn", "tr", "hT"))

    def normalise(self, dve, it, j=None):
        self.statistics(dve, it, j)
        for b in range(NB):
            self.scale_rows(dve, it, b, j)

    def statistics(self, dve, it, j=None):
        nc = self.nc
        j = it if j is None else j
        for b in range(NB):
            for t in range(TB):
                parts = self.halves(b, t, j)
                for k, part in enumerate(parts):
                    i = nc.vector.bn_stats(self.stats[:, b, t, k], part)
            i.then_inc(self.s_st, 1)
        dve.wait_ge(self.s_st, it * NB + NB)
        nc.vector.memset(self.settle[:], 0.0)
        for b in range(NB):
            for t in range(TB):
                i = nc.vector.bn_aggr(self.mv[:, b, t], self.stats[:, b, t, 0:len(self.halves(b, t, j))])
            i.then_inc(self.s_mv, 1)

    def scale_rows(self, dve, it, b, j=None, ahead=False):
        nc = self.nc
        j = it if j is None else j
        dve.wait_ge(self.s_rstd, it * NB + b + 1)
        dve.wait_ge(self.s_mv, it * NB + b + 1)
        nc.vector.scalar_tensor_tensor(out=self.nmr[:, b], in0=self.mv[:, b, :, 0], scalar=-1.0,
                                       in1=self.rstd[:, b], op0=ALU.mult, op1=ALU.mult).then_inc(self.s_nmr, 1)
        dve.wait_ge(self.s_nmr, it * NB + b + 1)
        if ahead:
            dve.wait_ge(self.s_tr, ((it - 1) * NB + b + 1) * KD)
        for t in range(TB):
            parts = self.halves(b, t, j)
            w = D // len(parts)
            for k, part in enumerate(parts):
                i = nc.vector.tensor_scalar(self.xn[:, b, t, k * w:(k + 1) * w], part, self.rstd[:, b, t:t + 1],
                                            self.nmr[:, b, t:t + 1], ALU.mult, ALU.add)
        i.then_inc(self.s_xn, 1)

    def inverse_deviation(self, act, it):
        nc = self.nc
        for b in range(NB):
            act.wait_ge(self.s_mv, it * NB + b + 1)
            nc.scalar.activation(self.lnv[:, b], self.mv[:, b, :, 1], ACT.Ln,
                                 bias=self.keep["eps"][:, 0:1]).then_inc(self.s_ln, 1)
            act.wait_ge(self.s_ln, it * NB + b + 1)
            nc.scalar.activation(self.rstd[:, b], self.lnv[:, b], ACT.Exp, scale=-0.5).then_inc(self.s_rstd, 1)

    def turn(self, pe, it, b, k, bank, first=False):
        pe.wait_ge(self.s_xn, it * NB + b + 1)
        if not first:
            pe.wait_ge(self.s_hT, (it * NB + b) * KD + k - self.banks + 1)
        for t in range(TB):
            i = self.nc.tensor.transpose(bank[:, t * P:(t + 1) * P], self.xn[:, b, t, k * P:(k + 1) * P],
                                         self.keep["ident"][:])
        i.then_inc(self.s_tr, 1)

    def affine_chunk(self, act, it, b, k, bank):
        act.wait_ge(self.s_tr, (it * NB + b) * KD + k + 1)
        self.nc.scalar.activation(self.hT[:, b, k], bank, ACT.Identity, scale=self.scale(b, k),
                                  bias=self.shift(b, k)).then_inc(self.s_hT, 1)

    def ready(self, it, b):
        return (it * NB + b + 1) * KD

    def transpose(self, pe, it, psum):
        for b in range(NB):
            for k in range(KD):
                self.turn(pe, it, b, k, psum(b, k), first=True)

    def affine(self, act, it, psum):
        for b in range(NB):
            for k in range(KD):
                self.affine_chunk(act, it, b, k, psum(b, k))


def blocks_ahead(eng, step):
    with eng.Fori(0, NBLK - 1) as j:
        step(j, True)
    step(NBLK - 1, False)


def load_and_modulate(nc, a, keep):
    with ExitStack() as ctx:
        m = Pool(nc, ctx, "mod")
        cT = m.sb("cT", [P, 2, KD, NB])
        cs = m.sb("cs", [P, 2, KD, NB])
        cwide = m.sb("cwide", [P, 2, KD, NB, P])
        wmod = m.sb("wmod", [P, 2, KD, 6 * D])
        rows = m.sb("rows", [P, 2, NB, 6 * D])
        sign = m.sb("sign", [P, 4, D])
        size = m.sb("size", [P, 4, D])
        ps_row = m.ps("ps_row", [P, 2, 512])
        ps_col = m.ps("ps_col", [P, 2, 512])
        s_c, s_w, s_x, s_k, s_bm = (m.sem(n) for n in ("c_in", "wmod_in", "x_in", "const_in", "bmix_in"))
        s_silu, s_wide, s_row, s_rowcp, s_col, s_colcp = (
            m.sem(n) for n in ("silu", "wide", "row", "rowcp", "col", "colcp"))
        s_g = m.sem("guard")

        with nc.Block() as block:
            @block.sync
            def _(sp):
                for l, name in enumerate(("L0_c", "L1_c")):
                    sp.dma_start(cT[:, l], a[name].rearrange("(k p) b -> p k b", p=P)).then_inc(s_c, 16)
                for l, name in enumerate(("L0_wmod", "L1_wmod")):
                    sp.dma_start(wmod[:, l], a[name].rearrange("(k p) n -> p k n", p=P)).then_inc(s_w, 16)
                sp.dma_start(keep["ident"][:], a["ident"]).then_inc(s_k, 16)
                sp.dma_start(keep["bmix_gated"][:, 0], on_all(a["L0_attn_b_mix"], D)).then_inc(s_bm, 16)
                sp.dma_start(keep["x"][:], a["x"].rearrange("(t p) d -> p t d", p=P)).then_inc(s_x, 16)
                sp.wait_ge(s_k, 16)
                sp.wait_ge(s_x, 16)

            @block.scalar
            def _(act):
                act.wait_ge(s_c, 32)
                nc.scalar.activation(cs[:], cT[:], ACT.Silu).then_inc(s_silu, 1)
                for n in range(12):
                    act.wait_ge(s_row, n + 1)
                    l, b, c = n // 6, n // 3 % 2, n % 3
                    nc.scalar.copy(rows[:, l, b, c * 512:(c + 1) * 512], ps_row[:, n % 2]).then_inc(s_rowcp, 1)

            @block.tensor
            def _(pe):
                pe.wait_ge(s_w, 32)
                pe.wait_ge(s_silu, 1)
                for l in range(2):
                    for c in range(6 * KD):
                        for k in range(KD):
                            mm = nc.tensor.matmul(ps_col[:, l, 2 * c:2 * c + 2], wmod[:, l, k, c * P:(c + 1) * P],
                                                  cs[:, l, k], start=(k == 0), stop=(k == KD - 1))
                mm.then_inc(s_col, 1)
                pe.wait_ge(s_wide, 1)
                for n in range(12):
                    l, b, c = n // 6, n // 3 % 2, n % 3
                    if n >= 2:
                        pe.wait_ge(s_rowcp, n - 1)
                    for k in range(KD):
                        mm = nc.tensor.matmul(ps_row[:, n % 2], cwide[:, l, k, b],
                                              wmod[:, l, k, c * 512:(c + 1) * 512], start=(k == 0), stop=(k == KD - 1))
                    mm.then_inc(s_row, 1)

            @block.vector
            def _(dve):
                dve.wait_ge(s_silu, 1)
                for l in range(2):
                    for k in range(KD):
                        i = nc.vector.tensor_copy(cwide[:, l, k], cs[:, l, k].unsqueeze(2).broadcast_to([P, NB, P]))
                i.then_inc(s_wide, 1)
                dve.wait_ge(s_col, 1)
                nc.vector.tensor_copy(keep["modf"][:], ps_col[:, :, 0:24].rearrange("p l (j n) -> p l j n", n=2 * KD)
                                      ).then_inc(s_colcp, 1)
                dve.wait_ge(s_colcp, 1)
                for j in (SCALE_A, SCALE_B):
                    nc.vector.tensor_scalar(keep["modf"][:, :, j], keep["modf"][:, :, j], 1.0, None,
                                            ALU.add).then_inc(s_colcp, 1)
                dve.wait_ge(s_rowcp, 12)
                n = 0
                for l in range(2):
                    for w, j in enumerate((GATE_A, GATE_B)):
                        g = rows[:, l, :, j * D:(j + 1) * D]
                        sg = sign[:, 2 * w:2 * w + 2]
                        sz = size[:, 2 * w:2 * w + 2]
                        nc.vector.tensor_scalar(sg, g, 0.0, 2.0, ALU.is_ge, ALU.mult).then_inc(s_g, 1)
                        nc.vector.scalar_tensor_tensor(out=sz, in0=g, scalar=-1.0, in1=g, op0=ALU.mult,
                                                       op1=ALU.max).then_inc(s_g, 1)
                        dve.wait_ge(s_g, n + 2)
                        nc.vector.tensor_scalar(sz, sz, 0.25, None, ALU.max).then_inc(s_g, 1)
                        dve.wait_ge(s_g, n + 3)
                        nc.vector.scalar_tensor_tensor(out=keep["gates"][:, l, w], in0=sg, scalar=-1.0, in1=sz,
                                                       op0=ALU.add, op1=ALU.mult).then_inc(s_g, 1)
                        n += 4
                        dve.wait_ge(s_g, n)
                nc.vector.tensor_scalar(keep["moe_scale_row"][:], rows[:, 0, :, SCALE_B * D:(SCALE_B + 1) * D], 1.0, None,
                                        ALU.add)
                nc.vector.tensor_copy(keep["moe_shift_row"][:], rows[:, 0, :, SHIFT_B * D:(SHIFT_B + 1) * D])
                nc.vector.tensor_scalar(keep["scale_row"][:], rows[:, 1, :, SCALE_B * D:(SCALE_B + 1) * D], 1.0, None,
                                        ALU.add).then_inc(s_g, 1)
                nc.vector.tensor_copy(keep["shift_row"][:], rows[:, 1, :, SHIFT_B * D:(SHIFT_B + 1) * D]).then_inc(s_g, 1)
                dve.wait_ge(s_bm, 16)
                bm = keep["bmix_gated"]
                nc.vector.tensor_tensor(bm[:, 1], bm[:, 0], keep["gates"][:, 0, 0, 1], ALU.mult).then_inc(s_g, 1)
                dve.wait_ge(s_g, n + 3)
                nc.vector.tensor_tensor(bm[:, 0], bm[:, 0], keep["gates"][:, 0, 0, 0], ALU.mult).then_inc(s_g, 1)
                dve.wait_ge(s_g, n + 4)
                dve.wait_ge(s_colcp, 3)
        m.clear()


def gated_recurrence(nc, a, keep):
    x, modf, ident = keep["x"], keep["modf"], keep["ident"]
    with ExitStack() as ctx:
        m = Pool(nc, ctx, "rec")
        w = m.sb("w", [P, KD, 3 * REC])
        wmix = m.sb("wmix", [P, NG, D])
        nbias = m.sb("nbias", [P, NG])
        keepmask = m.sb("keepmask", [P, BLK])
        ones = m.sb("ones", [P, CPB])
        norm = BlockNorm(m, keep, lambda b, t, it: [x[:, bass.ds(it * TB + b * TPB + t, 1)]],
                         lambda b, k: modf[:, 0, SCALE_A, NB * k + b:NB * k + b + 1],
                         lambda b, k: modf[:, 0, SHIFT_A, NB * k + b:NB * k + b + 1])
        hT = norm.hT
        e = m.sb("e", [P, 2, 2, BLK])
        u = m.sb("u", [P, 2, BLK])
        l = m.sb("l", [P, 2, 2, BLK])
        lu = m.sb("lu", [P, 2, BLK])
        cum = m.sb("cum", [P, 2, BLK])
        q = m.sb("q", [P, 2, BLK])
        z = m.sb("z", [P, 2, BLK])
        ez = m.sb("ez", [P, 2, BLK])
        dec = m.sb("dec", [P, 2, BLK])
        wt = m.sb("wt", [P, 2, BLK])
        ws = m.sb("ws", [P, 2, BLK])
        st = m.sb("st", [P, 3, BLK])
        last = m.sb("last", [P, 2, CPB])
        lc = m.sb("lc", [P, NB, NG, CPB + 1])
        lcm = m.sb("lcm", [P, 2, CPB])
        c9 = m.sb("c9", [P, 2, CPB])
        rc = m.sb("rc", [P, 2, CPB])
        fin = m.sb("fin", [P, 2, CPB])
        fin2 = m.sb("fin2", [P, 2, CPB])
        cw = m.sb("cw", [P, NB, NG, CPB + 1])
        inc = m.sb("inc", [P, 2, CPB])
        og = m.sb("og", [P, TB, D])
        ps = m.ps("ps", [P, 2, 3, BLK])
        pso = m.ps("pso", [P, TB, D])

        s_w, s_wm = m.sem("w_in"), m.sem("wmix_in")
        (s_aiv, s_e, s_ec, s_u, s_l, s_lu, s_cum, s_q, s_q2, s_z, s_last, s_lc, s_lcm, s_ez, s_rc) = (
            m.sem(n) for n in ("aiv", "e", "ec", "u", "l", "lu", "cum", "q", "q2", "z", "last", "lc", "lcm", "ez", "rc"))
        (s_wt, s_ws, s_fin, s_fin2, s_cw, s_inc, s_carry, s_wi, s_state, s_mix, s_og, s_ogb, s_x) = (
            m.sem(n) for n in ("wt", "ws", "fin", "fin2", "cw", "inc", "carry", "wi", "state", "mix", "og", "ogb", "x"))
        s_init = m.sem("init")
        US = NB * NG
        STATS = NG + 1

        with nc.Block() as block:
            @block.sync
            def _(sp):
                for k in range(KD):
                    sp.dma_start(w[:, k], a["L0_attn_W_aiv"][k * P:(k + 1) * P]).then_inc(s_w, 16)
                sp.dma_start(nbias[:], a["L0_attn_decay_bias"]).then_inc(s_w, 16)
                sp.dma_start(keepmask[:], on_all(a["keepmask"], BLK)).then_inc(s_w, 16)
                sp.dma_start(wmix[:], a["L0_attn_W_mix"].rearrange("(g p) d -> p g d", p=P)).then_inc(s_wm, 16)

            @block.gpsimd
            def _(pool):
                with pool.Fori(0, NBLK) as it:
                    for s in range(US + 1):
                        if s >= 1:
                            b, g, par, n = (s - 1) // NG, (s - 1) % NG, (s - 1) % 2, it * US + s
                            pool.wait_ge(s_inc, n)
                            nc.gpsimd.tensor_tensor(ws[:, par].rearrange("p (c t) -> p c t", c=CPB),
                                                    ws[:, par].rearrange("p (c t) -> p c t", c=CPB),
                                                    inc[:, par].unsqueeze(2).broadcast_to([P, CPB, CHUNK]),
                                                    ALU.add).then_inc(s_wi, 1)
                            pool.wait_ge(s_wi, n)
                            nc.gpsimd.tensor_tensor(st[:, (s - 1) % 3], ws[:, par], dec[:, par],
                                                    ALU.mult).then_inc(s_state, 1)
                        if s and s % NG == 0:
                            b = s // NG - 1
                            pool.wait_ge(s_og, it * NB + b + 1)
                            nc.gpsimd.tensor_tensor(og[:], og[:], keep["bmix_gated"][:, b:b + 1].broadcast_to([P, TB, D]),
                                                    ALU.add).then_inc(s_ogb, 1)
                            pool.wait_ge(s_ogb, it * NB + b + 1)
                            xt = x[:, bass.ds(it * TB + b * TPB, TB)]
                            nc.gpsimd.tensor_tensor(xt, xt, og[:], ALU.add).then_inc(s_x, 1)

            @block.scalar
            def _(act):
                nc.scalar.preload_act_table_set(LN_SET)
                act.wait_ge(s_init, 1)
                norm.inverse_deviation(act, 0)

                def step(it, ahead):
                    norm.affine(act, it, lambda b, k: ps[:, b, k])

                    def first(s):
                        b, g, par, n = s // NG, s % NG, s % 2, it * US + s
                        act.wait_ge(s_aiv, n + 1)
                        nc.scalar.activation(e[:, par, 0], ps[:, par, 0], ACT.Exp, scale=-1.0, bias=nbias[:, g:g + 1])
                        nc.scalar.activation(e[:, par, 1], ps[:, par, 1], ACT.Exp, scale=-1.0).then_inc(s_e, 1)

                    def logs(s):
                        par, n = s % 2, it * US + s
                        act.wait_ge(s_ec, n + 1)
                        nc.scalar.activation(l[:, par], e[:, par], ACT.Ln, bias=1.0).then_inc(s_l, 1)
                        act.wait_ge(s_u, n + 1)
                        nc.scalar.activation(lu[:, par], u[:, par], ACT.Ln, scale=U_SCALE).then_inc(s_lu, 1)

                    def exps(s):
                        b, g, par, n = s // NG, s % NG, s % 2, it * US + s
                        act.wait_ge(s_z, n + 1)
                        nc.scalar.activation(ez[:, par], z[:, par], ACT.Exp, scale=-1.0,
                                             bias=keep["u_log"][:, 0:1]).then_inc(s_ez, 1)
                        act.wait_ge(s_lcm, n + 1)
                        if s >= 2:
                            act.wait_ge(s_state, n - 1)
                        nc.scalar.activation(dec[:, par], cum[:, par], ACT.Exp)
                        nc.scalar.activation(c9[:, par], lc[:, b, g, 0:CPB], ACT.Exp)
                        nc.scalar.activation(rc[:, par], lcm[:, par], ACT.Exp, scale=-1.0).then_inc(s_rc, 1)

                    for s in range(US + 1):
                        if s < US:
                            first(s)
                        if s >= 1:
                            exps(s - 1)
                        if s < US:
                            logs(s)
                        if ahead and s == STATS:
                            norm.inverse_deviation(act, it + 1)

                blocks_ahead(act, step)

            @block.vector
            def _(dve):
                nc.vector.memset(lc[:], 0.0)
                nc.vector.memset(cw[:], 0.0)
                nc.vector.memset(ones[:], 1.0)
                dve.wait_ge(s_w, 16 * 4)
                nc.vector.tensor_scalar(nbias[:], nbias[:], -1.0, None, ALU.mult).then_inc(s_init, 1)
                dve.wait_ge(s_init, 1)
                norm.normalise(dve, 0)

                def step(it, ahead):

                    def clamp(s):
                        par, n = s % 2, it * US + s
                        dve.wait_ge(s_e, n + 1)
                        nc.vector.tensor_scalar(e[:, par, 0], e[:, par, 0], 1e-12, 1e10, ALU.max, ALU.min)
                        nc.vector.tensor_scalar(e[:, par, 1], e[:, par, 1], 1e19, None, ALU.min).then_inc(s_ec, 1)
                        dve.wait_ge(s_ec, n + 1)
                        nc.vector.scalar_tensor_tensor(out=u[:, par], in0=e[:, par, 0], scalar=2.0, in1=e[:, par, 0],
                                                       op0=ALU.add, op1=ALU.mult).then_inc(s_u, 1)

                    def sums(s):
                        b, g, par, n = s // NG, s % NG, s % 2, it * US + s
                        dve.wait_ge(s_l, n + 1)
                        nc.vector.tensor_tensor_scan(cum[:, par], keepmask[:], l[:, par, 0], 0.0, ALU.mult,
                                                     ALU.subtract).then_inc(s_cum, 1)
                        dve.wait_ge(s_lu, n + 1)
                        nc.vector.scalar_tensor_tensor(out=q[:, par], in0=lu[:, par], scalar=0.5, in1=l[:, par, 0],
                                                       op0=ALU.mult, op1=ALU.subtract).then_inc(s_q, 1)
                        dve.wait_ge(s_q, n + 1)
                        nc.vector.scalar_tensor_tensor(out=q[:, par], in0=q[:, par], scalar=SIG_FLOOR, in1=l[:, par, 1],
                                                       op0=ALU.max, op1=ALU.subtract).then_inc(s_q2, 1)
                        dve.wait_ge(s_q2, n + 1)
                        nc.vector.scalar_tensor_tensor(out=z[:, par], in0=cum[:, par], scalar=LN_TINY, in1=q[:, par],
                                                       op0=ALU.max, op1=ALU.subtract).then_inc(s_z, 1)
                        ends = cum[:, par].rearrange("p (c t) -> p c t", c=CPB)[:, :, CHUNK - 1]
                        nc.vector.tensor_scalar(last[:, par], ends, LN_TINY, None, ALU.max).then_inc(s_last, 1)
                        dve.wait_ge(s_last, n + 1)
                        nc.vector.tensor_tensor_scan(lc[:, b, g, 1:CPB + 1], ones[:], last[:, par], lc[:, b, g, 0:1],
                                                     ALU.mult, ALU.add).then_inc(s_lc, 1)
                        dve.wait_ge(s_lc, n + 1)
                        nc.vector.tensor_scalar(lcm[:, par], lc[:, b, g, 1:CPB + 1], LN_TINY, None,
                                                ALU.max).then_inc(s_lcm, 1)

                    def states(s):
                        b, g, par, n = s // NG, s % NG, s % 2, it * US + s
                        dve.wait_ge(s_ez, n + 1)
                        nc.vector.tensor_tensor(wt[:, par], ps[:, par, 2], ez[:, par], ALU.mult).then_inc(s_wt, 1)
                        dve.wait_ge(s_wt, n + 1)
                        if s >= 2:
                            dve.wait_ge(s_state, n - 1)
                        nc.vector.tensor_tensor_scan(ws[:, par], keepmask[:], wt[:, par], 0.0, ALU.mult,
                                                     ALU.add).then_inc(s_ws, 1)
                        dve.wait_ge(s_rc, n + 1)
                        dve.wait_ge(s_ws, n + 1)
                        wend = ws[:, par].rearrange("p (c t) -> p c t", c=CPB)[:, :, CHUNK - 1]
                        dend = dec[:, par].rearrange("p (c t) -> p c t", c=CPB)[:, :, CHUNK - 1]
                        nc.vector.tensor_tensor(fin[:, par], wend, dend, ALU.mult).then_inc(s_fin, 1)
                        dve.wait_ge(s_fin, n + 1)
                        nc.vector.tensor_tensor(fin2[:, par], fin[:, par], rc[:, par], ALU.mult).then_inc(s_fin2, 1)
                        dve.wait_ge(s_fin2, n + 1)
                        nc.vector.tensor_tensor_scan(cw[:, b, g, 1:CPB + 1], ones[:], fin2[:, par], cw[:, b, g, 0:1],
                                                     ALU.mult, ALU.add).then_inc(s_cw, 1)
                        dve.wait_ge(s_cw, n + 1)
                        nc.vector.tensor_tensor(inc[:, par], cw[:, b, g, 0:CPB], c9[:, par], ALU.mult).then_inc(s_inc, 1)
                        dve.wait_ge(s_inc, n + 1)
                        nc.vector.tensor_copy(lc[:, b, g, 0:1], lc[:, b, g, CPB:CPB + 1])
                        nc.vector.tensor_copy(cw[:, b, g, 0:1], cw[:, b, g, CPB:CPB + 1]).then_inc(s_carry, 1)

                    for s in range(US + 1):
                        if s < US:
                            clamp(s)
                        if s >= 1:
                            states(s - 1)
                        if s < US:
                            sums(s)
                        if ahead and s == STATS:
                            norm.statistics(dve, it + 1)
                        if ahead and s in (STATS + 2, STATS + 4):
                            norm.scale_rows(dve, it + 1, (s - STATS) // 2 - 1, ahead=True)
                        if s and s % NG == 0:
                            b = s // NG - 1
                            dve.wait_ge(s_mix, it * NB + b + 1)
                            if b:
                                dve.wait_ge(s_x, it * NB + b)
                            nc.vector.tensor_tensor(og[:], pso[:], keep["gates"][:, 0, 0, b:b + 1].broadcast_to([P, TB, D]),
                                                    ALU.mult).then_inc(s_og, 1)
                    dve.wait_ge(s_x, it * NB + NB)

                blocks_ahead(dve, step)

            @block.tensor
            def _(pe):
                pe.wait_ge(s_w, 16 * 4)
                pe.wait_ge(s_wm, 16)
                def step(it, ahead):
                    norm.transpose(pe, it, lambda b, k: ps[:, b, k])

                    def project(s):
                        b, g, par, n = s // NG, s % NG, s % 2, it * US + s
                        pe.wait_ge(norm.s_hT, norm.ready(it, NB - 1))
                        if s >= 2:
                            pe.wait_ge(s_wt, n - 1)
                        for j in range(3):
                            for k in range(KD):
                                i = nc.tensor.matmul(ps[:, par, j], w[:, k, j * REC + g * P:j * REC + (g + 1) * P],
                                                     hT[:, b, k], start=(k == 0), stop=(k == KD - 1))
                        i.then_inc(s_aiv, 1)

                    def mix(s):
                        b, g, n = s // NG, s % NG, it * US + s
                        pe.wait_ge(s_state, n + 1)
                        if g == 0 and b:
                            pe.wait_ge(s_og, it * NB + b)
                        for t in range(TB):
                            i = nc.tensor.matmul(pso[:, t], st[:, s % 3, t * P:(t + 1) * P], wmix[:, g],
                                                 start=(g == 0 and t % 2 == 0), stop=(g == NG - 1 and t % 2 == 1),
                                                 skip_group_check=True)
                        if g == NG - 1:
                            i.then_inc(s_mix, 1)

                    for s in range(US + 2):
                        if s < US:
                            project(s)
                        if s >= 2:
                            mix(s - 2)
                    pe.wait_ge(s_og, it * NB + NB)

                blocks_ahead(pe, step)
        m.clear()


def experts(nc, a, keep):
    with ExitStack() as ctx:
        m = Pool(nc, ctx, "moe")
        soft = {name: keep["soft"].sem(name) for name in ("before_in", "sorted", "padded", "got0", "got1")}
        t = {
            "w_in": m.sb("w_in", [P, EXP + 1, KD, FF]),
            "w_sw": m.sb("w_sw", [P, EXP + 1, KD, FF]),
            "row": m.sb("row", [P, NBLK, NB * TB, 2], U32),
            "block_expert": m.sb("block_expert", [1, XBLOCKS], I32),
            "block_row": m.sb("block_row", [1, XBLOCKS], I32),
            "sorted": nc.dram_tensor("sorted_tokens", [(EXP + 1) * REGION, D], F32).ap(),
            "results": nc.dram_tensor("expert_results", [XBLOCKS * P, D], F32).ap(),
            "w_here": m.sem("weights_in"),
            "soft": soft,
        }
        route_tokens(nc, a, keep, t)
        run_experts(nc, a, keep, t)
        collect_experts(nc, a, keep, t)
        m.clear()


def route_tokens(nc, a, keep, t):
    x, modf, ident = keep["x"], keep["modf"], keep["ident"]
    w_in, w_sw = t["w_in"], t["w_sw"]
    TI = NB * TB
    UF = NB * KF
    with ExitStack() as ctx:
        m = Pool(nc, ctx, "route")
        norm = BlockNorm(m, keep, lambda b, t, it: [x[:, bass.ds(it * TB + b * TPB + t, 1)]],
                         lambda b, k: modf[:, 0, SCALE_B, NB * k + b:NB * k + b + 1],
                         lambda b, k: modf[:, 0, SHIFT_B, NB * k + b:NB * k + b + 1])
        hT = norm.hT
        w_out = m.sb("w_out", [P, KF, D])
        router = m.sb("router", [P, KD, EXP])
        number = m.sb("number", [P, EXP])
        region = m.sb("region", [P, EXP])
        iota = m.sb("iota", [P, 1])
        steps = m.sb("steps", [P, SEQ * NB // P])
        block_no = m.sb("block_no", [1, XBLOCKS])
        before = m.sb("before", [P, P], BF16)
        ones = m.sb("ones", [P, P], BF16)
        zeros = m.sb("zeros", [P, D])
        score = m.sb("score", [P, TI, EXP])
        top = m.sb("top", [P, TI, 8])
        topi = m.sb("topi", [P, TI, 8], U32)
        topf = m.sb("topf", [P, TI, 8])
        pick = m.sb("pick", [P, 2, TI, EXP])
        chosen = m.sb("chosen", [P, TI, EXP], BF16)
        run = m.sb("run", [P, EXP])
        place = m.sb("place", [P, 2, TI, EXP])
        rowf = m.sb("rowf", [P, TI, 2])
        rowu = m.sb("rowu", [P, TI, 2], U32)
        rows = m.sb("rows", [P, NBLK, TI, 2])
        gate = m.sb("gate", [P, TI, 2])
        gated = m.sb("gated", [P, TI, 2, D])
        act_f = m.sb("act_f", [P, 2, BLK])
        hid = m.sb("hid", [P, 2, KF, BLK])
        og = m.sb("og", [P, TB, D])
        settle = m.sb("settle1", [P, 1])
        padf = m.sb("padf", [P, EXP])
        padu = m.sb("padu", [P, EXP], U32)
        count = m.sb("count", [P, EXP])
        over = m.sb("over", [P, EXP, SEQ * NB // P])
        blocks = m.sb("blocks", [P, EXP])
        end = m.sb("end", [P, EXP])
        past = m.sb("past", [1, 2, XBLOCKS, EXP])
        bexp = m.sb("bexp", [1, XBLOCKS])
        brow = m.sb("brow", [1, 2, XBLOCKS])
        shift = m.sb("shift", [P, 3, EXP])
        above = m.sb("above", [P, 2, NBLK * TI * 2, EXP])
        moved = m.sb("moved", [P, NBLK * TI * 2])
        ps = m.ps("ps", [P, 2, 2, BLK])
        pso = m.ps("pso", [P, TB, D])
        psg = m.ps("psg", [P, BLK])
        psr = psg
        pst = m.ps("pst", [P, BLK])
        s_b, s_sorted, s_padded = (t["soft"][n] for n in ("before_in", "sorted", "padded"))
        names = ("w_load ones score scorecp top topi topf pick chosen es es1 gate rank run place placed rowf rowu row "
                 "hmul h gated pair silu hid out og xadd pad padzero table settle")
        (s_w, s_ones, s_score, s_scorecp, s_top, s_topi, s_topf, s_pick, s_chosen, s_es, s_es1, s_gate, s_rank, s_run,
         s_place, s_placed, s_rowf, s_rowu, s_row, s_hmul, s_h, s_gated, s_pair, s_silu, s_hid, s_out, s_og, s_x,
         s_pad, s_padzero, s_table, s_settle) = (m.sem(n) for n in names.split())
        ROUTED = TI * 2

        with nc.Block() as block:
            @block.sync
            def _(sp):
                sp.dma_start(router[:], a["L0_ffn_router_DE"].rearrange("(k p) e -> p k e", p=P)).then_inc(s_w, 16)
                sp.dma_start(number[:], on_all(a["number"], EXP)).then_inc(s_w, 16)
                sp.dma_start(region[:], on_all(a["region"], EXP)).then_inc(s_w, 16)
                sp.dma_start(iota[:], a["iota"]).then_inc(s_w, 16)
                sp.dma_start(steps[:], on_all(a["steps"], SEQ * NB // P)).then_inc(s_w, 16)
                sp.dma_start(block_no[:], a["block_no"].unsqueeze(0)).then_inc(s_w, 16)
                sp.dma_start(w_in[:, EXP], a["shared_in"].rearrange("(k p) f -> p k f", p=P)).then_inc(s_w, 16)
                sp.dma_start(w_sw[:, EXP], a["shared_sw"].rearrange("(k p) f -> p k f", p=P)).then_inc(s_w, 16)
                sp.dma_start(w_out[:], a["shared_out"].rearrange("(k p) d -> p k d", p=P)).then_inc(s_w, 16)
                for e in range(EXP):
                    for dst, name in ((w_in, "L0_ffn_w_in_eDF"), (w_sw, "L0_ffn_w_swiglu_eDF")):
                        sp.dma_start(dst[:, e], a[name][e].rearrange("(k p) f -> p k f", p=P)).then_inc(t["w_here"], 16)
                sp.wait_ge(s_ones, 3)
                spare = t["sorted"][EXP * REGION:EXP * REGION + SPARE * P]
                sp.dma_start(spare.rearrange("(n p) d -> p n d", p=P), zeros[:].unsqueeze(1).broadcast_to([P, SPARE, D])
                             ).then_inc(s_padzero, 16)

            @block.gpsimd
            def _(pool):
                pool.dma_start(before[:], a["before"]).then_inc(s_b, 16)
                pool.wait_ge(s_w, 16 * 9)
                with pool.Fori(0, NBLK) as it:
                    for b in range(NB):
                        u = it * NB + b + 1
                        pool.wait_ge(norm.s_tr, norm.ready(it, b))
                        xn = norm.xn[:, b]
                        nc.gpsimd.tensor_tensor(xn, xn, keep["moe_scale_row"][:, b:b + 1].broadcast_to([P, TB, D]),
                                                ALU.mult).then_inc(s_hmul, 1)
                        pool.wait_ge(s_hmul, u)
                        nc.gpsimd.tensor_tensor(xn, xn, keep["moe_shift_row"][:, b:b + 1].broadcast_to([P, TB, D]),
                                                ALU.add).then_inc(s_h, 1)
                    pool.wait_ge(s_gated, it + 1)
                    pool.wait_ge(s_rowu, it + 1)
                    nc.gpsimd.tensor_tensor(settle[:], keep["one"][:], keep["one"][:], ALU.mult).then_inc(s_settle, 1)
                    for n in range(TI):
                        for c in range(2):
                            pool.indirect_dma_start(t["sorted"], bass.IndirectOffsetOnAxis(ap=rowu[:, n, c:c + 1], axis=0),
                                                    gated[:, n, c], None).then_inc(s_sorted, 16)
                    pool.wait_ge(s_settle, it + 1)
                    for b in range(NB):
                        pool.wait_ge(s_og, it * NB + b + 1)
                        xt = x[:, bass.ds(it * TB + b * TPB, TB)]
                        nc.gpsimd.tensor_tensor(xt, xt, og[:], ALU.add).then_inc(s_x, 1)
                pool.wait_ge(s_pad, 2)
                pool.wait_ge(s_sorted, NBLK * ROUTED * 16)
                for e in range(EXP):
                    pool.indirect_dma_start(t["sorted"], bass.IndirectOffsetOnAxis(ap=padu[:, e:e + 1], axis=0),
                                            zeros[:], None).then_inc(s_padded, 16)
                pool.wait_ge(s_padded, EXP * 16)
                pool.wait_ge(s_padzero, 16)

            @block.scalar
            def _(act):
                nc.scalar.preload_act_table_set(LN_SET)
                norm.inverse_deviation(act, 0)
                norm.affine(act, 0, lambda b, k: ps[:, b, k])

                def step(it, ahead):
                    nc.scalar.preload_act_table_set(LN_SET)
                    act.wait_ge(s_top, it + 1)
                    nc.scalar.activation(gate[:], top[:, :, 0:2], ACT.Exp, scale=-1.0).then_inc(s_es, 1)
                    for q in range(UF):
                        n = it * UF + q
                        act.wait_ge(s_pair, n + 1)
                        if q >= 2:
                            act.wait_ge(s_hid, n - 1)
                        nc.scalar.activation(act_f[:, q % 2], ps[:, q % 2, 0], ACT.Silu).then_inc(s_silu, 1)
                        if ahead and q == KF + 1:
                            nc.scalar.preload_act_table_set(LN_SET)
                            norm.inverse_deviation(act, it + 1)
                        if ahead and q == UF - 1:
                            for b in range(NB):
                                for k in range(KD):
                                    norm.affine_chunk(act, it + 1, b, k, pst[:])

                blocks_ahead(act, step)

            @block.vector
            def _(dve):
                nc.vector.memset(ones[:], 1.0).then_inc(s_ones, 1)
                nc.vector.memset(zeros[:], 0.0).then_inc(s_ones, 2)
                dve.wait_ge(s_w, 16 * 9)
                nc.vector.tensor_copy(run[:], region[:]).then_inc(s_run, 1)
                norm.normalise(dve, 0)

                def step(it, ahead):
                    u = it + 1
                    dve.wait_ge(s_score, u)
                    nc.vector.tensor_copy(score[:], psg[:, 0:TI * EXP].rearrange("p (t e) -> p t e", e=EXP)
                                          ).then_inc(s_scorecp, 1)
                    dve.wait_ge(s_scorecp, u)
                    nc.vector.memset(norm.settle[:], 0.0)
                    for n in range(TI):
                        i = nc.vector.max(top[:, n], score[:, n])
                    i.then_inc(s_top, 1)
                    dve.wait_ge(s_top, u)
                    nc.vector.memset(norm.settle[:], 0.0)
                    for n in range(TI):
                        i = nc.vector.max_index(topi[:, n], top[:, n], score[:, n])
                    i.then_inc(s_topi, 1)
                    dve.wait_ge(s_topi, u)
                    nc.vector.tensor_copy(topf[:], topi[:]).then_inc(s_topf, 1)
                    dve.wait_ge(s_topf, u)
                    for c in range(2):
                        i = nc.vector.tensor_tensor(pick[:, c], number[:].unsqueeze(1).broadcast_to([P, TI, EXP]),
                                                    topf[:, :, c:c + 1].broadcast_to([P, TI, EXP]), ALU.is_equal)
                    i.then_inc(s_pick, 1)
                    dve.wait_ge(s_pick, u)
                    nc.vector.tensor_tensor(chosen[:], pick[:, 0], pick[:, 1], ALU.add).then_inc(s_chosen, 1)
                    dve.wait_ge(s_es, u)
                    nc.vector.tensor_scalar(gate[:], gate[:], 1.0, None, ALU.add).then_inc(s_es1, 1)
                    dve.wait_ge(s_es1, u)
                    nc.vector.reciprocal(gate[:], gate[:]).then_inc(s_gate, 1)

                    def product(q):
                        n = it * UF + q
                        dve.wait_ge(s_silu, n + 1)
                        nc.vector.tensor_tensor(hid[:, q // KF, q % KF], ps[:, q % 2, 1], act_f[:, q % 2],
                                                ALU.mult).then_inc(s_hid, 1)

                    def output(b):
                        dve.wait_ge(s_out, it * NB + b + 1)
                        if b:
                            dve.wait_ge(s_x, it * NB + b)
                        nc.vector.tensor_tensor(og[:], pso[:], keep["gates"][:, 0, 1, b:b + 1].broadcast_to([P, TB, D]),
                                                ALU.mult).then_inc(s_og, 1)

                    product(0)
                    product(1)
                    dve.wait_ge(s_rank, u)
                    dve.wait_ge(s_run, u)
                    nc.vector.tensor_tensor(place[:, 0], psr[:, 0:TI * EXP].rearrange("p (t e) -> p t e", e=EXP),
                                            run[:].unsqueeze(1).broadcast_to([P, TI, EXP]), ALU.add).then_inc(s_place, 1)
                    dve.wait_ge(s_place, u)
                    nc.vector.tensor_tensor(run[:], run[:], psr[:, TI * EXP:(TI + 1) * EXP], ALU.add).then_inc(s_run, 1)
                    product(2)
                    for c in (1, 0):
                        i = nc.vector.tensor_tensor(place[:, c], place[:, 0], pick[:, c], ALU.mult)
                        i.then_inc(s_placed, 1)
                        dve.wait_ge(s_placed, 2 * it + 2 - c)
                    for c in range(2):
                        i = nc.vector.tensor_reduce(rowf[:, :, c:c + 1], place[:, c], AX_X, ALU.add)
                    i.then_inc(s_rowf, 1)
                    product(3)
                    dve.wait_ge(s_rowf, u)
                    nc.vector.tensor_copy(rowu[:], rowf[:]).then_inc(s_rowu, 1)
                    nc.vector.tensor_copy(rows[:, bass.ds(it, 1)], rowf[:].unsqueeze(1)).then_inc(s_row, 1)
                    dve.wait_ge(s_gate, u)
                    dve.wait_ge(s_h, it * NB + NB)
                    for n in range(TI):
                        for c in range(2):
                            i = nc.vector.tensor_scalar(gated[:, n, c], norm.xn[:, n // TB, n % TB], gate[:, n, c:c + 1],
                                                        None, ALU.mult)
                    i.then_inc(s_gated, 1)
                    product(KF)
                    product(KF + 1)
                    if ahead:
                        norm.statistics(dve, it + 1)
                    output(0)
                    product(KF + 2)
                    if ahead:
                        dve.wait_ge(s_gated, u)
                        norm.scale_rows(dve, it + 1, 0, ahead=True)
                    product(KF + 3)
                    if ahead:
                        norm.scale_rows(dve, it + 1, 1, ahead=True)
                    output(1)
                    dve.wait_ge(s_x, it * NB + NB)
                    dve.wait_ge(s_sorted, it * ROUTED * 16 + ROUTED * 16)

                blocks_ahead(dve, step)
                dve.wait_ge(s_run, NBLK + 1)
                nc.vector.tensor_scalar(padf[:], run[:], iota[:, 0:1], None, ALU.add).then_inc(s_pad, 1)
                dve.wait_ge(s_pad, 1)
                nc.vector.tensor_copy(padu[:], padf[:]).then_inc(s_pad, 1)
                n = [0]

                def one(instruction):
                    n[0] += 1
                    instruction.then_inc(s_table, 1)
                    dve.wait_ge(s_table, n[0])

                one(nc.vector.tensor_tensor(count[:], run[:], region[:], ALU.subtract))
                shape = [P, EXP, SEQ * NB // P]
                one(nc.vector.tensor_tensor(over[:], count[:].unsqueeze(2).broadcast_to(shape),
                                            steps[:].unsqueeze(1).broadcast_to(shape), ALU.is_gt))
                one(nc.vector.tensor_reduce(blocks[:], over[:], AX_X, ALU.add))
                one(nc.vector.tensor_tensor_scan(end[:], keep["one"][:].broadcast_to([P, EXP]), blocks[:], 0.0,
                                                 ALU.mult, ALU.add))
                shape = [1, XBLOCKS, EXP]
                one(nc.vector.tensor_tensor(past[:, 0], block_no[:].unsqueeze(2).broadcast_to(shape),
                                            end[0:1].unsqueeze(1).broadcast_to(shape), ALU.is_ge))
                one(nc.vector.tensor_tensor(past[:, 1], past[:, 0], blocks[0:1].unsqueeze(1).broadcast_to(shape), ALU.mult))
                one(nc.vector.tensor_reduce(bexp[:], past[:, 0], AX_X, ALU.add))
                one(nc.vector.tensor_reduce(brow[:, 0], past[:, 1], AX_X, ALU.add))
                one(nc.vector.tensor_tensor(brow[:, 1], block_no[:], brow[:, 0], ALU.subtract))
                one(nc.vector.tensor_scalar(brow[:, 0], brow[:, 1], float(P), None, ALU.mult))
                one(nc.vector.scalar_tensor_tensor(out=brow[:, 1], in0=bexp[:], scalar=float(REGION), in1=brow[:, 0],
                                                   op0=ALU.mult, op1=ALU.add))
                one(nc.vector.tensor_copy(t["block_expert"][:], bexp[:]))
                one(nc.vector.tensor_copy(t["block_row"][:], brow[:, 1]))
                one(nc.vector.tensor_tensor(shift[:, 0], end[:], blocks[:], ALU.subtract))
                one(nc.vector.scalar_tensor_tensor(out=shift[:, 1], in0=shift[:, 0], scalar=-float(P), in1=region[:],
                                                   op0=ALU.mult, op1=ALU.add))
                one(nc.vector.tensor_copy(shift[:, 2, 0:1], shift[:, 1, 0:1]))
                one(nc.vector.tensor_tensor(shift[:, 2, 1:EXP], shift[:, 1, 1:EXP], shift[:, 1, 0:EXP - 1], ALU.subtract))
                dve.wait_ge(s_row, NBLK)
                shape = [P, NBLK * TI * 2, EXP]
                flat = rows[:].rearrange("p i n c -> p (i n c)")
                one(nc.vector.tensor_tensor(above[:, 0], flat.unsqueeze(2).broadcast_to(shape),
                                            region[:].unsqueeze(1).broadcast_to(shape), ALU.is_ge))
                one(nc.vector.tensor_tensor(above[:, 1], above[:, 0], shift[:, 2].unsqueeze(1).broadcast_to(shape), ALU.mult))
                one(nc.vector.tensor_reduce(moved[:], above[:, 1], AX_X, ALU.add))
                one(nc.vector.tensor_tensor(moved[:], flat, moved[:], ALU.subtract))
                one(nc.vector.tensor_copy(t["row"][:].rearrange("p i n c -> p (i n c)"), moved[:]))

            @block.tensor
            def _(pe):
                pe.wait_ge(s_w, 16 * 9)
                pe.wait_ge(s_ones, 1)
                pe.wait_ge(s_b, 16)
                norm.transpose(pe, 0, lambda b, k: ps[:, b, k])

                def step(it, ahead):
                    for b in range(NB):
                        pe.wait_ge(norm.s_hT, norm.ready(it, b))
                        for n in range(TB):
                            at = (b * TB + n) * EXP
                            for k in range(KD):
                                i = nc.tensor.matmul(psg[:, at:at + EXP], hT[:, b, k, n * P:(n + 1) * P],
                                                     router[:, k], start=(k == 0), stop=(k == KD - 1))
                    i.then_inc(s_score, 1)

                    def up(q):
                        n, b, f = it * UF + q, q // KF, q % KF
                        if q >= 2:
                            pe.wait_ge(s_hid, n - 1)
                        for j, wt in enumerate((w_in, w_sw)):
                            for k in range(KD):
                                i = nc.tensor.matmul(ps[:, q % 2, j], wt[:, EXP, k, f * P:(f + 1) * P], hT[:, b, k],
                                                     start=(k == 0), stop=(k == KD - 1))
                        i.then_inc(s_pair, 1)

                    def ranks():
                        pe.wait_ge(s_chosen, it + 1)
                        nc.tensor.matmul(psr[:, 0:TI * EXP], before[:], chosen[:].rearrange("p t e -> p (t e)"),
                                         start=True, stop=False, skip_group_check=True)
                        for n in range(TI - 1):
                            nc.tensor.matmul(psr[:, (n + 1) * EXP:TI * EXP].rearrange("p (t e) -> p t e", e=EXP), ones[:],
                                             chosen[:, n:n + 1].broadcast_to([P, TI - 1 - n, EXP]), start=False,
                                             stop=False, skip_group_check=True)
                        for n in range(TI):
                            i = nc.tensor.matmul(psr[:, TI * EXP:(TI + 1) * EXP], ones[:], chosen[:, n], start=False,
                                                 stop=(n == TI - 1), skip_group_check=True)
                        i.then_inc(s_rank, 1)

                    def down(b):
                        pe.wait_ge(s_hid, it * UF + (b + 1) * KF)
                        if b:
                            pe.wait_ge(s_og, it * NB + b)
                        for f in range(KF):
                            if ahead and b:
                                norm.turn(pe, it + 1, f // KD, f % KD, pst[:])
                            for n in range(TB):
                                i = nc.tensor.matmul(pso[:, n], hid[:, b, f, n * P:(n + 1) * P], w_out[:, f],
                                                     start=(f == 0 and n % 2 == 0), stop=(f == KF - 1 and n % 2 == 1),
                                                     skip_group_check=True)
                        i.then_inc(s_out, 1)

                    for q in range(UF):
                        up(q)
                        if q == 1:
                            ranks()
                        if q == KF + 1:
                            down(0)
                    down(1)
                    pe.wait_ge(s_og, it * NB + NB)

                blocks_ahead(pe, step)
        m.clear()


def run_experts(nc, a, keep, t):
    w_in, w_sw, ident = t["w_in"], t["w_sw"], keep["ident"]
    FIRST, UNROLL = 5, 4
    with ExitStack() as ctx:
        m = Pool(nc, ctx, "exp")
        w_out = m.sb("w_out", [P, EXP + 1, KF, D])
        rows = m.sb("rows", [P, UNROLL, D])
        xT = m.sb("xT", [P, 2, KD, P])
        act_f = m.sb("act_f", [P, 2, FF])
        hid = m.sb("hid", [P, 2, FF])
        hidT = m.sb("hidT", [P, 2, FF])
        res = m.sb("res", [P, UNROLL, D])
        psx = m.ps("psx", [P, 512])
        ps = m.ps("ps", [P, 2, 2, FF])
        psh = m.ps("psh", [P, FF])
        pso = m.ps("pso", [P, 512])
        s_turned, s_xT, s_mid, s_sw, s_silu, s_hid, s_hturned, s_hidT, s_out, s_res = (
            m.sem(n) for n in "turned xT mid sw silu hid hturned hidT out res".split())
        s_wo = m.sem("w_out_in")
        s_in = [m.sem(f"rows_in{n}") for n in range(UNROLL)]
        s_st = [m.sem(f"stored{n}") for n in range(UNROLL)]

        def pipeline(eng, step):
            for n in range(1, FIRST):
                step(0, n)
            rounds = (XBLOCKS - FIRST) // UNROLL
            with eng.Fori(0, rounds) as r:
                for k in range(UNROLL):
                    step(r * UNROLL, FIRST + k)
            for n in range(FIRST + rounds * UNROLL, XBLOCKS):
                step(0, n)

        with nc.Block() as block:
            @block.sync
            def _(sp):
                def load(base, k):
                    row = sp.value_load(t["block_row"][0:1, bass.ds(base + k, 1)], min_val=0, max_val=LAST_ROW)
                    sp.dma_start(rows[:, k % UNROLL], t["sorted"][bass.ds(row, P)]).then_inc(s_in[k % UNROLL], 16)

                def store(base, k):
                    sp.dma_start(t["results"][bass.ds((base + k) * P, P)], res[:, k % UNROLL]).then_inc(s_st[k % UNROLL], 16)

                for n in range(UNROLL):
                    load(0, n)
                for e in range(EXP + 1):
                    src = a["L0_ffn_w_out_eFD"][e] if e < EXP else a["shared_out"]
                    sp.dma_start(w_out[:, e], src.rearrange("(k p) d -> p k d", p=P)).then_inc(s_wo, 16)

                def step(base, k):
                    if not (isinstance(base, int) and k + 3 >= XBLOCKS):
                        sp.wait_ge(s_turned, base + k)
                        load(base, k + 3)
                    if k >= 2:
                        sp.wait_ge(s_res, base + k - 1)
                        store(base, k - 2)

                pipeline(sp, step)
                for n in (XBLOCKS - 2, XBLOCKS - 1):
                    sp.wait_ge(s_res, n + 1)
                    store(0, n)
                for n in range(UNROLL):
                    sp.wait_ge(s_st[n], 16 * (XBLOCKS // UNROLL))

            @block.scalar
            def _(act):
                def rows_in(base, k):
                    act.wait_ge(s_turned, base + k + 1)
                    nc.scalar.copy(xT[:, k % 2].rearrange("p k n -> p (k n)"), psx[:, 0:D]).then_inc(s_xT, 1)

                def silu(base, k):
                    act.wait_ge(s_mid, base + k + 1)
                    nc.scalar.activation(act_f[:, k % 2], ps[:, k % 2, 0], ACT.Silu).then_inc(s_silu, 1)

                def hidden(base, k):
                    act.wait_ge(s_hturned, base + k + 1)
                    nc.scalar.copy(hidT[:, k % 2], psh[:]).then_inc(s_hidT, 1)

                rows_in(0, 0)
                rows_in(0, 1)
                silu(0, 0)

                def step(base, k):
                    hidden(base, k - 1)
                    if not (isinstance(base, int) and k + 1 >= XBLOCKS):
                        rows_in(base, k + 1)
                    silu(base, k)

                pipeline(act, step)
                hidden(0, XBLOCKS - 1)

            @block.vector
            def _(dve):
                def product(base, k):
                    dve.wait_ge(s_silu, base + k + 1)
                    dve.wait_ge(s_sw, base + k + 1)
                    nc.vector.tensor_tensor(hid[:, k % 2], ps[:, k % 2, 1], act_f[:, k % 2], ALU.mult).then_inc(s_hid, 1)

                def result(base, k):
                    dve.wait_ge(s_out, base + k + 1)
                    if k >= UNROLL:
                        dve.wait_ge(s_st[k % UNROLL], base * (16 // UNROLL) + k // UNROLL * 16)
                    nc.vector.tensor_copy(res[:, k % UNROLL], pso[:, 0:D]).then_inc(s_res, 1)

                product(0, 0)

                def step(base, k):
                    product(base, k)
                    result(base, k - 1)

                pipeline(dve, step)
                result(0, XBLOCKS - 1)

            @block.tensor
            def _(pe):
                def turn(base, k):
                    pe.wait_ge(s_in[k % UNROLL], base * (16 // UNROLL) + k // UNROLL * 16 + 16)
                    if k:
                        pe.wait_ge(s_xT, base + k)
                    for c in range(KD):
                        i = nc.tensor.transpose(psx[:, c * P:(c + 1) * P], rows[:, k % UNROLL, c * P:(c + 1) * P], ident[:])
                    i.then_inc(s_turned, 1)

                def up(base, k):
                    e = pe.value_load(t["block_expert"][0:1, bass.ds(base + k, 1)], min_val=0, max_val=EXP)
                    pe.wait_ge(s_xT, base + k + 1)
                    for j, (wt, done) in enumerate(((w_in, s_mid), (w_sw, s_sw))):
                        for c in range(KD):
                            i = nc.tensor.matmul(ps[:, k % 2, j], xT[:, k % 2, c],
                                                 wt[:, bass.ds(e, 1), c].rearrange("p a f -> p (a f)"),
                                                 start=(c == 0), stop=(c == KD - 1))
                        i.then_inc(done, 1)

                def turn_hidden(base, k):
                    pe.wait_ge(s_hid, base + k + 1)
                    for f in range(KF):
                        i = nc.tensor.transpose(psh[:, f * P:(f + 1) * P], hid[:, k % 2, f * P:(f + 1) * P], ident[:])
                    i.then_inc(s_hturned, 1)

                def down(base, k):
                    e = pe.value_load(t["block_expert"][0:1, bass.ds(base + k, 1)], min_val=0, max_val=EXP)
                    pe.wait_ge(s_hidT, base + k + 1)
                    if k:
                        pe.wait_ge(s_res, base + k)
                    else:
                        pe.wait_ge(s_wo, 16 * (EXP + 1))
                    for f in range(KF):
                        i = nc.tensor.matmul(pso[:, 0:D], hidT[:, k % 2, f * P:(f + 1) * P],
                                             w_out[:, bass.ds(e, 1), f].rearrange("p a f -> p (a f)"),
                                             start=(f == 0), stop=(f == KF - 1))
                    i.then_inc(s_out, 1)

                pe.wait_ge(t["w_here"], 16 * 2 * EXP)
                turn(0, 0)
                turn(0, 1)
                up(0, 0)

                def step(base, k):
                    turn_hidden(base, k - 1)
                    if not (isinstance(base, int) and k + 1 >= XBLOCKS):
                        turn(base, k + 1)
                    up(base, k)
                    down(base, k - 1)

                pipeline(pe, step)
                turn_hidden(0, XBLOCKS - 1)
                down(0, XBLOCKS - 1)
        m.clear()


def collect_experts(nc, a, keep, t):
    x = keep["x"]
    TI = NB * TB
    with ExitStack() as ctx:
        m = Pool(nc, ctx, "col")
        rowu = m.sb("rowu", [P, 2, TI, 2], U32)
        got = m.sb("got", [P, 2, TI, 2, D])
        total = m.sb("total", [P, TI, D])
        s_row, s_sum, s_gated, s_x = (m.sem(n) for n in "row sum gated xadd".split())
        s_got = [t["soft"][f"got{n}"] for n in range(2)]
        with nc.Block() as block:
            @block.gpsimd
            def _(pool):
                for it in range(NBLK):
                    pool.wait_ge(s_row, it + 1)
                    if it >= 2:
                        pool.wait_ge(s_sum, it - 1)
                    for n in range(TI):
                        for c in range(2):
                            pool.indirect_dma_start(got[:, it % 2, n, c], None, t["results"],
                                                    bass.IndirectOffsetOnAxis(ap=rowu[:, it % 2, n, c:c + 1], axis=0)
                                                    ).then_inc(s_got[it % 2], 16)

            @block.vector
            def _(dve):
                def number(it):
                    nc.vector.tensor_copy(rowu[:, it % 2], t["row"][:, it]).then_inc(s_row, 1)

                number(0)
                number(1)
                for it in range(NBLK):
                    dve.wait_ge(s_got[it % 2], (it // 2 + 1) * TI * 2 * 16)
                    if it + 2 < NBLK:
                        number(it + 2)
                    nc.vector.tensor_tensor(total[:], got[:, it % 2, :, 0], got[:, it % 2, :, 1], ALU.add).then_inc(s_sum, 1)
                    dve.wait_ge(s_sum, it + 1)
                    for b in range(NB):
                        part = total[:, b * TB:(b + 1) * TB]
                        i = nc.vector.tensor_tensor(part, part, keep["gates"][:, 0, 1, b:b + 1].broadcast_to([P, TB, D]),
                                                    ALU.mult)
                    i.then_inc(s_gated, 1)
                    dve.wait_ge(s_gated, it + 1)
                    for b in range(NB):
                        xt = x[:, it * TB + b * TPB:it * TB + b * TPB + TB]
                        i = nc.vector.tensor_tensor(xt, xt, total[:, b * TB:(b + 1) * TB], ALU.add)
                    i.then_inc(s_x, 1)
                    dve.wait_ge(s_x, it + 1)
        m.clear()


def windowed_attention(nc, a, keep):
    x, modf, ident = keep["x"], keep["modf"], keep["ident"]
    with ExitStack() as outer:
        mo = Pool(nc, outer, "att")
        qhi = mo.sb("qhi", [P, KD, NB, SEQ], F32R)
        qlo = mo.sb("qlo", [P, KD, NB, SEQ], F32R)
        kT = mo.sb("kT", [P, KD, (NT + 2) * P], F32R)
        v = mo.sb("v", [P, NT + 2, AKV * AHD])

        with ExitStack() as ctx:
            m = Pool(nc, ctx, "qkv")
            norm = BlockNorm(m, keep, lambda b, t, it: [x[:, bass.ds(it * TB + b * TPB + t, 1)]],
                             lambda b, k: modf[:, 1, SCALE_A, NB * k + b:NB * k + b + 1],
                             lambda b, k: modf[:, 1, SHIFT_A, NB * k + b:NB * k + b + 1], banks=KD)
            hT = norm.hT
            wq = m.sb("wq", [P, KD, D])
            wk = m.sb("wk", [P, KD, D])
            wv = m.sb("wv", [P, KD, AKV * AHD])
            parts = m.sb("parts", [P, 2])
            khi = m.sb("khi", [P, KD, BLK], F32R)
            kpart = m.sb("kpart", [P, KD, BLK])
            ps = m.ps("ps", [P, 2 * KD, BLK])
            psv = m.ps("psv", [P, BLK])
            pst = m.ps("pst", [P, KD, BLK])
            s_w, s_q, s_k, s_v, s_qhi, s_qlo, s_khi, s_kpart, s_kc, s_vc, s_pad, s_kpad = (
                m.sem(n) for n in ("w_in", "q", "k", "v", "qhi", "qlo", "khi", "kpart", "kcp", "vcp", "pad", "kpad"))
            with nc.Block() as block:
                @block.sync
                def _(sp):
                    for dst, name in ((wq, "att_wq"), (wk, "att_wk"), (wv, "att_wv")):
                        sp.dma_start(dst[:], a[name].rearrange("(k p) n -> p k n", p=P)).then_inc(s_w, 16)
                    sp.dma_start(parts[:], a["key_parts"]).then_inc(s_w, 16)

                @block.gpsimd
                def _(pool):
                    for t in (0, NT + 1):
                        nc.gpsimd.memset(v[:, t], 0.0).then_inc(s_pad, 1)
                    pool.wait_ge(s_pad, 2)

                @block.scalar
                def _(act):
                    nc.scalar.preload_act_table_set(LN_SET)
                    norm.inverse_deviation(act, 0)
                    norm.affine(act, 0, lambda b, k: pst[:, k])

                    def step(it, ahead):
                        if ahead:
                            norm.inverse_deviation(act, it + 1)
                        for b in range(NB):
                            act.wait_ge(s_q, it * NB + b + 1)
                            nc.scalar.copy(qhi[:, :, b, bass.ds(it * BLK, BLK)], ps[:, 0:KD]).then_inc(s_qhi, 1)
                            act.wait_ge(s_k, it * NB + b + 1)
                            if b:
                                act.wait_ge(s_kpart, it * NB + b)
                            nc.scalar.copy(khi[:], ps[:, KD:2 * KD]).then_inc(s_khi, 1)
                            if ahead:
                                for k in range(KD):
                                    norm.affine_chunk(act, it + 1, b, k, pst[:, k])

                    blocks_ahead(act, step)

                @block.vector
                def _(dve):
                    norm.normalise(dve, 0)
                    for t in (0, NT + 1):
                        nc.vector.tensor_scalar(kT[:, :, t * P:(t + 1) * P],
                                                ident[:].unsqueeze(1).broadcast_to([P, KD, P]), 0.0, None,
                                                ALU.mult).then_inc(s_kpad, 1)
                    dve.wait_ge(s_w, 64)

                    def step(it, ahead):
                        if ahead:
                            norm.statistics(dve, it + 1)
                        for b in range(NB):
                            u = it * NB + b + 1
                            dve.wait_ge(s_qhi, u)
                            nc.vector.tensor_tensor(qlo[:, :, b, bass.ds(it * BLK, BLK)], ps[:, 0:KD],
                                                    qhi[:, :, b, bass.ds(it * BLK, BLK)], ALU.subtract).then_inc(s_qlo, 1)
                            if ahead:
                                norm.scale_rows(dve, it + 1, b, ahead=True)
                            dve.wait_ge(s_khi, u)
                            nc.vector.tensor_scalar(kpart[:], khi[:], parts[:, 0:1], None, ALU.mult).then_inc(s_kpart, 1)
                            dve.wait_ge(s_kpart, u)
                            nc.vector.scalar_tensor_tensor(out=kT[:, :, bass.ds(it * BLK + b * SEQ + P, BLK)],
                                                           in0=ps[:, KD:2 * KD], scalar=parts[:, 1:2], in1=kpart[:],
                                                           op0=ALU.mult, op1=ALU.add).then_inc(s_kc, 1)
                            dve.wait_ge(s_kc, u)
                            dve.wait_ge(s_v, u)
                            nc.vector.tensor_copy(v[:, bass.ds(it * TB + b * TPB + 1, TB)],
                                                  psv[:, 0:TB * AKV * AHD].rearrange("p (t d) -> p t d", t=TB)
                                                  ).then_inc(s_vc, 1)

                    blocks_ahead(dve, step)
                    dve.wait_ge(s_kpad, 2)

                @block.tensor
                def _(pe):
                    for b in range(NB):
                        if b:
                            pe.wait_ge(norm.s_hT, norm.ready(0, 0))
                        for k in range(KD):
                            norm.turn(pe, 0, b, k, pst[:, k], first=True)
                    pe.wait_ge(s_w, 64)

                    def step(it, ahead):
                        for b in range(NB):
                            pe.wait_ge(norm.s_hT, norm.ready(it, b))
                            for w, copied, done, at in ((wq, s_qlo, s_q, 0), (wk, s_kc, s_k, KD)):
                                if b:
                                    pe.wait_ge(copied, it * NB + b)
                                for c in range(KD):
                                    for k in range(KD):
                                        i = nc.tensor.matmul(ps[:, at + c], w[:, k, c * P:(c + 1) * P], hT[:, b, k],
                                                             start=(k == 0), stop=(k == KD - 1))
                                i.then_inc(done, 1)
                            if b:
                                pe.wait_ge(s_vc, it * NB + b)
                            for t in range(TB):
                                for k in range(KD):
                                    i = nc.tensor.matmul(psv[:, t * AKV * AHD:(t + 1) * AKV * AHD],
                                                         hT[:, b, k, t * P:(t + 1) * P], wv[:, k],
                                                         start=(k == 0), stop=(k == KD - 1))
                            i.then_inc(s_v, 1)
                            if ahead:
                                for k in range(KD):
                                    norm.turn(pe, it + 1, b, k, pst[:, k])
                        pe.wait_ge(s_qlo, it * NB + NB)
                        pe.wait_ge(s_kc, it * NB + NB)
                        pe.wait_ge(s_vc, it * NB + NB)

                    blocks_ahead(pe, step)
            m.clear()

        m = Pool(nc, outer, "win")
        wo = m.sb("wo", [P, KD, D])
        mask = m.sb("mask", [P, TPB, 2, P], BF16)
        identb = m.sb("identb", [P, P], BF16)
        pick = m.sb("pick", [P, AG, 2, P], F32R)
        qs = m.sb("qs", [P, KD, AG, NB, P], F32R)
        kw = m.sb("kw", [P, NB, KD, AW], F32R)
        top = m.sb("top", [P, 3, HPR])
        nb = m.sb("nb", [P, 3, HPR])
        rs = m.sb("rs", [P, NB, AH])
        ri = m.sb("ri", [P, NB, AH])
        pr = m.sb("pr", [P, 3, HPR, AW])
        pT = m.sb("pT", [P, 3, HPR, AW])
        o = m.sb("o", [P, D])
        oT = m.sb("oT", [P, D])
        og = keep["bmix_gated"]
        psw = m.ps("psw", [P, 3, HPR, 512])
        pso = m.ps("pso", [P, NB, 512])
        (s_w, s_pick, s_sel, s_qa, s_qb, s_kw, s_s, s_top, s_nb, s_e, s_t, s_pTa, s_pTb, s_pv, s_ri, s_o, s_oTp, s_oT, s_out,
         s_og, s_x) = (m.sem(n) for n in ("w_in pick sel queries_a queries_b keys scores top nb exp tp pTa pTb pv ri o oTp oT "
                                          "out og xadd").split())
        s_m = keep["soft"].sem("mask_in")
        RU = AH // HPR
        RI = NB * RU
        SC = float(AHD) ** -0.5
        HEAD = 1

        def head(r, h):
            c, g = r % RU // AG, r % AG
            return c, g, (2 * c + h) * AG + g

        def slot(r):
            return (r + 2) % 3

        def tiles(eng, step):
            step(0, False)
            with eng.Fori(1, TPB) as it:
                step(it, True)

        with nc.Block() as block:
            @block.sync
            def _(sp):
                sp.dma_start(wo[:], a["att_wo"].rearrange("(k p) n -> p k n", p=P)).then_inc(s_w, 16)
                sp.dma_start(pr[:].rearrange("p a b n -> p (a b n)")[:, 0:AG * 2 * P],
                             a["pick"].rearrange("p g s n -> p (g s n)")).then_inc(s_w, 16)

            @block.gpsimd
            def _(pool):
                pool.dma_start(mask[:], a["win_mask"]).then_inc(s_m, 16)
                pool.dma_start(identb[:], a["ident"]).then_inc(s_m, 16)

                def keys(it, b):
                    nc.gpsimd.tensor_tensor(kw[:, b], kT[:, :, bass.ds(it * P + b * SEQ, AW)],
                                            keep["one"][:].unsqueeze(2).broadcast_to([P, KD, AW]), ALU.mult
                                            ).then_inc(s_kw, 1)

                for b in range(NB):
                    keys(0, b)
                with pool.Fori(1, TPB) as it:
                    for b in range(NB):
                        pool.wait_ge(s_s, (it - 1) * RI + (b + 1) * RU)
                        keys(it, b)

            @block.scalar
            def _(act):
                nc.scalar.preload_act_table_set(LN_SET)

                def queries(it, c):
                    act.wait_ge(s_sel, it * KD + c + 1)
                    nc.scalar.copy(qs[:, c, 0:2].rearrange("p g b n -> p (g b n)"), psw[:, c, 0]).then_inc(s_qa, 1)

                def exps(it, r):
                    n, w, b = it * RI + r, slot(r), r // RU
                    act.wait_ge(s_nb, n + 1)
                    for h in range(HPR):
                        hh = head(r, h)[2]
                        i = nc.scalar.activation(pr[:, w, h], psw[:, w, h, 0:AW], ACT.Exp, scale=SC,
                                                 bias=nb[:, w, h:h + 1], accum_out=rs[:, b, hh:hh + 1])
                    i.then_inc(s_e, 1)

                def move(it, r):
                    w = slot(r)
                    act.wait_ge(s_t, it * RI + r + 1)
                    nc.scalar.copy(pT[:, w, 1], psw[:, w, 1, 0:AW]).then_inc(s_pTb, 1)

                def output(it, b):
                    act.wait_ge(s_oTp, it * NB + b + 1)
                    nc.scalar.copy(oT[:], pso[:, b, 0:D]).then_inc(s_oT, 1)

                act.wait_ge(s_pick, 1)

                def step(it, due):
                    for c in range(KD):
                        queries(it, c)
                        if c == 0 and due:
                            move(it - 1, RI - 1)
                    for r in range(RI):
                        exps(it, r)
                        if r == 2 and due:
                            output(it - 1, 1)
                        if r >= 1:
                            move(it, r - 1)
                        if r == RU + 4:
                            output(it, 0)

                tiles(act, step)
                move(TPB - 1, RI - 1)
                output(TPB - 1, 1)

            @block.vector
            def _(dve):
                dve.sem_inc(s_og, HEAD)
                dve.wait_ge(s_w, 32)
                nc.vector.tensor_copy(pick[:].rearrange("p g s n -> p (g s n)"),
                                      pr[:].rearrange("p a b n -> p (a b n)")[:, 0:AG * 2 * P]).then_inc(s_pick, 1)

                def queries(it, c):
                    dve.wait_ge(s_sel, it * KD + c + 1)
                    nc.vector.tensor_copy(qs[:, c, 2:4].rearrange("p g b n -> p (g b n)"), psw[:, c, 1]).then_inc(s_qb, 1)

                def maxima(it, r):
                    n, w = it * RI + r, slot(r)
                    dve.wait_ge(s_s, n + 1)
                    nc.vector.tensor_reduce(top[:, w], psw[:, w, :, 0:AW], AX_X, ALU.max).then_inc(s_top, 1)
                    dve.wait_ge(s_top, n + 1)
                    nc.vector.tensor_scalar(nb[:, w], top[:, w], -SC, None, ALU.mult).then_inc(s_nb, 1)

                def move(it, r):
                    w = slot(r)
                    dve.wait_ge(s_t, it * RI + r + 1)
                    nc.vector.tensor_copy(pT[:, w, 0], psw[:, w, 0, 0:AW]).then_inc(s_pTa, 1)

                def normalise(it, b):
                    u = it * NB + b
                    nc.vector.reciprocal(ri[:, b], rs[:, b]).then_inc(s_ri, 1)
                    dve.wait_ge(s_ri, u + 1)
                    dve.wait_ge(s_pv, it * RI + (b + 1) * RU)
                    sums = pso[:, b].rearrange("p (c h g d) -> p c h g d", c=KD, h=HPR, g=AG)
                    outs = o[:].rearrange("p (c h g d) -> p c h g d", c=KD, h=HPR, g=AG)
                    inv = ri[:, b].rearrange("p (c h g) -> p c h g", c=KD, h=HPR)
                    for c in range(KD):
                        for h in range(HPR):
                            i = nc.vector.tensor_tensor(outs[:, c, h], sums[:, c, h, :, h * AHD:(h + 1) * AHD],
                                                        inv[:, c, h].unsqueeze(2).broadcast_to([P, AG, AHD]), ALU.mult)
                    i.then_inc(s_o, 1)

                def output(it, b):
                    u = it * NB + b
                    dve.wait_ge(s_out, u + 1)
                    nc.vector.tensor_tensor(og[:, b], pso[:, b, D:2 * D], keep["gates"][:, 1, 0, b],
                                            ALU.mult).then_inc(s_og, 1)
                    dve.wait_ge(s_og, u + 1 + HEAD)
                    xt = x[:, bass.ds(it + b * TPB, 1)]
                    nc.vector.tensor_tensor(xt, xt, og[:, b:b + 1], ALU.add).then_inc(s_x, 1)

                def step(it, due):
                    for c in range(KD):
                        queries(it, c)
                        if c == 0 and due:
                            move(it - 1, RI - 1)
                    for r in range(RI):
                        maxima(it, r)
                        if r == 0 and due:
                            normalise(it - 1, 1)
                        if r >= 1:
                            move(it, r - 1)
                        if r == 5 and due:
                            output(it - 1, 1)
                        if r == RU + 2:
                            normalise(it, 0)
                        if r == RU + 7:
                            output(it, 0)

                tiles(dve, step)
                move(TPB - 1, RI - 1)
                normalise(TPB - 1, 1)
                output(TPB - 1, 1)

            @block.tensor
            def _(pe):
                pe.wait_ge(s_w, 32)
                pe.wait_ge(s_m, 32)
                pe.wait_ge(s_pick, 1)

                def queries(it, c):
                    for g in range(AG):
                        for s, q in enumerate((qhi, qlo)):
                            i = nc.tensor.matmul(psw[:, c, g // 2, g % 2 * 256:g % 2 * 256 + 256].rearrange(
                                "p (b n) -> p b n", b=NB), pick[:, g, s], q[:, c, :, bass.ds(it * P, P)],
                                start=(g % 2 == 0 and s == 0), stop=(g % 2 == 1 and s == 1), skip_group_check=True)
                    i.then_inc(s_sel, 1)

                def scores(it, r):
                    w, b = slot(r), r // RU
                    c = head(r, 0)[0]
                    if r % RU == 0:
                        pe.wait_ge(s_kw, it * NB + b + 1)
                    if r in (0, AG):
                        pe.wait_ge(s_qa, it * KD + c + 1)
                        pe.wait_ge(s_qb, it * KD + c + 1)
                    if r == 2:
                        pe.wait_ge(s_qa, it * KD + KD)
                        pe.wait_ge(s_qb, it * KD + KD)
                    if r >= 3:
                        pe.wait_ge(s_pTa, it * RI + r - 2)
                        pe.wait_ge(s_pTb, it * RI + r - 2)
                    for h in range(HPR):
                        nc.tensor.matmul(psw[:, w, h].rearrange("p (a n) -> p a n", a=2)[:, :, 0:P], identb[:],
                                         mask[:, bass.ds(it, 1)].rearrange("p i a n -> p (i a) n"), start=True,
                                         stop=False, skip_group_check=True)
                    for h in range(HPR):
                        c, g, _ = head(r, h)
                        rows = slice(h * (P // 2), (h + 1) * (P // 2))
                        i = nc.tensor.matmul(psw[:, w, h, 0:AW], qs[rows, c, g, b], kw[rows, b, c],
                                             start=False, stop=True, skip_group_check=True)
                    i.then_inc(s_s, 1)

                def turn(it, r):
                    w = slot(r)
                    pe.wait_ge(s_e, it * RI + r + 1)
                    for h in range(HPR):
                        for kb in range(3):
                            i = nc.tensor.transpose(psw[:, w, h, kb * P:(kb + 1) * P], pr[:, w, h, kb * P:(kb + 1) * P],
                                                    ident[:])
                    i.then_inc(s_t, 1)

                def values(it, r):
                    n, w, b = it * RI + r, slot(r), r // RU
                    pe.wait_ge(s_pTa, n + 1)
                    pe.wait_ge(s_pTb, n + 1)
                    if r % RU == 0:
                        pe.wait_ge(s_og, (it - 1) * NB + b + 1 + HEAD if not (isinstance(it, int) and it == 0) else HEAD)
                    for h in range(HPR):
                        c, _, hh = head(r, h)
                        for kb in range(3):
                            i = nc.tensor.matmul(pso[:, b, hh * 2 * AHD:(hh + 1) * 2 * AHD],
                                                 pT[:, w, h, kb * P:(kb + 1) * P],
                                                 v[:, bass.ds(it + b * TPB + kb, 1), c * 2 * AHD:(c + 1) * 2 * AHD],
                                                 start=(r % RU == 0 and h == 0 and kb == 0),
                                                 stop=(r % RU == RU - 1 and h == 1 and kb == 2), skip_group_check=True)
                    i.then_inc(s_pv, 1)

                def turn_out(it, b):
                    pe.wait_ge(s_o, it * NB + b + 1)
                    for c in range(KD):
                        i = nc.tensor.transpose(pso[:, b, c * P:(c + 1) * P], o[:, c * P:(c + 1) * P], ident[:])
                    i.then_inc(s_oTp, 1)

                def project_out(it, b):
                    pe.wait_ge(s_oT, it * NB + b + 1)
                    for c in range(KD):
                        i = nc.tensor.matmul(pso[:, b, D:2 * D], oT[:, c * P:(c + 1) * P], wo[:, c],
                                             start=(c == 0), stop=(c == KD - 1))
                    i.then_inc(s_out, 1)

                def step(it, due):
                    queries(it, 0)
                    if due:
                        turn(it - 1, RI - 1)
                        pe.wait_ge(s_pTa, it * RI - 1)
                        pe.wait_ge(s_pTb, it * RI - 1)
                    queries(it, 1)
                    if due:
                        values(it - 1, RI - 2)
                        pe.wait_ge(s_pTa, it * RI)
                        pe.wait_ge(s_pTb, it * RI)
                    for r in range(RI):
                        scores(it, r)
                        if r == 0 and due:
                            values(it - 1, RI - 1)
                        if r == 2 and due:
                            turn_out(it - 1, 1)
                        if r >= 1:
                            turn(it, r - 1)
                        if r == 4 and due:
                            project_out(it - 1, 1)
                        if r >= 2:
                            values(it, r - 2)
                        if r == RU + 4:
                            turn_out(it, 0)
                        if r == RU + 6:
                            project_out(it, 0)

                tiles(pe, step)
                turn(TPB - 1, RI - 1)
                values(TPB - 1, RI - 2)
                values(TPB - 1, RI - 1)
                turn_out(TPB - 1, 1)
                project_out(TPB - 1, 1)


def enter_local_stack(nc, a, keep, y, xs_a, spill, tables):
    x = keep["x"]
    with ExitStack() as ctx:
        m = Pool(nc, ctx, "ent")
        norm = BlockNorm(m, keep, lambda b, t, it: [x[:, bass.ds(it * TB + b * TPB + t, 1)]], None, None)
        s_zero, s_xs, s_sp = m.sem("zero"), m.sem("shifted"), m.sem("spilled")
        s_m = [m.sem(f"mult{b}") for b in range(NB)]
        s_y = [m.sem(f"y{b}") for b in range(NB)]
        s_t, s_mk = m.sem("tables"), keep["soft"].sem("masks")
        cos, sin, mask, identb = tables

        def modulate(eng, it, b):
            xn = norm.xn[:, b]
            eng.tensor_tensor(xn, xn, keep["scale_row"][:, b:b + 1].broadcast_to([P, TB, D]), ALU.mult).then_inc(s_m[b], 1)
            eng.wait_ge(s_m[b], it + 1)
            eng.tensor_tensor(y[:, bass.ds(it * TB + b * TPB, TB)], xn,
                              keep["shift_row"][:, b:b + 1].broadcast_to([P, TB, D]), ALU.add).then_inc(s_y[b], 1)

        with nc.Block() as block:
            @block.sync
            def _(sp):
                sp.dma_start(spill.rearrange("(t p) d -> p t d", p=P), x[:]).then_inc(s_sp, 16)
                for dst, name in ((cos, "cos"), (sin, "sin")):
                    sp.dma_start(dst[:], a[name]).then_inc(s_t, 16)
                sp.wait_ge(s_zero, 1)
                with sp.Fori(0, NBLK) as it:
                    for b in range(NB):
                        sp.wait_ge(s_y[b], it + 1)
                        shift_tokens(sp, y, xs_a, b, it * TB, TB, s_xs)
                sp.wait_ge(s_xs, NBLK * NB * 32)
                sp.wait_ge(s_t, 32)

            @block.scalar
            def _(act):
                nc.scalar.preload_act_table_set(LN_SET)
                with act.Fori(0, NBLK) as it:
                    norm.inverse_deviation(act, it)

            @block.vector
            def _(dve):
                nc.vector.memset(xs_a[0:1, :, 0], 0.0).then_inc(s_zero, 1)
                dve.wait_ge(s_sp, 16)
                with dve.Fori(0, NBLK) as it:
                    norm.normalise(dve, it)
                    dve.wait_ge(norm.s_xn, it * NB + NB)
                    modulate(dve, it, 1)
                    for b in range(NB):
                        dve.wait_ge(s_y[b], it + 1)

            @block.gpsimd
            def _(pool):
                for dst, name in ((mask, "loc_mask"), (identb, "ident")):
                    pool.dma_start(dst[:], a[name]).then_inc(s_mk, 16)
                pool.wait_ge(s_sp, 16)
                with pool.Fori(0, NBLK) as it:
                    pool.wait_ge(norm.s_xn, it * NB + 1)
                    modulate(pool, it, 0)
                pool.wait_ge(s_mk, 32)


def shift_tokens(eng, y, xs, b, tile, n, sem):
    src = y[:, bass.ds(tile + b * TPB, n), P:D]
    eng.dma_start(xs[1:P, b, bass.ds(tile, n)], src[0:P - 1]).then_inc(sem, 16)
    eng.dma_start(xs[0:1, b, bass.ds(tile + 1, n)], src[P - 1:P]).then_inc(sem, 16)


def local_attention(nc, a, keep, y, xs_a, xs_b, tabs, layer):
    ident = keep["ident"]
    cos, sin, mask, identb = tabs
    with ExitStack() as ctx:
        m = Pool(nc, ctx, "loc")
        w = m.sb("w", [P, KD, 3 * INNER])
        wo = m.sb("wo", [P, KI, D])
        scl = m.sb("scl", [P, 2, LHD])
        tc = m.sb("tc", [P, TPB, 2, LHD])
        ts = m.sb("ts", [P, TPB, 2, LHD])
        xst = m.sb("xst", [P, NB, D])
        hT = m.sb("hT", [P, NB, D])
        sq = m.sb("sq", [P, 2 * INNER])
        ss = m.sb("ss", [P, NB, 2 * LH])
        rn = m.sb("rn", [P, NB, 2 * LH])
        t1 = m.sb("t1", [P, NB, 2 * INNER])
        t2 = m.sb("t2", [P, NB, 2 * INNER])
        v = m.sb("v", [P, NB, 2, INNER])
        qT = m.sb("qT", [P, NB, KI, P])
        kT = m.sb("kT", [P, NB, KI, 2 * P])
        top = m.sb("top", [P, 2, 4])
        nb = m.sb("nb", [P, 2, 4])
        sc8 = m.sb("sc8", [P, NB, LH])
        rs = m.sb("rs", [P, NB, LH])
        ri = m.sb("ri", [P, NB, LH])
        pr = m.sb("pr", [P, 2, 4, 2 * P])
        pT = m.sb("pT", [P, 2, 8, P])
        o = m.sb("o", [P, INNER])
        oT = m.sb("oT", [P, INNER])
        psa = m.ps("psa", [P, 3, 512])
        psw = m.ps("psw", [P, 2, 2, 512])
        pso = m.ps("pso", [P, 512])
        names = ("w_in tab stage hTp hT qk vproj sq vcp ss ssm lnss rn sc8 t1 t2 rope krope ksc vprev kprev qkTp qT kT scores top "
                 "nb exp tp pTa pTb pv ri o oTp oT out y shifted")
        (s_w, s_tab, s_stage, s_hTp, s_hT, s_qk, s_v, s_sq, s_vcp, s_ss, s_ssm, s_lnss, s_rn, s_sc8, s_t1, s_t2,
         s_rope, s_krope, s_ksc, s_vprev, s_kprev, s_qkTp, s_qT, s_kT, s_s, s_top, s_nb, s_e, s_tp, s_pTa, s_pTb, s_pv, s_ri,
         s_o, s_oTp, s_oT, s_out, s_y, s_xs) = (m.sem(n) for n in names.split())
        L = layer

        def tile_of(j, b, ahead):
            jj, bb = j + (b + ahead) // NB, (b + ahead) % NB
            return jj, bb, L * (TPB * NB) + jj * NB + bb

        def pipeline(eng, step):
            with eng.Fori(0, TPB - 1) as j:
                for b in range(NB):
                    step(j, b, True, True)
            step(TPB - 1, 0, True, False)
            step(TPB - 1, 1, False, False)

        def heads(t):
            return t.rearrange("p (j h d) -> p j h d", j=2, h=LH)

        with nc.Block() as block:
            @block.sync
            def _(sp):
                sp.dma_start(w[:], a["wqkv"][bass.ds(L, 1)].rearrange("a (k p) n -> p (a k) n", p=P)).then_inc(s_w, 16)
                sp.dma_start(wo[:], a["loc_wo"][bass.ds(L, 1)].rearrange("a (k p) n -> p (a k) n", p=P)).then_inc(s_w, 16)
                sp.dma_start(scl[:], a["qk_scale"][bass.ds(L, 1)].broadcast_to([P, 2, LHD])).then_inc(s_w, 16)
                with sp.Fori(0, TPB) as j:
                    for b in range(NB):
                        u = L * (TPB * NB) + j * NB + b
                        sp.wait_ge(s_y, u + 2 + L)
                        shift_tokens(sp, y, xs_b, b, j, 1, s_xs)

            @block.gpsimd
            def _(pool):
                def copy(dst, src):
                    one = keep["one"][:]
                    for _ in range(len(src.shape) - 2):
                        one = one.unsqueeze(1)
                    return nc.gpsimd.tensor_tensor(dst, src, one.broadcast_to(list(src.shape)), ALU.mult)

                def stage(j, b):
                    copy(xst[:, b, 0:P].unsqueeze(1), y[:, bass.ds(j + b * TPB, 1), 0:P])
                    copy(xst[:, b, P:D].unsqueeze(1), xs_a[:, b, bass.ds(j, 1)]).then_inc(s_stage, 1)

                def rotate(b, u):
                    pool.wait_ge(s_t2, u + 1)
                    qq = t1[:, b, 0:INNER]
                    nc.gpsimd.tensor_tensor(qq, qq, t2[:, b, 0:INNER], ALU.add).then_inc(s_rope, 1)
                    pool.wait_ge(s_krope, u + 1)
                    pool.wait_ge(s_rn, u + 1)
                    kk = t1[:, b, INNER:].rearrange("p (h d) -> p h d", h=LH)
                    nc.gpsimd.tensor_tensor(kk, kk, rn[:, b, LH:].unsqueeze(2).broadcast_to([P, LH, LHD]),
                                            ALU.mult).then_inc(s_ksc, 1)

                for b in range(NB):
                    stage(0, b)
                    nc.gpsimd.memset(v[:, b, 0], 0.0).then_inc(s_vprev, 1)
                    nc.gpsimd.memset(kT[:, b, :, 0:P], 0.0).then_inc(s_kprev, 1)
                pool.wait_ge(s_w, (L + 1) * 48)
                nc.gpsimd.tensor_tensor(tc[:], cos[:], scl[:].unsqueeze(1).broadcast_to([P, TPB, 2, LHD]),
                                        ALU.mult).then_inc(s_tab, 1)
                for half in range(2):
                    d, s = slice(half * 32, half * 32 + 32), slice(32 - half * 32, 64 - half * 32)
                    nc.gpsimd.tensor_tensor(ts[:, :, :, d], sin[:, :, :, d],
                                            scl[:, :, s].unsqueeze(1).broadcast_to([P, TPB, 2, 32]),
                                            ALU.mult).then_inc(s_tab, 1)
                rotate(0, L * (TPB * NB))

                def step(j, b, ahead1, ahead2):
                    _, _, u = tile_of(j, b, 0)
                    if ahead2:
                        j2, b2, u2 = tile_of(j, b, 2)
                        pool.wait_ge(s_hTp, u2)
                        stage(j2, b2)
                        pool.wait_ge(s_s, 2 * u + 2)
                        copy(kT[:, b, :, 0:P], kT[:, b, :, P:2 * P]).then_inc(s_kprev, 1)
                    if ahead1:
                        _, b1, u1 = tile_of(j, b, 1)
                        rotate(b1, u1)
                    if ahead2:
                        pool.wait_ge(s_pv, 2 * u + 2)
                        copy(v[:, b, 0], v[:, b, 1]).then_inc(s_vprev, 1)

                pipeline(pool, step)
                pool.wait_ge(s_xs, (L + 1) * (TPB * NB * 32))

            @block.scalar
            def _(act):
                def copy_input(b, u):
                    act.wait_ge(s_hTp, u + 1)
                    nc.scalar.copy(hT[:, b], psa[:, 2, 0:D]).then_inc(s_hT, 1)

                def squares(b, u):
                    act.wait_ge(s_qk, u + 1)
                    nc.scalar.activation(sq[:], psa[:, 0:2].rearrange("p a n -> p (a n)"), ACT.Square).then_inc(s_sq, 1)

                def copy_values(b, u):
                    act.wait_ge(s_v, u + 1)
                    act.wait_ge(s_vprev, u + 1)
                    nc.scalar.copy(v[:, b, 1], psa[:, 2]).then_inc(s_vcp, 1)

                def inverse_norms(b, u):
                    act.wait_ge(s_ssm, u + 1)
                    nc.scalar.activation(rn[:, b], ss[:, b], ACT.Ln, scale=SS_SCALE).then_inc(s_lnss, 1)
                    act.wait_ge(s_lnss, u + 1)
                    nc.scalar.activation(rn[:, b], rn[:, b], ACT.Exp, scale=-0.5,
                                         bias=keep["ss_log"][:, 0:1]).then_inc(s_rn, 1)

                def copy_queries(b, u):
                    act.wait_ge(s_qkTp, u + 1)
                    nc.scalar.copy(qT[:, b].rearrange("p k n -> p (k n)"), psa[:, 0]).then_inc(s_qT, 1)

                def exps(b, u, hf):
                    act.wait_ge(s_nb, 2 * u + hf + 1)
                    for h in range(4):
                        hh = hf * 4 + h % 2 * 2 + h // 2
                        i = nc.scalar.activation(pr[:, hf, h], psw[:, hf, h // 2, h % 2 * 256:h % 2 * 256 + 256], ACT.Exp,
                                                 scale=sc8[:, b, hh:hh + 1], bias=nb[:, hf, h:h + 1],
                                                 accum_out=rs[:, b, hh:hh + 1])
                    i.then_inc(s_e, 1)

                def move(b, u, hf):
                    act.wait_ge(s_tp, 2 * u + hf + 1)
                    nc.scalar.copy(pT[:, hf, 4:8].rearrange("p k n -> p (k n)"), psw[:, hf, 1]).then_inc(s_pTb, 1)

                nc.scalar.preload_act_table_set(LN_SET)
                first = L * (TPB * NB)
                copy_input(0, first)
                squares(0, first)
                copy_values(0, first)
                inverse_norms(0, first)
                copy_input(1, first + 1)
                copy_queries(0, first)

                def step(j, b, ahead1, ahead2):
                    _, _, u = tile_of(j, b, 0)
                    _, b1, u1 = tile_of(j, b, 1)
                    exps(b, u, 0)
                    exps(b, u, 1)
                    if ahead1:
                        squares(b1, u1)
                        copy_values(b1, u1)
                    move(b, u, 0)
                    move(b, u, 1)
                    if ahead1:
                        inverse_norms(b1, u1)
                    if ahead2:
                        _, b2, u2 = tile_of(j, b, 2)
                        copy_input(b2, u2)
                    act.wait_ge(s_oTp, u + 1)
                    nc.scalar.copy(oT[:], pso[:]).then_inc(s_oT, 1)
                    if ahead1:
                        copy_queries(b1, u1)

                pipeline(act, step)

            @block.vector
            def _(dve):
                def rotate_cos(j, b, u):
                    dve.wait_ge(s_sq, u + 1)
                    qk = heads(psa[:, 0:2].rearrange("p a n -> p (a n)"))
                    for q in range(2):
                        cosq = tc[:, bass.ds(j, 1), q].broadcast_to([P, LH, LHD])
                        i = nc.vector.tensor_tensor(heads(t1[:, b])[:, q], qk[:, q], cosq, ALU.mult)
                    i.then_inc(s_t1, 1)

                def rotate_sin(j, b, u):
                    qk = heads(psa[:, 0:2].rearrange("p a n -> p (a n)"))
                    for q in range(2):
                        for half in range(2):
                            d, s = slice(half * 32, half * 32 + 32), slice(32 - half * 32, 64 - half * 32)
                            i = nc.vector.tensor_tensor(heads(t2[:, b])[:, q, :, d], qk[:, q, :, s],
                                                        ts[:, bass.ds(j, 1), q, d].broadcast_to([P, LH, 32]), ALU.mult)
                    i.then_inc(s_t2, 1)
                    dve.wait_ge(s_t2, u + 1)
                    kk = t1[:, b, INNER:]
                    nc.vector.tensor_tensor(kk, kk, t2[:, b, INNER:], ALU.add).then_inc(s_krope, 1)

                def sum_squares(b, u):
                    nc.vector.tensor_reduce(ss[:, b], sq[:].rearrange("p (h d) -> p h d", d=LHD), AX_X,
                                            ALU.add).then_inc(s_ss, 1)
                    dve.wait_ge(s_ss, u + 1)
                    nc.vector.tensor_scalar(ss[:, b], ss[:, b], 1e-24, None, ALU.max).then_inc(s_ssm, 1)

                def query_scale(b, u):
                    dve.wait_ge(s_rn, u + 1)
                    nc.vector.tensor_scalar(sc8[:, b], rn[:, b, 0:LH], QK_SCALE, None, ALU.mult).then_inc(s_sc8, 1)

                def copy_keys(b, u):
                    dve.wait_ge(s_qkTp, u + 1)
                    dve.wait_ge(s_kprev, u + 1)
                    nc.vector.tensor_copy(kT[:, b, :, P:2 * P], psa[:, 1].rearrange("p (k n) -> p k n", k=KI)
                                          ).then_inc(s_kT, 1)

                def maxima(b, u, hf):
                    dve.wait_ge(s_s, 2 * u + hf + 1)
                    nc.vector.tensor_reduce(top[:, hf], psw[:, hf].rearrange("p a (h n) -> p (a h) n", h=2), AX_X,
                                            ALU.max).then_inc(s_top, 1)
                    dve.wait_ge(s_top, 2 * u + hf + 1)
                    dve.wait_ge(s_sc8, u + 1)
                    nc.vector.scalar_tensor_tensor(
                        out=nb[:, hf].rearrange("p (r s) -> p r s", r=2),
                        in0=top[:, hf].rearrange("p (r s) -> p r s", r=2), scalar=-1.0,
                        in1=sc8[:, b, hf * 4:hf * 4 + 4].rearrange("p (s r) -> p r s", r=2), op0=ALU.mult,
                        op1=ALU.mult).then_inc(s_nb, 1)

                def move(b, u, hf):
                    dve.wait_ge(s_tp, 2 * u + hf + 1)
                    nc.vector.tensor_copy(pT[:, hf, 0:4].rearrange("p k n -> p (k n)"), psw[:, hf, 0]).then_inc(s_pTa, 1)

                nc.vector.memset(xs_b[0:1, :, 0], 0.0).then_inc(s_y, 1)
                dve.wait_ge(s_tab, (L + 1) * 3)
                first = L * (TPB * NB)
                rotate_cos(0, 0, first)
                rotate_sin(0, 0, first)
                sum_squares(0, first)
                query_scale(0, first)
                copy_keys(0, first)

                def step(j, b, ahead1, ahead2):
                    _, _, u = tile_of(j, b, 0)
                    j1, b1, u1 = tile_of(j, b, 1)
                    maxima(b, u, 0)
                    maxima(b, u, 1)
                    if ahead1:
                        rotate_cos(j1, b1, u1)
                    move(b, u, 0)
                    move(b, u, 1)
                    if ahead1:
                        rotate_sin(j1, b1, u1)
                        sum_squares(b1, u1)
                    nc.vector.reciprocal(ri[:, b], rs[:, b]).then_inc(s_ri, 1)
                    dve.wait_ge(s_ri, u + 1)
                    dve.wait_ge(s_pv, 2 * u + 2)
                    nc.vector.tensor_tensor(o[:].rearrange("p (h d) -> p h d", h=LH),
                                            pso[:].rearrange("p (h d) -> p h d", h=LH),
                                            ri[:, b].unsqueeze(2).broadcast_to([P, LH, LHD]), ALU.mult).then_inc(s_o, 1)
                    if ahead1:
                        query_scale(b1, u1)
                        copy_keys(b1, u1)
                    dve.wait_ge(s_out, u + 1)
                    yt = y[:, bass.ds(j + b * TPB, 1)]
                    nc.vector.tensor_tensor(yt, pso[:, 0:D].unsqueeze(1), yt, ALU.add).then_inc(s_y, 1)

                pipeline(dve, step)

            @block.tensor
            def _(pe):
                def turn_input(b, u):
                    pe.wait_ge(s_stage, u + 1)
                    for k in range(KD):
                        i = nc.tensor.transpose(psa[:, 2, k * P:(k + 1) * P], xst[:, b, k * P:(k + 1) * P], ident[:])
                    i.then_inc(s_hTp, 1)

                def project(b, u):
                    pe.wait_ge(s_hT, u + 1)
                    for c, done in ((0, None), (1, s_qk), (2, s_v)):
                        for k in range(KD):
                            i = nc.tensor.matmul(psa[:, c], hT[:, b, k * P:(k + 1) * P], w[:, k, c * 512:(c + 1) * 512],
                                                 start=(k == 0), stop=(k == KD - 1))
                        if done is not None:
                            i.then_inc(done, 1)

                def turn_rotated(b, u, q, rotated):
                    pe.wait_ge(rotated, u + 1)
                    for c in range(KI):
                        i = nc.tensor.transpose(psa[:, q, c * P:(c + 1) * P],
                                                t1[:, b, q * INNER + c * P:q * INNER + (c + 1) * P], ident[:])
                    return i

                def turn_queries(b, u):
                    turn_rotated(b, u, 0, s_rope)

                def turn_keys(b, u):
                    turn_rotated(b, u, 1, s_ksc).then_inc(s_qkTp, 1)

                def scores(j, b, u, hf):
                    if hf == 0:
                        pe.wait_ge(s_qT, u + 1)
                        pe.wait_ge(s_kT, u + 1)
                    for i2 in range(2):
                        out = psw[:, hf, i2].rearrange("p (h w n) -> p h w n", h=2, w=2)
                        nc.tensor.matmul(out[:, :, 0], identb[:], mask[:, bass.ds(j, 1), 0:P].broadcast_to([P, 2, P]),
                                         start=True, stop=False, skip_group_check=True)
                        nc.tensor.matmul(out[:, :, 1], identb[:], mask[:, 0:1, P:2 * P].broadcast_to([P, 2, P]),
                                         start=False, stop=False, skip_group_check=True)
                    for h in range(2):
                        for i2 in range(2):
                            hh, r = hf * 4 + h * 2 + i2, i2 * LHD
                            i = nc.tensor.matmul(psw[:, hf, i2, h * 256:(h + 1) * 256], qT[r:r + LHD, b, hh // 2],
                                                 kT[r:r + LHD, b, hh // 2], start=False, stop=(h == 1),
                                                 skip_group_check=True)
                    i.then_inc(s_s, 1)

                def turn(b, u, hf):
                    pe.wait_ge(s_e, 2 * u + hf + 1)
                    for h in range(4):
                        for kb in range(2):
                            i = nc.tensor.transpose(psw[:, hf, h // 2, (h % 2 * 2 + kb) * P:(h % 2 * 2 + kb + 1) * P],
                                                    pr[:, hf, h, kb * P:(kb + 1) * P], ident[:])
                    i.then_inc(s_tp, 1)

                def values(b, u, hf):
                    if hf == 0:
                        pe.wait_ge(s_y, u + 1 + L)
                        pe.wait_ge(s_vcp, u + 1)
                    pe.wait_ge(s_pTa, 2 * u + hf + 1)
                    pe.wait_ge(s_pTb, 2 * u + hf + 1)
                    for h in range(4):
                        hh = hf * 4 + h % 2 * 2 + h // 2
                        for kb in range(2):
                            i = nc.tensor.matmul(pso[:, hh * LHD:(hh + 1) * LHD], pT[:, hf, h * 2 + kb],
                                                 v[:, b, kb, hh * LHD:(hh + 1) * LHD], start=(hh == 0 and kb == 0),
                                                 stop=(hh == LH - 1 and kb == 1), skip_group_check=True)
                    i.then_inc(s_pv, 1)

                first = L * (TPB * NB)
                turn_input(0, first)
                pe.wait_ge(s_w, (L + 1) * 48)
                project(0, first)
                pe.wait_ge(s_vcp, first + 1)
                turn_input(1, first + 1)
                turn_queries(0, first)
                turn_keys(0, first)

                def step(j, b, ahead1, ahead2):
                    _, _, u = tile_of(j, b, 0)
                    _, b1, u1 = tile_of(j, b, 1)
                    scores(j, b, u, 0)
                    scores(j, b, u, 1)
                    if ahead1:
                        project(b1, u1)
                    turn(b, u, 0)
                    turn(b, u, 1)
                    values(b, u, 0)
                    values(b, u, 1)
                    if ahead2:
                        _, b2, u2 = tile_of(j, b, 2)
                        pe.wait_ge(s_vcp, u1 + 1)
                        turn_input(b2, u2)
                    if ahead1:
                        turn_queries(b1, u1)
                    pe.wait_ge(s_o, u + 1)
                    for c in range(KI):
                        i = nc.tensor.transpose(pso[:, c * P:(c + 1) * P], o[:, c * P:(c + 1) * P], ident[:])
                    i.then_inc(s_oTp, 1)
                    if ahead1:
                        turn_keys(b1, u1)
                    pe.wait_ge(s_oT, u + 1)
                    for c in range(KI):
                        i = nc.tensor.matmul(pso[:, 0:D], oT[:, c * P:(c + 1) * P], wo[:, c],
                                             start=(c == 0), stop=(c == KI - 1))
                    i.then_inc(s_out, 1)

                pipeline(pe, step)


def gated_mlp(nc, a, keep, y, xs_a, xs_b, layer):
    L = layer
    with ExitStack() as ctx:
        m = Pool(nc, ctx, "mlp")
        col = m.sb("col", [P, 2 * KD + 2 * KH])
        norm = BlockNorm(m, keep, lambda b, t, j: [y[:, bass.ds(j * TB + b * TPB + t, 1), 0:P],
                                                   xs_b[:, b, bass.ds(j * TB + t, 1)]],
                         lambda b, k: col[:, k:k + 1], lambda b, k: col[:, KD + k:KD + k + 1], banks=KD)
        hT = norm.hT
        w1 = m.sb("w1", [P, KD, 2 * HID])
        w2 = m.sb("w2", [P, KH, D])
        b2 = m.sb("b2", [P, 1, D])
        gl = m.sb("gl", [P, 2, BLK])
        hid = m.sb("hid", [P, 2, KH, BLK])
        ps = m.ps("ps", [P, 2, 2, BLK])
        pso = m.ps("pso", [P, TB, D])
        pst = m.ps("pst", [P, KD, BLK])
        s_w, s_pair, s_gl, s_hid, s_out, s_yo, s_y, s_xs = (
            m.sem(n) for n in ("w_in", "pair", "gelu", "hid", "out", "yo", "y", "shifted"))
        UF = NB * KH
        STATS = 3
        TURN = KH + 2

        with nc.Block() as block:
            @block.sync
            def _(sp):
                sp.dma_start(w1[:], a["w1"][bass.ds(L, 1)].rearrange("a (k p) n -> p (a k) n", p=P)).then_inc(s_w, 16)
                full = (KH - 1) * P
                sp.dma_start(w2[:, 0:KH - 1], a["w2"][bass.ds(L, 1), 0:full].rearrange("a (k p) n -> p (a k) n", p=P)
                             ).then_inc(s_w, 16)
                sp.dma_start(w2[0:HTAIL, KH - 1:KH], a["w2"][bass.ds(L, 1), full:HID].rearrange("a p n -> p a n")
                             ).then_inc(s_w, 16)
                sp.dma_start(b2[:], a["b2"][bass.ds(L, 1)].unsqueeze(0).broadcast_to([P, 1, D])).then_inc(s_w, 16)
                sp.dma_start(col[:], a["mlp_col"][bass.ds(L, 1)].rearrange("a p n -> p (a n)")).then_inc(s_w, 16)
                with sp.Fori(0, NBLK) as j:
                    it = L * NBLK + j
                    for b in range(NB):
                        sp.wait_ge(s_y, it * NB + b + 1)
                        shift_tokens(sp, y, xs_a, b, j * TB, TB, s_xs)

            @block.gpsimd
            def _(pool):
                with pool.Fori(0, NBLK) as j:
                    it = L * NBLK + j
                    pool.wait_ge(s_w, (L + 1) * 80)
                    for b in range(NB):
                        pool.wait_ge(s_yo, it * NB + b + 1)
                        yt = y[:, bass.ds(j * TB + b * TPB, TB)]
                        nc.gpsimd.tensor_tensor(yt, yt, b2[:].broadcast_to([P, TB, D]), ALU.add).then_inc(s_y, 1)
                pool.wait_ge(s_xs, (L + 1) * (NBLK * NB * 32))

            @block.scalar
            def _(act):
                def deviation(it):
                    nc.scalar.preload_act_table_set(LN_SET)
                    norm.inverse_deviation(act, it)

                def affine(it, b):
                    for k in range(KD):
                        norm.affine_chunk(act, it, b, k, pst[:, k])

                deviation(L * NBLK)
                act.wait_ge(s_w, (L + 1) * 80)
                for b in range(NB):
                    affine(L * NBLK, b)

                def step(j, ahead):
                    it = L * NBLK + j
                    for q in range(UF):
                        n, f = it * UF + q, q % KH
                        M = P if f < KH - 1 else HTAIL
                        act.wait_ge(s_pair, n + 1)
                        if q >= 2:
                            act.wait_ge(s_hid, n - 1)
                        c = 2 * KD + KH + f
                        nc.scalar.activation(gl[0:M, q % 2], ps[0:M, q % 2, 1], ACT.Gelu,
                                             bias=col[0:M, c:c + 1]).then_inc(s_gl, 1)
                        if ahead and q == STATS:
                            deviation(it + 1)
                        if ahead and q == TURN + 1:
                            affine(it + 1, 0)
                    if ahead:
                        affine(it + 1, 1)

                blocks_ahead(act, step)

            @block.vector
            def _(dve):
                norm.statistics(dve, L * NBLK, 0)
                dve.wait_ge(s_w, (L + 1) * 80)
                for b in range(NB):
                    norm.scale_rows(dve, L * NBLK, b, 0)

                def step(j, ahead):
                    it = L * NBLK + j
                    for q in range(UF):
                        n, f, b = it * UF + q, q % KH, q // KH
                        M = P if f < KH - 1 else HTAIL
                        dve.wait_ge(s_gl, n + 1)
                        c = 2 * KD + f
                        nc.vector.scalar_tensor_tensor(out=hid[0:M, b, f], in0=ps[0:M, q % 2, 0], scalar=col[0:M, c:c + 1],
                                                       in1=gl[0:M, q % 2], op0=ALU.add, op1=ALU.mult).then_inc(s_hid, 1)
                        if ahead and q == STATS:
                            norm.statistics(dve, it + 1, j + 1)
                        if ahead and q in (STATS + 2, STATS + 3):
                            norm.scale_rows(dve, it + 1, q - STATS - 2, j + 1, ahead=True)
                        if q == KH + 3 or q == UF - 1:
                            bb = 0 if q == KH + 3 else 1
                            dve.wait_ge(s_out, it * NB + bb + 1)
                            yt = y[:, bass.ds(j * TB + bb * TPB, TB)]
                            nc.vector.tensor_tensor(yt, pso[:], yt, ALU.add).then_inc(s_yo, 1)

                blocks_ahead(dve, step)

            @block.tensor
            def _(pe):
                def turn(it, b, first=False):
                    for k in range(KD):
                        norm.turn(pe, it, b, k, pst[:, k], first=first)

                turn(L * NBLK, 0, first=True)
                pe.wait_ge(s_w, (L + 1) * 80)
                pe.wait_ge(norm.s_hT, norm.ready(L * NBLK, 0))
                turn(L * NBLK, 1, first=True)

                def step(j, ahead):
                    it = L * NBLK + j

                    def up(q):
                        n, f, b = it * UF + q, q % KH, q // KH
                        M = P if f < KH - 1 else HTAIL
                        if f == 0:
                            pe.wait_ge(norm.s_hT, norm.ready(it, b))
                        if q >= 2:
                            pe.wait_ge(s_hid, n - 1)
                        for i2 in range(2):
                            for k in range(KD):
                                i = nc.tensor.matmul(ps[0:M, q % 2, i2], w1[:, k, i2 * HID + f * P:i2 * HID + f * P + M],
                                                     hT[:, b, k], start=(k == 0), stop=(k == KD - 1))
                        i.then_inc(s_pair, 1)

                    def down(b):
                        pe.wait_ge(s_hid, it * UF + (b + 1) * KH)
                        if b:
                            pe.wait_ge(s_yo, it * NB + b)
                        for f in range(KH):
                            M = P if f < KH - 1 else HTAIL
                            for t in range(TB):
                                i = nc.tensor.matmul(pso[:, t], hid[0:M, b, f, t * P:(t + 1) * P], w2[0:M, f],
                                                     start=(f == 0 and t % 2 == 0), stop=(f == KH - 1 and t % 2 == 1),
                                                     skip_group_check=True)
                        i.then_inc(s_out, 1)

                    for q in range(UF):
                        up(q)
                        if q == KH + 1:
                            down(0)
                        if ahead and q == TURN:
                            turn(it + 1, 0)
                    if ahead:
                        turn(it + 1, 1)
                    down(1)

                blocks_ahead(pe, step)


def leave_local_stack(nc, a, keep, y, spill):
    with ExitStack() as ctx:
        m = Pool(nc, ctx, "fin")
        xr = m.sb("xr", [P, NT, D])
        s_g, s_r, s_o = m.sem("gated"), m.sem("ready"), m.sem("stored")
        s_x = [m.sem(f"x_in{n}") for n in range(NT // TB)]
        with nc.Block() as block:
            @block.vector
            def _(dve):
                for n in range(NT // TB):
                    t = slice(n * TB, (n + 1) * TB)
                    g = keep["gates"][:, 1, 1, n // NBLK:n // NBLK + 1].broadcast_to([P, TB, D])
                    nc.vector.tensor_tensor(y[:, t], y[:, t], g, ALU.mult).then_inc(s_g, 1)

            @block.gpsimd
            def _(pool):
                for n in range(NT // TB):
                    t = slice(n * TB, (n + 1) * TB)
                    pool.wait_ge(s_g, n + 1)
                    pool.wait_ge(s_x[n], 16)
                    nc.gpsimd.tensor_tensor(y[:, t], xr[:, t], y[:, t], ALU.add).then_inc(s_r, 1)

            @block.sync
            def _(sp):
                back = spill.rearrange("(t p) d -> p t d", p=P)
                out = a["y"].rearrange("(t p) d -> p t d", p=P)
                for n in range(NT // TB):
                    t = slice(n * TB, (n + 1) * TB)
                    sp.dma_start(xr[:, t], back[:, t]).then_inc(s_x[n], 16)
                for n in range(NT // TB):
                    t = slice(n * TB, (n + 1) * TB)
                    sp.wait_ge(s_r, n + 1)
                    sp.dma_start(out[:, t], y[:, t]).then_inc(s_o, 16)
                sp.wait_ge(s_o, 16 * (NT // TB))


def local_stack(nc, a, keep):
    with ExitStack() as ctx:
        m = Pool(nc, ctx, "stk")
        y = keep["x"]
        spill = nc.dram_tensor("x_aside", [NT * P, D], F32).ap()
        xs_a = m.sb("xs_a", [P, NB, TPB + 1, P])
        xs_b = m.sb("xs_b", [P, NB, TPB + 1, P])
        cos = m.sb("cos", [P, TPB, 2, LHD])
        sin = m.sb("sin", [P, TPB, 2, LHD])
        mask = m.sb("mask", [P, TPB, 2 * P], BF16)
        identb = m.sb("identb", [P, P], BF16)
        enter_local_stack(nc, a, keep, y, xs_a, spill, (cos, sin, mask, identb))
        with nc.Fori(0, DEPTH) as layer:
            local_attention(nc, a, keep, y, xs_a, xs_b, (cos, sin, mask, identb), layer)
            gated_mlp(nc, a, keep, y, xs_a, xs_b, layer)
        leave_local_stack(nc, a, keep, y, spill)


def write_out(nc, a, keep):
    with ExitStack() as ctx:
        m = Pool(nc, ctx, "out")
        s_o = m.sem("stored")
        with nc.Block() as block:
            @block.sync
            def _(sp):
                sp.dma_start(a["y"].rearrange("(t p) d -> p t d", p=P), keep["x"][:]).then_inc(s_o, 16)
                sp.wait_ge(s_o, 16)


def build_program(nc, a, stages=(1, 2, 3, 4)):
    with ExitStack() as ctx:
        m = Pool(nc, ctx, "keep")
        keep = {
            "x": m.sb("x", [P, NT, D]),
            "ident": m.sb("ident", [P, P]),
            "modf": m.sb("modf", [P, 2, 6, KD * NB]),
            "gates": m.sb("gates", [P, 2, 2, NB, D]),
            "moe_scale_row": m.sb("moe_scale_row", [P, NB, D]),
            "moe_shift_row": m.sb("moe_shift_row", [P, NB, D]),
            "scale_row": m.sb("scale_row", [P, NB, D]),
            "shift_row": m.sb("shift_row", [P, NB, D]),
            "bmix_gated": m.sb("bmix_gated", [P, NB, D]),
            "eps": m.sb("eps", [P, 1]),
            "one": m.sb("one", [P, 1]),
            "u_log": m.sb("u_log", [P, 1]),
            "ss_log": m.sb("ss_log", [P, 1]),
        }
        keep["soft"] = Pool(nc, ctx, "soft")
        s_c = m.sem("consts")
        with nc.Block() as block:
            @block.vector
            def _(dve):
                nc.vector.memset(keep["eps"][:], EPS).then_inc(s_c, 1)
                nc.vector.memset(keep["one"][:], 1.0).then_inc(s_c, 1)
                nc.vector.memset(keep["u_log"][:], U_LOG).then_inc(s_c, 1)
                nc.vector.memset(keep["ss_log"][:], SS_LOG).then_inc(s_c, 1)
                dve.wait_ge(s_c, 4)
        load_and_modulate(nc, a, keep)
        if 1 in stages:
            gated_recurrence(nc, a, keep)
        if 2 in stages:
            experts(nc, a, keep)
        if 3 in stages:
            windowed_attention(nc, a, keep)
        if 4 in stages:
            local_stack(nc, a, keep)
        else:
            write_out(nc, a, keep)


def lay_out(inputs):
    c = np.ascontiguousarray
    out = {k: c(inputs[k]) for k in (
        "L0_attn_W_aiv", "L0_attn_decay_bias", "L0_attn_W_mix", "L0_attn_b_mix", "L0_wmod", "L1_wmod",
        "L0_ffn_router_DE", "L0_ffn_w_in_eDF", "L0_ffn_w_swiglu_eDF", "L0_ffn_w_out_eFD")}
    out["L0_c"], out["L1_c"] = c(np.asarray(inputs["L0_c"]).T), c(np.asarray(inputs["L1_c"]).T)
    out["x"] = c(inputs["L0_attn_x"]).reshape(NB * SEQ, D)
    out["L0_attn_decay_bias"] = c(c(inputs["L0_attn_decay_bias"]).reshape(NG, P).T)
    out["shared_in"] = c(np.asarray(inputs["L0_ffn_w_in_shared_FD"]).T)
    out["shared_sw"] = c(np.asarray(inputs["L0_ffn_w_swiglu_FD"]).T)
    out["shared_out"] = c(np.asarray(inputs["L0_ffn_w_out_shared_DF"]).T)
    out["number"] = np.arange(EXP, dtype=np.float32)
    out["region"] = (np.arange(EXP) * REGION).astype(np.float32)
    out["iota"] = np.arange(P, dtype=np.float32)[:, None]
    out["steps"] = (np.arange(NB * TPB) * P).astype(np.float32)
    out["block_no"] = np.arange(XBLOCKS, dtype=np.float32)
    out["before"] = np.triu(np.ones((P, P), np.float32), 1)
    out["ident"] = np.eye(P, dtype=np.float32)
    out["keepmask"] = (np.arange(BLK) % CHUNK != 0).astype(np.float32)
    out["att_wq"] = c(np.asarray(inputs["L1_attn_Wq"]).T)
    wk = np.asarray(inputs["L1_attn_Wk"]).T.reshape(D, AKV, 1, AHD)
    out["att_wk"] = c(np.broadcast_to(wk, (D, AKV, AG, AHD)).reshape(D, D))
    out["att_wv"] = c(np.asarray(inputs["L1_attn_Wv"]).T)
    out["att_wo"] = c(np.asarray(inputs["L1_attn_Wo"]).T)
    out.update(shape_constants())
    out["wqkv"] = c(inputs["L1_ffn_wqkv"])
    out["loc_wo"] = c(inputs["L1_ffn_wo"])
    out["qk_scale"] = np.stack([np.asarray(inputs["L1_ffn_q_scale"]), np.asarray(inputs["L1_ffn_k_scale"])], axis=1)
    out["w1"] = c(inputs["L1_ffn_w1"])
    out["w2"] = c(inputs["L1_ffn_w2"])
    out["b2"] = c(inputs["L1_ffn_b2"])
    col = np.zeros((DEPTH, 2 * KD + 2 * KH, P), np.float32)
    col[:, 0:KD] = np.asarray(inputs["L1_ffn_ln_g"]).reshape(DEPTH, KD, P)
    col[:, KD:2 * KD] = np.asarray(inputs["L1_ffn_ln_b"]).reshape(DEPTH, KD, P)
    b1 = np.asarray(inputs["L1_ffn_b1"])
    for half in range(2):
        part = np.zeros((DEPTH, KH * P), np.float32)
        part[:, :HID] = b1[:, half * HID:(half + 1) * HID]
        col[:, 2 * KD + half * KH:2 * KD + (half + 1) * KH] = part.reshape(DEPTH, KH, P)
    out["mlp_col"] = c(col.transpose(0, 2, 1))
    return out


def shape_constants():
    far = np.float32(-1e30)
    q, key = np.arange(P)[:, None], np.arange(P)[None, :]
    before = np.where(key >= q, 0, far)
    after = np.where(key <= q, 0, far)
    never = np.full((P, P), far)
    win = np.zeros((P, TPB, 2, P), np.float32)
    loc = np.zeros((P, TPB, 2 * P), np.float32)
    for t in range(TPB):
        win[:, t, 0] = loc[:, t, 0:P] = before if t else never
        win[:, t, 1] = after if t < TPB - 1 else never
        loc[:, t, P:] = after
    part = np.arange(P) // AHD % AG
    pick = np.zeros((2, AG, AHD, AG, 2, 2, 2, 2, AHD), np.float32)
    for hf in range(2):
        for g in range(AG):
            for s in range(2):
                for d in range(AHD):
                    pick[hf, g, d, g, s, hf, s, :, d] = 1
    half = np.arange(0, LHD, 2, dtype=np.float32)
    inv_freq = np.float32(1.0) / np.float32(10000.0) ** (half / np.float32(LHD))
    t = np.arange(SEQ, dtype=np.float32)
    freqs = t[:, None] * inv_freq[None]
    base = (half + np.float32(0.4 * LHD)) / np.float32(1.4 * LHD)
    scale = (base[None].astype(np.float64) ** ((t - SEQ // 2) / 64.0)[:, None])
    cosf, sinf = np.cos(freqs.astype(np.float64)), np.sin(freqs.astype(np.float64))
    cos, sin = np.zeros((SEQ, 2, LHD)), np.zeros((SEQ, 2, LHD))
    for i, s in enumerate((scale, 1 / scale)):
        cos[:, i] = np.concatenate([cosf * s, cosf * s], axis=1)
        sin[:, i] = np.concatenate([-sinf * s, sinf * s], axis=1)
    tile = lambda x: np.ascontiguousarray(x.reshape(TPB, P, 2, LHD).transpose(1, 0, 2, 3).astype(np.float32))
    return {
        "win_mask": win, "loc_mask": loc,
        "key_parts": np.stack([np.where(part % 2, -1, 1), part % 2], axis=1).astype(np.float32),
        "pick": pick.reshape(P, AG, 2, P),
        "cos": tile(cos), "sin": tile(sin),
    }


def kernel(**inputs):
    import concourse.bacc as bacc
    from concourse.bass_utils import run_bass_kernel_spmd

    nc = bacc.Bacc("TRN2", target_bir_lowering=False, num_devices=1)
    arrays = {f"in_{name}": value for name, value in lay_out(inputs).items()}
    aps = {name[3:]: nc.dram_tensor(name, value.shape, mybir.dt.from_np(value.dtype), kind="ExternalInput").ap()
           for name, value in arrays.items()}
    aps["y"] = nc.dram_tensor("out_y", (NB * SEQ, D), F32, kind="ExternalOutput").ap()
    build_program(nc, aps)
    result = run_bass_kernel_spmd(nc, [arrays], core_ids=[0])
    return result.results[0]["out_y"].reshape(NB, SEQ, D)
```
